# Optimizing a Trainium2 kernel written in Bass

```python
import numpy as np
import jax
import jax.numpy as jnp

def _softmax(x, axis=-1):
    return jax.nn.softmax(x, axis=axis)

def _gelu(x):
    return jax.nn.gelu(x, approximate=True)

def _silu(x):
    return jax.nn.silu(x)

def _sigmoid(x):
    return jax.nn.sigmoid(x)

def _layernorm(x, axis=-1, eps=1e-05):
    m = jnp.mean(x, axis=axis, keepdims=True)
    v = jnp.var(x, axis=axis, keepdims=True)
    return (x - m) / jnp.sqrt(v + eps)

def _scatter_add(tgt, idx, src, axis=0):
    return tgt.at[idx].add(src)

def _segment_sum(src, seg, n):
    return jax.ops.segment_sum(src, seg, n)
kernel_name = 'mk_xattn_ffn_d4_seqx_r8_4746a9'

def setup_inputs(seed: int=0):
    np.random.seed(seed)
    _w = jnp.asarray

    def _rec_inputs():
        import jax
        import jax.numpy as jnp
        _rk = jax.random.key(seed)
        x = -0.0002928 + 1 * jax.random.normal(jax.random.fold_in(_rk, 1), (4, 512, 128), jnp.float32)
        _lenS = 512 - jax.random.randint(jax.random.fold_in(_rk, 7), (4,), 0, max(1, 512 // 4) + 1, jnp.int32)
        _lenS2 = 154 - jax.random.randint(jax.random.fold_in(_rk, 8), (4,), 0, max(1, 154 // 4) + 1, jnp.int32)
        _ctx_1024P = jax.random.normal(jax.random.fold_in(_rk, 11), (4, 16, 128), jnp.float32)
        _ctx_1024c = jax.random.dirichlet(jax.random.fold_in(_rk, 511), 0.3 * jnp.ones((16,), jnp.float32), (4, 154))
        _ctx_1024t = jnp.einsum('bsk,bkd->bsd', _ctx_1024c, _ctx_1024P)
        _ctx_1024t = _ctx_1024t * jax.lax.rsqrt(jnp.mean(jnp.square(_ctx_1024t)) + 1e-12) * 0.953939
        ctx_1024 = -1.39393e-06 + 0.999914 * (_ctx_1024t + 0.3 * jax.random.normal(jax.random.fold_in(_rk, 611), (4, 154, 128), jnp.float32))
        _validS = jnp.arange(512)[None, :] < _lenS[:, None]
        _validS2 = jnp.arange(154)[None, :] < _lenS2[:, None]
        _causal = jnp.tril(jnp.ones((512, 512), dtype=bool))
        mask_Bx1x1xS2_ik0 = jnp.where(jnp.broadcast_to(_validS2[:, None, None, :], (4, 1, 1, 154)), 0, 1).astype(jnp.int32)
        mask_Bx1x1xS2_bf1 = jnp.ones((4, 1, 1, 154), dtype=bool)
        return (x, ctx_1024, mask_Bx1x1xS2_ik0, mask_Bx1x1xS2_bf1)
    x, ctx_1024, mask_Bx1x1xS2_ik0, mask_Bx1x1xS2_bf1 = _rec_inputs()

    def _L0_xattn_setup():
        import jax, jax.numpy as jnp
        import numpy as np
        import math
        B, S, D, H, M = (2, 256, 128, 16, 64)
        HD = D // H
        key = jax.random.key(seed)
        ks = jax.random.split(key, 16)
        inp = {'query': jax.random.normal(ks[0], (B, S, D), jnp.float32), 'key': jax.random.normal(ks[1], (B, S, D), jnp.float32), 'value': jax.random.normal(ks[2], (B, S, D), jnp.float32), 'mask': jax.random.randint(ks[3], (B, 1, 1, S), 0, 2, jnp.int32), 'Wq': jax.random.normal(ks[4], (D, D), jnp.float32) * 0.02, 'bq': jnp.zeros((D,), jnp.float32), 'Wk': jax.random.normal(ks[5], (D, D), jnp.float32) * 0.02, 'bk': jnp.zeros((D,), jnp.float32), 'Wv': jax.random.normal(ks[6], (D, D), jnp.float32) * 0.02, 'bv': jnp.zeros((D,), jnp.float32), 'Wo': jax.random.normal(ks[7], (D, D), jnp.float32) * 0.02, 'bo': jnp.zeros((D,), jnp.float32), 'm_k': jax.random.normal(ks[8], (1, M, D), jnp.float32) * (1.0 / HD), 'm_v': jax.random.normal(ks[9], (1, M, D), jnp.float32) * (1.0 / M)}
        return inp
    _L0_xattn_all = _L0_xattn_setup()
    _L0_xattn_in = {k: v for k, v in _L0_xattn_all.items() if k in ('Wq', 'bq', 'Wk', 'bk', 'Wv', 'bv', 'Wo', 'bo', 'm_k', 'm_v')}
    del _L0_xattn_all

    def _L0_ffn_setup():
        import jax, jax.numpy as jnp
        import numpy as np
        LORA_DIM = 16
        LORA_TOKEN_INDEX = 1
        B, S, D, H = (4, 256, 128, 512)
        key = jax.random.key(seed)
        ks = jax.random.split(key, 6)
        x = jax.random.normal(ks[0], (B, S, D), dtype=jnp.float32)
        W1 = jax.random.normal(ks[1], (H, D), dtype=jnp.float32) * 0.02
        b1 = jnp.zeros((H,), dtype=jnp.float32)
        W2 = jax.random.normal(ks[2], (D, H), dtype=jnp.float32) * 0.02
        b2 = jnp.zeros((D,), dtype=jnp.float32)
        scale = jnp.asarray(0.001, dtype=jnp.float32)
        return {'x': x, 'W1': W1, 'b1': b1, 'W2': W2, 'b2': b2, 'scale': scale}
    _L0_ffn_all = _L0_ffn_setup()
    _L0_ffn_in = {k: v for k, v in _L0_ffn_all.items() if k in ('W1', 'b1', 'W2', 'b2', 'scale')}
    del _L0_ffn_all

    def _L1_xattn_setup():
        import jax, jax.numpy as jnp
        import numpy as np
        D = 128
        H = 16
        HD = D // H
        EPS = 1e-06

        def rms_norm(x, w):
            xf = x.astype(jnp.float32)
            rms = jnp.sqrt(jnp.mean(xf * xf, axis=-1, keepdims=True) + EPS)
            return (xf / rms * w.astype(jnp.float32)).astype(x.dtype)
        key = jax.random.key(seed)
        ks = jax.random.split(key, 10)
        B, S, Sc = (4, 256, 256)
        s = 0.02
        return {'x': jax.random.normal(ks[0], (B, S, D), jnp.float32), 'ctx': jax.random.normal(ks[1], (B, Sc, D), jnp.float32), 'Wq': jax.random.normal(ks[2], (D, D), jnp.float32) * s, 'bq': jnp.zeros((D,), jnp.float32), 'Wkv': jax.random.normal(ks[3], (D, 2 * D), jnp.float32) * s, 'bkv': jnp.zeros((2 * D,), jnp.float32), 'Wproj': jax.random.normal(ks[4], (D, D), jnp.float32) * s, 'bproj': jnp.zeros((D,), jnp.float32), 'gq': jnp.ones((HD,), jnp.float32), 'gk': jnp.ones((HD,), jnp.float32)}
    _L1_xattn_all = _L1_xattn_setup()
    _L1_xattn_in = {k: v for k, v in _L1_xattn_all.items() if k in ('Wq', 'bq', 'Wkv', 'bkv', 'Wproj', 'bproj', 'gq', 'gk')}
    del _L1_xattn_all

    def _L1_ffn_setup():
        import jax, jax.numpy as jnp
        import numpy as np
        B, S, D, F, E, K = (4, 256, 128, 512, 4, 2)
        key = jax.random.key(seed)
        k = jax.random.split(key, 6)
        x = jax.random.normal(k[0], (B, S, D), jnp.float32)
        router_w = jax.random.normal(k[1], (D, E), jnp.float32) * D ** (-0.5)
        router_b = jnp.zeros((E,), jnp.float32)
        w1 = jax.random.normal(k[2], (E, D, F), jnp.float32) * 0.02
        w3 = jax.random.normal(k[3], (E, D, F), jnp.float32) * 0.02
        w2 = jax.random.normal(k[4], (E, F, D), jnp.float32) * 0.02
        return {'x': x, 'router_w': router_w, 'router_b': router_b, 'w1': w1, 'w3': w3, 'w2': w2}
    _L1_ffn_all = _L1_ffn_setup()
    _L1_ffn_in = {k: v for k, v in _L1_ffn_all.items() if k in ('router_w', 'router_b', 'w1', 'w3', 'w2')}
    del _L1_ffn_all

    def _L2_xattn_setup():
        import math
        import jax, jax.numpy as jnp
        import numpy as np
        D_MODEL = 128
        N_HEADS = 16
        D_K = D_MODEL // N_HEADS

        def _rope(x):
            s, d = (x.shape[2], x.shape[3])
            pos = jnp.arange(s, dtype=x.dtype)[:, None]
            inv = 10000.0 ** (jnp.arange(0, d, 2, dtype=x.dtype) / d)
            theta = pos / inv
            sin = jnp.repeat(jnp.sin(theta), 2, axis=-1)
            cos = jnp.repeat(jnp.cos(theta), 2, axis=-1)
            rot = jnp.stack([-x[..., 1::2], x[..., 0::2]], axis=-1).reshape(x.shape)
            return x * cos + rot * sin
        key = jax.random.key(seed)
        ks = jax.random.split(key, 12)
        b, s, d = (2, 256, D_MODEL)
        sc = 1.0 / math.sqrt(d)
        inp = {'q': jax.random.normal(ks[0], (b, s, d), jnp.float32), 'k': jax.random.normal(ks[1], (b, s, d), jnp.float32), 'v': jax.random.normal(ks[2], (b, s, d), jnp.float32), 'mask': jnp.ones((b, 1, 1, s), dtype=bool), 'w_q': jax.random.normal(ks[3], (d, d), jnp.float32) * sc, 'b_q': jnp.zeros((d,), jnp.float32), 'w_k': jax.random.normal(ks[4], (d, d), jnp.float32) * sc, 'b_k': jnp.zeros((d,), jnp.float32), 'w_v': jax.random.normal(ks[5], (d, d), jnp.float32) * sc, 'b_v': jnp.zeros((d,), jnp.float32), 'w_o': jax.random.normal(ks[6], (d, d), jnp.float32) * sc, 'b_o': jnp.zeros((d,), jnp.float32)}
        return inp
    _L2_xattn_all = _L2_xattn_setup()
    _L2_xattn_in = {k: v for k, v in _L2_xattn_all.items() if k in ('w_q', 'b_q', 'w_k', 'b_k', 'w_v', 'b_v', 'w_o', 'b_o')}
    del _L2_xattn_all

    def _L2_ffn_setup():
        import jax, jax.numpy as jnp
        import numpy as np
        B, S = (4, 64)
        H = 128
        I = 352
        E = 8
        K = 2
        IS = 176
        key = jax.random.key(seed)
        ks = jax.random.split(key, 8)

        def init(k, shape, fan_in):
            return (jax.random.normal(k, shape, jnp.float32) / np.sqrt(fan_in)).astype(jnp.float32)
        return {'hidden_states': jax.random.normal(ks[0], (B, S, H), jnp.float32), 'gate_w': init(ks[1], (H, E), H), 'Wg': init(ks[2], (E, H, I), H), 'Wu': init(ks[3], (E, H, I), H), 'Wd': init(ks[4], (E, I, H), I), 'Sg': init(ks[5], (H, IS), H), 'Su': init(ks[6], (H, IS), H), 'Sd': init(ks[7], (IS, H), IS)}
    _L2_ffn_all = _L2_ffn_setup()
    _L2_ffn_in = {k: v for k, v in _L2_ffn_all.items() if k in ('gate_w', 'Wg', 'Wu', 'Wd', 'Sg', 'Su', 'Sd')}
    del _L2_ffn_all

    def _L3_xattn_setup():
        import jax, jax.numpy as jnp
        import numpy as np
        D_MODEL = 128
        D_FEATURE = 128
        B, S = (8, 256)
        key = jax.random.key(seed)
        ks = jax.random.split(key, 9)
        s = 1.0 / np.sqrt(D_MODEL)
        return {'queries': jax.random.normal(ks[0], (B, S, D_MODEL), jnp.float32), 'keys': jax.random.normal(ks[1], (B, S, D_MODEL), jnp.float32), 'values': jax.random.normal(ks[2], (B, S, D_MODEL), jnp.float32), 'Wq': jax.random.uniform(ks[3], (D_MODEL, D_FEATURE), jnp.float32, -s, s), 'bq': jax.random.uniform(ks[4], (D_FEATURE,), jnp.float32, -s, s), 'Wk': jax.random.uniform(ks[5], (D_MODEL, D_FEATURE), jnp.float32, -s, s), 'bk': jax.random.uniform(ks[6], (D_FEATURE,), jnp.float32, -s, s), 'Wv': jax.random.uniform(ks[7], (D_MODEL, D_FEATURE), jnp.float32, -s, s), 'bv': jax.random.uniform(ks[8], (D_FEATURE,), jnp.float32, -s, s)}
    _L3_xattn_all = _L3_xattn_setup()
    _L3_xattn_in = {k: v for k, v in _L3_xattn_all.items() if k in ('Wq', 'bq', 'Wk', 'bk', 'Wv', 'bv')}
    del _L3_xattn_all

    def _L3_ffn_setup():
        import jax, jax.numpy as jnp
        import numpy as np
        E = 8
        K = 2
        D = 128
        B, N = (4, 512)
        DC = 64
        key = jax.random.key(seed)
        ks = jax.random.split(key, 6)
        x = jax.random.normal(ks[0], (B, N, D), jnp.float32)
        cond = jax.random.normal(ks[1], (B, N, DC), jnp.float32)
        mask = jnp.ones((B, N), jnp.float32)
        W_shared = jax.random.normal(ks[2], (D, D), jnp.float32) * 0.02
        W_expert = jax.random.normal(ks[3], (D, D), jnp.float32) * 0.02
        W_gate = jax.random.normal(ks[4], (D, E - 1), jnp.float32) * 0.02
        bias = jnp.zeros((D,), jnp.float32)
        return dict(x=x, cond=cond, mask=mask, W_shared=W_shared, W_expert=W_expert, W_gate=W_gate, bias=bias)
    _L3_ffn_all = _L3_ffn_setup()
    _L3_ffn_in = {k: v for k, v in _L3_ffn_all.items() if k in ('cond', 'mask', 'W_shared', 'W_expert', 'W_gate', 'bias')}
    del _L3_ffn_all
    return {'x': x, 'ctx_1024': ctx_1024, 'mask_Bx1x1xS2_ik0': mask_Bx1x1xS2_ik0, 'mask_Bx1x1xS2_bf1': mask_Bx1x1xS2_bf1, 'L0_xattn_Wq': _L0_xattn_in['Wq'], 'L0_xattn_bq': _L0_xattn_in['bq'], 'L0_xattn_Wk': _L0_xattn_in['Wk'], 'L0_xattn_bk': _L0_xattn_in['bk'], 'L0_xattn_Wv': _L0_xattn_in['Wv'], 'L0_xattn_bv': _L0_xattn_in['bv'], 'L0_xattn_Wo': _L0_xattn_in['Wo'], 'L0_xattn_bo': _L0_xattn_in['bo'], 'L0_xattn_m_k': _L0_xattn_in['m_k'], 'L0_xattn_m_v': _L0_xattn_in['m_v'], 'L0_ffn_W1': _L0_ffn_in['W1'], 'L0_ffn_b1': _L0_ffn_in['b1'], 'L0_ffn_W2': _L0_ffn_in['W2'], 'L0_ffn_b2': _L0_ffn_in['b2'], 'L0_ffn_scale': _L0_ffn_in['scale'], 'L1_xattn_Wq': _L1_xattn_in['Wq'], 'L1_xattn_bq': _L1_xattn_in['bq'], 'L1_xattn_Wkv': _L1_xattn_in['Wkv'], 'L1_xattn_bkv': _L1_xattn_in['bkv'], 'L1_xattn_Wproj': _L1_xattn_in['Wproj'], 'L1_xattn_bproj': _L1_xattn_in['bproj'], 'L1_xattn_gq': _L1_xattn_in['gq'], 'L1_xattn_gk': _L1_xattn_in['gk'], 'L1_ffn_router_w': _L1_ffn_in['router_w'], 'L1_ffn_router_b': _L1_ffn_in['router_b'], 'L1_ffn_w1': _L1_ffn_in['w1'], 'L1_ffn_w3': _L1_ffn_in['w3'], 'L1_ffn_w2': _L1_ffn_in['w2'], 'L2_xattn_w_q': _L2_xattn_in['w_q'], 'L2_xattn_b_q': _L2_xattn_in['b_q'], 'L2_xattn_w_k': _L2_xattn_in['w_k'], 'L2_xattn_b_k': _L2_xattn_in['b_k'], 'L2_xattn_w_v': _L2_xattn_in['w_v'], 'L2_xattn_b_v': _L2_xattn_in['b_v'], 'L2_xattn_w_o': _L2_xattn_in['w_o'], 'L2_xattn_b_o': _L2_xattn_in['b_o'], 'L2_ffn_gate_w': _L2_ffn_in['gate_w'], 'L2_ffn_Wg': _L2_ffn_in['Wg'], 'L2_ffn_Wu': _L2_ffn_in['Wu'], 'L2_ffn_Wd': _L2_ffn_in['Wd'], 'L2_ffn_Sg': _L2_ffn_in['Sg'], 'L2_ffn_Su': _L2_ffn_in['Su'], 'L2_ffn_Sd': _L2_ffn_in['Sd'], 'L3_xattn_Wq': _L3_xattn_in['Wq'], 'L3_xattn_bq': _L3_xattn_in['bq'], 'L3_xattn_Wk': _L3_xattn_in['Wk'], 'L3_xattn_bk': _L3_xattn_in['bk'], 'L3_xattn_Wv': _L3_xattn_in['Wv'], 'L3_xattn_bv': _L3_xattn_in['bv'], 'L3_ffn_cond': _L3_ffn_in['cond'], 'L3_ffn_mask': _L3_ffn_in['mask'], 'L3_ffn_W_shared': _L3_ffn_in['W_shared'], 'L3_ffn_W_expert': _L3_ffn_in['W_expert'], 'L3_ffn_W_gate': _L3_ffn_in['W_gate'], 'L3_ffn_bias': _L3_ffn_in['bias']}

def reference(x, ctx_1024, mask_Bx1x1xS2_ik0, mask_Bx1x1xS2_bf1, L0_xattn_Wq, L0_xattn_bq, L0_xattn_Wk, L0_xattn_bk, L0_xattn_Wv, L0_xattn_bv, L0_xattn_Wo, L0_xattn_bo, L0_xattn_m_k, L0_xattn_m_v, L0_ffn_W1, L0_ffn_b1, L0_ffn_W2, L0_ffn_b2, L0_ffn_scale, L1_xattn_Wq, L1_xattn_bq, L1_xattn_Wkv, L1_xattn_bkv, L1_xattn_Wproj, L1_xattn_bproj, L1_xattn_gq, L1_xattn_gk, L1_ffn_router_w, L1_ffn_router_b, L1_ffn_w1, L1_ffn_w3, L1_ffn_w2, L2_xattn_w_q, L2_xattn_b_q, L2_xattn_w_k, L2_xattn_b_k, L2_xattn_w_v, L2_xattn_b_v, L2_xattn_w_o, L2_xattn_b_o, L2_ffn_gate_w, L2_ffn_Wg, L2_ffn_Wu, L2_ffn_Wd, L2_ffn_Sg, L2_ffn_Su, L2_ffn_Sd, L3_xattn_Wq, L3_xattn_bq, L3_xattn_Wk, L3_xattn_bk, L3_xattn_Wv, L3_xattn_bv, L3_ffn_cond, L3_ffn_mask, L3_ffn_W_shared, L3_ffn_W_expert, L3_ffn_W_gate, L3_ffn_bias):
    import jax
    import jax.numpy as jnp

    def _L0_xattn_ref(query, key, value, mask, Wq, bq, Wk, bk, Wv, bv, Wo, bo, m_k, m_v):
        import jax, jax.numpy as jnp
        import numpy as np
        import math
        B, S, D, H, M = (2, 256, 128, 16, 64)
        HD = D // H
        b, nq, d = query.shape
        nk = key.shape[1]
        h, hd, m = (H, HD, M)
        scale = math.sqrt(hd)
        Q = query @ Wq.T + bq
        K = key @ Wk.T + bk
        V = value @ Wv.T + bv
        mk = scale * jnp.broadcast_to(m_k, (b, m, d))
        mv = math.sqrt(m) * jnp.broadcast_to(m_v, (b, m, d))
        K = jnp.concatenate([K, mk], axis=1)
        V = jnp.concatenate([V, mv], axis=1)
        Qh = Q.reshape(b, nq, h, hd).transpose(0, 2, 1, 3)
        Kh = K.reshape(b, nk + m, h, hd).transpose(0, 2, 1, 3)
        Vh = V.reshape(b, nk + m, h, hd).transpose(0, 2, 1, 3)
        energy = jnp.einsum('bhqd,bhkd->bhqk', Qh, Kh) / scale
        masked = jnp.where(mask == 0, jnp.float32(-1e+20), energy[..., :nk])
        energy = jnp.concatenate([masked, energy[..., nk:]], axis=-1)
        attention = jax.nn.softmax(energy, axis=-1)
        x = jnp.einsum('bhqk,bhkd->bhqd', attention, Vh)
        x = x.transpose(0, 2, 1, 3).reshape(b, nq, d)
        return x @ Wo.T + bo

    def _L0_ffn_ref(x, W1, b1, W2, b2, scale):
        import jax, jax.numpy as jnp
        import numpy as np
        LORA_DIM = 16
        LORA_TOKEN_INDEX = 1
        B, S, D, H = (4, 256, 128, 512)
        Bx, Sx, Dx = x.shape
        Hx = W1.shape[0]
        lt = jax.lax.dynamic_slice_in_dim(x, LORA_TOKEN_INDEX, LORA_DIM, axis=1)
        even = lt[:, ::2, :]
        odd = lt[:, 1::2, :]
        m1 = (even[:, :4, :, None] * odd[:, :4, None, :]).reshape(Bx, Hx, Dx)
        m2 = (even[:, 4:, :, None] * odd[:, 4:, None, :]).reshape(Bx, Dx, Hx)
        h = jnp.einsum('bsd,hd->bsh', x, W1) + scale * jnp.einsum('bsd,bhd->bsh', x, m1) + b1
        h = jax.nn.gelu(h, approximate=False)
        out = jnp.einsum('bsh,oh->bso', h, W2) + scale * jnp.einsum('bsh,boh->bso', h, m2) + b2
        return out

    def _L1_xattn_ref(x, ctx, Wq, bq, Wkv, bkv, Wproj, bproj, gq, gk):
        import jax, jax.numpy as jnp
        import numpy as np
        D = 128
        H = 16
        HD = D // H
        EPS = 1e-06

        def rms_norm(x, w):
            xf = x.astype(jnp.float32)
            rms = jnp.sqrt(jnp.mean(xf * xf, axis=-1, keepdims=True) + EPS)
            return (xf / rms * w.astype(jnp.float32)).astype(x.dtype)
        B, S, _ = x.shape
        Sc = ctx.shape[1]
        q = (x @ Wq + bq).reshape(B, S, H, HD)
        q = rms_norm(q, gq).transpose(0, 2, 1, 3)
        kv = (ctx @ Wkv + bkv).reshape(B, Sc, 2, H, HD)
        k = rms_norm(kv[:, :, 0], gk).transpose(0, 2, 1, 3)
        v = kv[:, :, 1].transpose(0, 2, 1, 3)
        scale = 1.0 / jnp.sqrt(jnp.asarray(HD, q.dtype))
        scores = jnp.einsum('bhsd,bhtd->bhst', q, k) * scale
        attn = jax.nn.softmax(scores, axis=-1)
        out = jnp.einsum('bhst,bhtd->bhsd', attn, v)
        out = out.transpose(0, 2, 1, 3).reshape(B, S, D)
        return out @ Wproj + bproj

    def _L1_ffn_ref(x, router_w, router_b, w1, w3, w2):
        import jax, jax.numpy as jnp
        import numpy as np
        B, S, D, F, E, K = (4, 256, 128, 512, 4, 2)
        b, s, d = x.shape
        T = b * s
        e = router_w.shape[1]
        xf = x.reshape(T, d)
        logits = xf @ router_w + router_b
        probs = jax.nn.softmax(logits, axis=-1)
        top_p, top_i = jax.lax.top_k(probs, K)
        top_p = top_p / jnp.sum(top_p, axis=-1, keepdims=True)
        gates = jnp.zeros((T, e), xf.dtype).at[jnp.arange(T)[:, None], top_i].add(top_p)
        h = jax.nn.silu(jnp.einsum('td,edf->etf', xf, w1)) * jnp.einsum('td,edf->etf', xf, w3)
        expert_out = jnp.einsum('etf,efd->etd', h, w2)
        out = jnp.einsum('te,etd->td', gates, expert_out)
        return out.reshape(b, s, d)

    def _L2_xattn_ref(q, k, v, mask, w_q, b_q, w_k, b_k, w_v, b_v, w_o, b_o):
        import math
        import jax, jax.numpy as jnp
        import numpy as np
        D_MODEL = 128
        N_HEADS = 16
        D_K = D_MODEL // N_HEADS

        def _rope(x):
            s, d = (x.shape[2], x.shape[3])
            pos = jnp.arange(s, dtype=x.dtype)[:, None]
            inv = 10000.0 ** (jnp.arange(0, d, 2, dtype=x.dtype) / d)
            theta = pos / inv
            sin = jnp.repeat(jnp.sin(theta), 2, axis=-1)
            cos = jnp.repeat(jnp.cos(theta), 2, axis=-1)
            rot = jnp.stack([-x[..., 1::2], x[..., 0::2]], axis=-1).reshape(x.shape)
            return x * cos + rot * sin
        b = q.shape[0]
        h, dk = (N_HEADS, D_K)
        qh = (q @ w_q + b_q).reshape(b, -1, h, dk).transpose(0, 2, 1, 3)
        kh = (k @ w_k + b_k).reshape(b, -1, h, dk).transpose(0, 2, 1, 3)
        vh = (v @ w_v + b_v).reshape(b, -1, h, dk).transpose(0, 2, 1, 3)
        qh = _rope(qh)
        kh = _rope(kh)
        scores = jnp.einsum('bhqd,bhkd->bhqk', qh, kh) / math.sqrt(dk)
        scores = jnp.where(mask, scores, jnp.finfo(scores.dtype).min)
        attn = jax.nn.softmax(scores, axis=-1)
        out = jnp.einsum('bhqk,bhkd->bhqd', attn, vh)
        out = out.transpose(0, 2, 1, 3).reshape(b, -1, h * dk)
        return out @ w_o + b_o

    def _L2_ffn_ref(hidden_states, gate_w, Wg, Wu, Wd, Sg, Su, Sd):
        import jax, jax.numpy as jnp
        import numpy as np
        B, S = (4, 64)
        H = 128
        I = 352
        E = 8
        K = 2
        IS = 176
        b, s, h = hidden_states.shape
        x = hidden_states.reshape(-1, h)
        T = x.shape[0]
        logits = x @ gate_w
        top_v, top_i = jax.lax.top_k(logits, K)
        top_p = jax.nn.softmax(top_v, axis=-1)
        combine = jnp.zeros((T, E), x.dtype).at[jnp.arange(T)[:, None], top_i].add(top_p)
        g = jnp.einsum('th,ehi->tei', x, Wg)
        u = jnp.einsum('th,ehi->tei', x, Wu)
        d = jnp.einsum('tei,eih->teh', jax.nn.silu(g) * u, Wd)
        expert_out = jnp.einsum('te,teh->th', combine, d)
        shared = jax.nn.silu(x @ Sg) * (x @ Su) @ Sd
        return (expert_out + shared).reshape(b, s, h)

    def _L3_xattn_ref(queries, keys, values, Wq, bq, Wk, bk, Wv, bv):
        import jax, jax.numpy as jnp
        import numpy as np
        D_MODEL = 128
        D_FEATURE = 128
        B, S = (8, 256)
        Q = jnp.einsum('bsd,df->bsf', queries, Wq) + bq
        K = jnp.einsum('bsd,df->bsf', keys, Wk) + bk
        V = jnp.einsum('bsd,df->bsf', values, Wv) + bv
        d_k = K.shape[-1]
        scores = jnp.einsum('bqf,bkf->bqk', Q, K) / jnp.sqrt(jnp.float32(d_k)).astype(Q.dtype)
        p_attn = jax.nn.softmax(scores, axis=-1)
        return jnp.einsum('bqk,bkf->bqf', p_attn, V)

    def _L3_ffn_ref(x, cond, mask, W_shared, W_expert, W_gate, bias):
        import jax, jax.numpy as jnp
        import numpy as np
        E = 8
        K = 2
        D = 128
        B, N = (4, 512)
        DC = 64
        b, n, d = x.shape
        T = b * n
        xf = x.reshape(T, d)
        scores = jax.nn.softmax(xf @ W_gate, axis=-1)
        expert_weights, _ = jax.lax.top_k(scores, K)
        expert_weights = expert_weights / expert_weights.sum(-1, keepdims=True)
        expert_indices = (jnp.arange(T * K) % E).reshape(T, K)
        te = expert_indices.reshape(-1)
        w = expert_weights.reshape(-1)
        capacity = K * T // E
        order = jnp.argsort(te, stable=True)
        sorted_e = te[order]
        hist = jnp.bincount(te, length=E)
        starts = jnp.concatenate([jnp.zeros((1,), hist.dtype), jnp.cumsum(hist)[:-1]])
        pos = jnp.arange(T * K) - starts[sorted_e]
        valid = pos < capacity
        dest = jnp.where(valid, sorted_e * capacity + pos, E * capacity)
        tok = order // K
        gathered = jnp.zeros((E * capacity + 1, d), x.dtype).at[dest].set(xf[tok])
        gathered = gathered[:-1]
        y = gathered @ W_expert.T
        contrib = w[order][:, None] * y[jnp.minimum(dest, E * capacity - 1)]
        moe_out = jnp.zeros((T, d), x.dtype).at[tok].add(jnp.where(valid[:, None], contrib, 0.0))
        shared = xf @ W_shared.T
        out = (shared + moe_out + bias).reshape(b, n, d)
        return out
    x = x + _L0_xattn_ref(_layernorm(x, axis=-1), ctx_1024, ctx_1024, mask_Bx1x1xS2_ik0, L0_xattn_Wq, L0_xattn_bq, L0_xattn_Wk, L0_xattn_bk, L0_xattn_Wv, L0_xattn_bv, L0_xattn_Wo, L0_xattn_bo, L0_xattn_m_k, L0_xattn_m_v)
    x = x + _L0_ffn_ref(_layernorm(x, axis=-1), L0_ffn_W1, L0_ffn_b1, L0_ffn_W2, L0_ffn_b2, L0_ffn_scale)
    x = x + _L1_xattn_ref(_layernorm(x, axis=-1), ctx_1024, L1_xattn_Wq, L1_xattn_bq, L1_xattn_Wkv, L1_xattn_bkv, L1_xattn_Wproj, L1_xattn_bproj, L1_xattn_gq, L1_xattn_gk)
    x = x + _L1_ffn_ref(_layernorm(x, axis=-1), L1_ffn_router_w, L1_ffn_router_b, L1_ffn_w1, L1_ffn_w3, L1_ffn_w2)
    x = x + _L2_xattn_ref(_layernorm(x, axis=-1), ctx_1024, ctx_1024, mask_Bx1x1xS2_bf1, L2_xattn_w_q, L2_xattn_b_q, L2_xattn_w_k, L2_xattn_b_k, L2_xattn_w_v, L2_xattn_b_v, L2_xattn_w_o, L2_xattn_b_o)
    x = x + _L2_ffn_ref(_layernorm(x, axis=-1), L2_ffn_gate_w, L2_ffn_Wg, L2_ffn_Wu, L2_ffn_Wd, L2_ffn_Sg, L2_ffn_Su, L2_ffn_Sd)
    x = x + _L3_xattn_ref(_layernorm(x, axis=-1), ctx_1024, ctx_1024, L3_xattn_Wq, L3_xattn_bq, L3_xattn_Wk, L3_xattn_bk, L3_xattn_Wv, L3_xattn_bv)
    x = x + _L3_ffn_ref(_layernorm(x, axis=-1), L3_ffn_cond, L3_ffn_mask, L3_ffn_W_shared, L3_ffn_W_expert, L3_ffn_W_gate, L3_ffn_bias)
    return x

_drawn_inputs = setup_inputs


def setup_inputs(seed=0):
    import zlib

    import numpy as np

    out = dict(_drawn_inputs(seed))
    spreads = {'L0_xattn_bq': (0.0, 0.8),
     'L0_xattn_bk': (0.0, 0.8),
     'L0_xattn_bv': (0.0, 0.414),
     'L0_xattn_bo': (0.0, 0.1),
     'L0_ffn_b1': (0.0, 0.1),
     'L0_ffn_b2': (0.0, 0.1),
     'L1_xattn_bq': (0.0, 2.0),
     'L1_xattn_bkv': (0.0, 0.1),
     'L1_xattn_bproj': (0.0, 0.1),
     'L1_xattn_gq': (1.0, 0.6),
     'L1_xattn_gk': (1.0, 0.6),
     'L1_ffn_router_b': (0.0, 0.8),
     'L2_xattn_b_q': (0.0, 0.1),
     'L2_xattn_b_k': (0.0, 0.286),
     'L2_xattn_b_v': (0.0, 0.1),
     'L2_xattn_b_o': (0.0, 0.1),
     'L3_ffn_bias': (0.0, 0.1)}
    factors = {'L0_xattn_Wq': 8.0,
     'L0_xattn_Wk': 8.0,
     'L0_xattn_Wv': 4.374,
     'L0_xattn_Wo': 3.055,
     'L0_xattn_m_k': 8.0,
     'L0_xattn_m_v': 4.794,
     'L1_xattn_Wq': 2.931,
     'L1_ffn_router_w': 3.202,
     'L1_ffn_w1': 2.871,
     'L1_ffn_w3': 3.08,
     'L1_ffn_w2': 2.689,
     'L3_xattn_bq': 22.413,
     'L3_xattn_bk': 64.0,
     'L3_ffn_W_gate': 64.0}
    for name, (base, spread) in spreads.items():
        noise = np.random.default_rng([zlib.crc32(name.encode()), seed]).standard_normal(out[name].shape)
        drawn = base * np.exp(spread * noise) if base else spread * noise
        out[name] = jnp.asarray(drawn.astype(out[name].dtype))
    for name, factor in factors.items():
        out[name] = (out[name] * factor).astype(out[name].dtype)
    return out
```

```python
import concourse.bass as bass
from concourse import mybir
from contextlib import ExitStack
import numpy as np

F32 = mybir.dt.float32
F32R = mybir.dt.float32r
I32 = mybir.dt.int32
U8 = mybir.dt.uint8
ALU = mybir.AluOpType
ACT = mybir.ActivationFunctionType
AX = mybir.AxisListType

B, S, D = 4, 512, 128
T = S // 128
H, HD = 16, 8
G, HL = 4, 4
KC, KM = 154, 64
KJ = KC // 2
PR = HL * 3 * HD
KX_ROWS = PR + 1
K_ALL = KX_ROWS + HL
XW = 100
R0, C0 = 125, 7
R1, C1 = 124, 5
HALF0 = 2 * KC + 2 * KM
BIG = 1.96875 * 2.0 ** 127
LN_EPS, RMS_EPS = 1e-5, 1e-6
SCALE = float(np.float32(1.0) / np.sqrt(np.float32(HD)))
SCALE3 = float(np.float32(1.0) / np.sqrt(np.float32(D)))
E1, F1 = 4, 512
E2, F2, FS = 8, 352, 176
E3 = 7
W2COLS = E2 * F2 + FS

KINDS = ["A", "F0", "A", "F1", "A", "F2", "A3", "F3"]
ITEMS = [(kind, n // 2, b) for n, kind in enumerate(KINDS) for b in range(B)]


def is_attn(i):
    return 0 <= i < len(ITEMS) and ITEMS[i][0] == "A"


def is_ffn(i):
    return 0 <= i < len(ITEMS) and ITEMS[i][0] != "A"


def item_of(a):
    return (a // B) * 8 + a % B


def chunk_shape(layer):
    return (R0, C0) if layer == 0 else (R1, C1)


def ffn_tiles(kind):
    if kind == "F0":
        return [(0, j * 128, 128, j) for j in range(4)]
    if kind == "F1":
        return [(e, e * F1 + j * 128, 128, e * 4 + j) for e in range(E1) for j in range(4)]
    out = [(e, e * F2 + j * 128, min(128, F2 - j * 128), e * 3 + j) for e in range(E2) for j in range(3)]
    return out + [(E2, E2 * F2 + j * 88, 88, E2 * 3 + j) for j in range(2)]


def weight_chunks(layer):
    if layer == 1:
        return [(m, e * F1, F1) for e in range(E1) for m in range(2)]
    return [(m, e * F2, F2) for e in range(E2) for m in range(2)] + [(m, E2 * F2, FS) for m in range(2)]


def n_slots(i):
    kind, layer, b = ITEMS[i]
    if kind == "A":
        return 4 * chunk_shape(layer)[1]
    return {"F0": 4, "F1": 16, "F2": 26, "A3": 1, "F3": 1}[kind]


def plan(i):
    slots = {}

    def put(n, *piece):
        slots.setdefault(n, []).append(piece)

    kind, layer, b = ITEMS[i]
    N = n_slots(i)
    a = layer * B + b
    nxt = i + 1
    if kind == "A":
        if is_attn(nxt):
            a1 = a + 1
            put(0, "kexp", a1)
            put(0, "q", a1)
            put(1, "qchain", a1)
            put(2, "v", a1, 0)
            put(3, "v", a1, 1)
            put(5, "qsplit", a1)
            for g in range(G):
                put(6 + g, "qxt", a1, g)
            left = list(range(G * T))
            n = 10
            while left:
                take = 2 if N == 20 else 1
                for k in left[:take]:
                    put(n, "max", a1, k)
                left = left[take:]
                n += 1
            put(max(n, N + 3), "mt", a1)
        if a + 2 < 12:
            put(4, "kproj", a + 2)
            put(5, "kchain", a + 2)
            put(N + 6, "kt", a + 2)
        if is_ffn(nxt):
            put(2, "ln", nxt)
            put(8, "xt", nxt)
            put(9, "after_xt", nxt)
            put(14, "late", nxt)
        if is_attn(i + 2):
            put(1, "ln", i + 2)
            put(N + 4, "xt", i + 2)
        if layer > 0:
            n_w = len(weight_chunks(layer))
            for c in range(b * n_w // B, (b + 1) * n_w // B):
                put(4 + 3 * (c - b * n_w // B), "w", layer, c)
    else:
        if is_ffn(nxt):
            put(0, "ln", nxt)
            at = {"F0": 1, "F1": 6, "F2": 10, "A3": 0, "F3": 0}[kind]
            put(at, "xt", nxt)
            put(at, "after_xt", nxt)
            put(at + (2 if kind in ("F1", "F2") else 1), "late", nxt)
        if is_attn(nxt):
            a1 = ITEMS[nxt][1] * B + ITEMS[nxt][2]
            step = {"F0": 0, "F1": 1, "F2": 1}[kind]
            put(0, "kexp", a1)
            put(0, "q", a1)
            put(step, "qchain", a1)
            put(step, "v", a1, 0)
            put(2 * step, "v", a1, 1)
            put(3 * step, "qsplit", a1)
            for g in range(G):
                put(4 * step + (g // 2) * step, "qxt", a1, g)
            for k in range(G * T):
                put(min(N, 6 + k // 2) if step else N, "max", a1, k)
            put(N + 1, "mt", a1)
        if is_attn(i + 2):
            put(1, "ln", i + 2)
            put(N + 2, "xt", i + 2)
    return slots


def all_slots(i):
    p = plan(i)
    return max([n_slots(i) + 4] + [n + 1 for n in p]), p


class Signal:

    def __init__(self, sem, known, step=1):
        self.sem, self.known, self.step, self.count, self.seen = sem, known, step, 0, {}

    def mark(self, label):
        assert label not in self.seen, label
        self.count += self.step
        self.seen[label] = self.count
        return self.sem, self.step

    def more(self, label):
        self.count += self.step
        self.seen[label] = self.count
        return self.sem, self.step

    def at(self, label):
        return self.sem, (self.known[label] if self.known is not None else 1)


DMA_SIGNALS = ["w_ffn3_in", "w_proj3_in", "x_in0", "x_in1", "x_in2", "x_in3", "const_in", "ctx_in", "mask_in", "wA_in0", "wA_in1", "wA_in2", "w_ffn0_in",
               "cr_in0", "cr_in1", "stage_in0", "stage_in1", "wd_in",
               "shift_in", "lora_in", "w3_in", "mem_in", "out_done"]
SIGNALS = [
    "init_pool", "init_dve", "init_act", "mask_ready", "gkq_ready", "mem_ready", "mem_kt", "mem_kb", "mem_kt_psum",
    "ln_stats", "ln_aggr", "ln_var", "ln_rstd", "xn", "bias_in_x", "xt_psum", "xt", "xh", "xl",
    "k_psum", "k", "k_sq", "k_ms", "k_var", "k_rr", "k_n", "k_ready", "k_t1", "k_t2", "kx_h", "kx_b", "kx_l",
    "kt_psum", "kt", "kb",
    "v_psum", "vb",
    "q_psum", "q", "q_sq", "q_ms", "q_var", "q_rr", "q_ready", "q_t1", "q_t2", "qx_h", "qx_l", "qxt_psum", "qxt",
    "mx_psum", "mx", "mx_mem", "mx_all", "mt_psum", "mt",
    "st", "p", "pv", "dn", "rden", "on", "o_psum", "resid",
    "up", "act", "h", "h_gelu", "y", "acc", "lg_psum", "lg", "lg_nm", "lg_sh", "lg_e", "lg_c", "lg_es", "lg_sum", "lg_r", "gates",
    "lora_bd", "lora_psum", "lora_w", "lora_h", "lora_l", "w_h", "w_l",
    "a3_psum", "a3_qk", "a3_v", "a3_s", "a3_nm", "a3_nms", "a3_p", "a3_r", "a3_ptp", "a3_pt", "a3_o", "f3_psum", "f3_y",
]

ORDER = ["x", "ctxT", "mask0", "mask2", "wqT0", "wkT0", "wvT0", "woT0", "bq0", "bk0", "bv0", "bo0", "mk0", "mvT0",
         "w1T0", "b1T0", "w2T0", "b2_0", "scale0",
         "wq1", "wkv1", "wo1", "bq1", "bkv1", "bo1", "gq1", "gk1", "rw1", "rb1", "w1_1", "w3_1", "w2_1",
         "wq2", "wk2", "wv2", "wo2", "bq2", "bk2", "bv2", "bo2", "gw2", "wg2", "wu2", "wd2", "sg2", "su2", "sd2",
         "wq3", "bq3", "wk3", "bk3", "wv3", "bv3", "we3T", "ws3T", "wgate3", "bias3",
         "ident", "maskk", "mv0", "mv1", "ind0", "cosq", "nsinq", "sinq", "cosk", "nsink", "sink", "lt", "eye4"]


def program(nc, A, out, known):
    ctx = ExitStack()
    with ctx:
        def sb(name, shape, dt=F32):
            return ctx.enter_context(nc.sbuf_tensor(name, shape, dt))

        sig = {}
        for name in SIGNALS + DMA_SIGNALS:
            step = 16 if name in DMA_SIGNALS else 1
            sig[name] = Signal(ctx.enter_context(nc.semaphore(name)), known[name] if known else None, step)

        PS = ctx.enter_context(nc.psum_tensor("PS", [128, 8, 512], F32))
        x = sb("x_res", [128, B * T, D])
        ident = sb("ident_sb", [128, 128])
        ctxT = sb("ctxT_sb", [128, B, KC])
        CR = sb("ctx_rep", [128, 2, R0 * C0])
        arena = sb("arena", [128, 12288], F32R)
        WD = sb("down_w", [128, 26 * 128])
        work = sb("work", [128, 5120])
        QXT = sb("qxt_sb", [K_ALL, 2, G, S], F32R)
        KB1 = sb("kb_sb", [K_ALL, 2, G, R1 * C1], F32R)
        KT = sb("kt_sb", [K_ALL, 2, G, KC])
        KX = sb("kx_sb", [KJ, 2, G, XW])
        QX = sb("qx_sb", [128, T, G, XW])
        q = sb("q_sb", [128, S])
        qa = sb("qa_sb", [128, S])
        qb = sb("qb_sb", [128, S])
        k = sb("k_sb", [KJ, 2 * D])
        ka = sb("ka_sb", [KJ, 2 * D])
        kb = sb("kb_tmp", [KJ, 2 * D])
        VB = sb("vb_sb", [R0, 2, C0, D])
        xn = sb("xn_sb", [128, 2, T, D])
        xT = sb("xt_sb", [128, 2, S])
        xH = sb("xh_sb", [128, 2, S], F32R)
        xL = sb("xl_sb", [128, 2, S], F32R)
        stage = sb("stage", [128, 2, 512])
        MV0 = sb("mv0_sb", [R0, C0, HL * HD])
        MV1 = sb("mv1_sb", [R1, C1, HL * HD])
        IND0 = sb("ind0_sb", [1, R0 * C0])
        maskk = sb("maskk_sb", [K_ALL, HL])
        WA = sb("w_attn", [128, 2, 4, D])
        BQ = sb("b_q", [128, 2, D])
        BK = sb("b_k", [KJ, 2, D])
        BVr = sb("b_v", [1, 3, D])
        BO = sb("b_out", [128, 5, D])
        KEEP = sb("keep", [KJ, 3, B, 2])
        KBIAS = sb("kbias", [KJ, 3, B, 2])
        mraw0 = sb("mask_raw0", [KJ, B, 2], I32)
        mraw2 = sb("mask_raw2", [KJ, B, 2], U8)
        ropeq = sb("rope_q", [128, T, 16])
        ropek = sb("rope_k", [KJ, 2, 16])
        gq = sb("gq_sb", [KJ, 2, HD])
        half = sb("minus_half", [128, 64])
        st6 = sb("bn_st", [128, 2, T, 6])
        mvar = sb("bn_mv", [128, 2, T, 2])
        rstd = sb("rstd", [128, 2, T])
        qms = sb("q_ms_sb", [128, T * H])
        qrr = sb("q_rr_sb", [128, T * H])
        kms = sb("k_ms_sb", [KJ, 2 * H])
        krr = sb("k_rr_sb", [KJ, 2 * H])
        mneg = sb("mneg", [128, 2, T, H])
        mneg2 = sb("mneg_mem", [128, T, H])
        mT = sb("mt_sb", [H, S], F32R)
        b1T = sb("b1t", [128, 4])
        scale0 = sb("scale0_sb", [128, 1])
        eye4 = sb("eye4_sb", [4, 4])
        LT = sb("lt_sb", [128, 8, 8])
        RW1 = sb("rw1_sb", [128, E1])
        RB1 = sb("rb1_sb", [128, E1])
        GW2 = sb("gw2_sb", [128, E2])
        lg = sb("lg_sb", [128, T, 8])
        lsh = sb("lsh_sb", [128, T, 8])
        le = sb("le_sb", [128, T, 8])
        lga = sb("lga_sb", [128, T, 8, 8])
        lgb = sb("lgb_sb", [128, T, 8, 8])
        lsm = sb("lsm_sb", [128, 4, T])
        gates = sb("gates_sb", [128, 2, T, 8])
        bqk3 = sb("bqk3_sb", [128, 2])
        stage1 = stage[:, :, :].rearrange("p r n -> p (r n)")
        MKX = stage1[0:KM, 0:G * XW].rearrange("p (g n) -> p g n", g=G)
        mk = stage1[0:KM, 400:400 + D]
        mvT = stage1[:, 528:528 + KM]
        KTM = stage1[0:K_ALL, 592:592 + G * KM].rearrange("p (g n) -> p g n", g=G)
        EV = qb[0:4, 0:2 * D].rearrange("p (n c) -> p n c", n=2)
        OD = qb[0:4, 2 * D:4 * D].rearrange("p (n c) -> p n c", n=2)
        EBD = work[0:4, 4096:5120].rearrange("p (n c) -> p n c", n=2)
        W3 = WA[:, 1, 0:3, :]
        BV3 = BK[:, 1, :]
        WF3 = WA[:, 0, :, :].rearrange("p n c -> p (n c)")

        W1T = WD[:, 0:512]
        W2T = WD[:, 512:1024]
        W2E = WD[:, 1024:2048].rearrange("p (r n) -> p r n", r=2)
        MR = WD[:, 2048:2048 + R0 * C0]
        KB0 = arena[0:K_ALL, 0:2 * G * R0 * C0].rearrange("p (r g n) -> p r g n", r=2, g=G)
        W1E = arena[:, 7168:7168 + 2048].rearrange("p (r h n) -> p r h n", r=2, h=2)
        UP1 = arena[:, 0:8192].rearrange("p (m h n) -> p m h n", m=2, h=2)
        UP2 = arena[:, 0:4 * W2COLS].rearrange("p (m h n) -> p m h n", m=2, h=2)
        P = work[:, 0:3072].rearrange("p (r n) -> p r n", r=6)
        RD, ON = work[:, 3072:3584], work[:, 3584:4096]
        HH = work[:, 0:4096].rearrange("p (r j n) -> p r j n", r=2, j=4)
        SS = work[:, 4096:5120].rearrange("p (r n) -> p r n", r=2)
        QT3, KT3 = work[:, 0:512], work[:, 512:512 + KC]
        V3 = work[0:KJ, 768:1024].rearrange("p (j n) -> p j n", j=2)
        P3 = work[:, 1024:1024 + T * KC].rearrange("p (t n) -> p t n", t=T)
        PT3 = work[0:KJ, 2048:3072].rearrange("p (b n) -> p b n", b=2)

        def KB(layer):
            return KB0 if layer == 0 else KB1

        def UP(layer):
            return UP1 if layer == 1 else UP2

        def layout0(t):
            v = t[:, 0:2 * HALF0].rearrange("p (f n) -> p f n", f=2)
            return (v[:, :, 0:2 * KC].rearrange("p f (h n) -> p f h n", h=2),
                    v[:, :, 2 * KC:HALF0].rearrange("p f (h n) -> p f h n", h=2))

        def first_of_kind(i):
            return i > 0 and ITEMS[i][2] == 0

        def bias_slot(i):
            kind, layer, b = ITEMS[i]
            return {"A": layer, "F0": 3, "F3": 4}.get(kind)

        def mx_banks(i_main, kk):
            if ITEMS[i_main][0] == "A":
                return (4, 2)[kk % 2], kk - 2
            return 4, kk - 1

        block = ctx.enter_context(nc.Block())

        @block.sync
        def _(sp):
            def load_cr(sp, a):
                if a >= 2:
                    sp.wait_ge(*sig["v_psum"].at((a - 2, 1)))
                src = A["ctxT"][:, a % B, :]
                if a < B:
                    ctx_cols, _ = layout0(CR[:, a % 2, :])
                    for f in range(2):
                        sp.dma_start(ctx_cols[:, f, :, :], src[:, None, :].to_broadcast([128, 2, KC])).then_inc(*sig[f"cr_in{a % 2}"].more(a))
                else:
                    sp.dma_start(CR[:, a % 2, 0:HL * KC].rearrange("p (h n) -> p h n", h=HL),
                                 src[:, None, :].to_broadcast([128, HL, KC])).then_inc(*sig[f"cr_in{a % 2}"].more(a))

            def mt_dma(sp, a):
                sp.wait_ge(*sig["mt"].at(a))
                for g in range(G):
                    sp.dma_start(QXT[KX_ROWS:K_ALL, a % 2, g, :].bitcast(F32), mT[g * HL:(g + 1) * HL, :].bitcast(F32)).then_inc(*sig["shift_in"].more(a))

            def stage_dma(sp, layer, c):
                which, lo, w = weight_chunks(layer)[c]
                serial = c + (8 if layer == 2 else 0)
                if serial >= 2:
                    sp.wait_ge(*sig["w_l"].at(serial - 2))
                if layer == 1:
                    src = A[("w1_1", "w3_1")[which]][lo // F1]
                elif lo < E2 * F2:
                    src = A[("wg2", "wu2")[which]][lo // F2]
                else:
                    src = A[("sg2", "su2")[which]]
                sp.dma_start(stage[:, serial % 2, 0:w], src).then_inc(*sig[f"stage_in{serial % 2}"].mark(serial))

            def lora_dma(sp, j):
                sp.wait_ge(*sig["xn"].at(j))
                if ITEMS[j][2] > 0:
                    sp.wait_ge(*sig["lora_psum"].at(j - 1))
                for n in range(2):
                    sp.dma_start(EV[:, n, :], xn[1 + 8 * n:9 + 8 * n:2, j % 2, 0, :]).then_inc(*sig["lora_in"].more(j))
                    sp.dma_start(OD[:, n, :], xn[2 + 8 * n:10 + 8 * n:2, j % 2, 0, :]).then_inc(*sig["lora_in"].more(j))

            def load(dst, src, name, label):
                sp.dma_start(dst, src).then_inc(*sig[name].more(label))

            xv = A["x"].rearrange("b (t p) d -> p b t d", p=128)
            for b in range(B):
                load(x[:, b * T:(b + 1) * T, :], xv[:, b, :, :], f"x_in{b}", 0)
                if b == 0:
                    load(ident[:, :], A["ident"], "const_in", 0)
                    load(ctxT[:, :, :], A["ctxT"], "ctx_in", 0)
                    load(mraw0[:, :, :], A["mask0"], "mask_in", 0)
                    load(mraw2[:, :, :], A["mask2"], "mask_in", 0)
                    for n, name in enumerate(["wqT0", "wkT0", "wvT0", "woT0"]):
                        load(WA[:, 0, n, :], A[name], "wA_in0", 0)
                    for dst, name in ((BQ[:, 0, :], "bq0"), (BK[:, 0, :], "bk0"), (BVr[:, 0, :], "bv0"), (BO[:, 0, :], "bo0")):
                        load(dst, A[name][None, :].to_broadcast([dst.shape[0], D]), "wA_in0", 0)
                    load(mk[:, :], A["mk0"], "mem_in", 0)
                    load(mvT[:, :], A["mvT0"], "mem_in", 0)
                    load(maskk[:, :], A["maskk"], "const_in", 0)
                    load(MV0[:, :, :], A["mv0"], "const_in", 0)
                    load(IND0[:, :], A["ind0"], "const_in", 0)
            for a in range(2):
                sp.wait_ge(*sig["init_pool"].at(0))
                load_cr(sp, a)
            for dst, name in ((W1T, "w1T0"), (W2T.rearrange("p (j n) -> p j n", j=4), "w2T0"), (b1T[:, :], "b1T0"), (eye4[:, :], "eye4"),
                              (scale0[:, :], None), (BO[:, 3, :], "b2_0")):
                src = A["scale0"].to_broadcast([128, 1]) if name is None else A[name]
                if name == "b2_0":
                    src = src[None, :].to_broadcast([128, D])
                load(dst, src, "w_ffn0_in", 0)
            for n, (name, lo) in enumerate([("wq1", 0), ("wkv1", 0), ("wkv1", D), ("wo1", 0)]):
                load(WA[:, 1, n, :], A[name][:, lo:lo + D], "wA_in1", 0)
            for dst, name, lo in ((BQ[:, 1, :], "bq1", 0), (BK[:, 1, :], "bkv1", 0), (BVr[:, 1, :], "bkv1", D), (BO[:, 1, :], "bo1", 0)):
                load(dst, A[name][None, lo:lo + D].to_broadcast([dst.shape[0], D]), "wA_in1", 0)
            for j, name in enumerate(["gq1", "gk1"]):
                load(gq[:, j, :], A[name][None, :].to_broadcast([KJ, HD]), "wA_in1", 0)
            load(MV1[:, :, :], A["mv1"], "wA_in1", 0)
            load(LT[:, :, :], A["lt"][None, :, :].to_broadcast([128, 8, 8]), "w3_in", 0)
            load(RW1[:, :], A["rw1"], "w3_in", 0)
            load(RB1[:, :], A["rb1"][None, :].to_broadcast([128, E1]), "w3_in", 0)
            load(GW2[:, :], A["gw2"], "w3_in", 0)
            for lo, hi, nq, nk in ((0, 8, "cosq", "cosk"), (8, 12, "nsinq", "nsink"), (12, 16, "sinq", "sink")):
                load(ropeq[:, :, lo:hi], A[nq], "wA_in2", 0)
                load(ropek[:, :, lo:hi], A[nk], "wA_in2", 0)
            load(bqk3[:, 0:1], A["bq3"].rearrange("(p n) -> p n", n=1), "w3_in", 0)
            load(bqk3[:, 1:2], A["bk3"].rearrange("(p n) -> p n", n=1), "w3_in", 0)
            load(BO[:, 4, :], A["bias3"][None, :].to_broadcast([128, D]), "w3_in", 0)

            mt_dma(sp, 0)
            for i in range(len(ITEMS)):
                total, pieces = all_slots(i)
                kind, layer, b = ITEMS[i]
                if i == 2 * B - 3:
                    sp.wait_ge(*sig["resid"].at(B - 1))
                    for n, name in enumerate(["wq2", "wk2", "wv2", "wo2"]):
                        load(WA[:, 0, n, :], A[name], "wA_in2", 0)
                    for dst, name in ((BQ[:, 0, :], "bq2"), (BK[:, 0, :], "bk2"), (BVr[:, 2, :], "bv2"), (BO[:, 2, :], "bo2")):
                        load(dst, A[name][None, :].to_broadcast([dst.shape[0], D]), "wA_in2", 0)
                if i == 4 * B - 3:
                    sp.wait_ge(*sig["resid"].at(3 * B - 1))
                    for n, name in enumerate(["wq3", "wk3", "wv3"]):
                        load(W3[:, n, :], A[name], "w_proj3_in", 0)
                    load(BV3[:, :], A["bv3"][None, :].to_broadcast([KJ, D]), "w_proj3_in", 0)
                if i == 6 * B - 3:
                    sp.wait_ge(*sig["resid"].at(5 * B - 1))
                    load(WF3[:, 0:D], A["we3T"], "w_ffn3_in", 0)
                    load(WF3[:, D:2 * D], A["ws3T"], "w_ffn3_in", 0)
                    load(WF3[:, 2 * D:2 * D + E3], A["wgate3"], "w_ffn3_in", 0)
                if kind == "A" and b == 0 and layer > 0:
                    sp.wait_ge(*sig["resid"].at(i - 1))
                    if layer == 1:
                        sp.dma_start(WD[:, 0:2048].rearrange("p (c n) -> p c n", c=16), A["w2_1"]).then_inc(*sig["wd_in"].more(1))
                    else:
                        for e in range(E2):
                            for j, w in ((0, 2 * 128), (2, 96)):
                                dst = WD[0:min(w, 128), (e * 3 + j) * 128:(e * 3 + j + (w + 127) // 128) * 128]
                                src = A["wd2"][e, j * 128:j * 128 + w, :]
                                if j == 0:
                                    dst = dst.rearrange("p (c n) -> p c n", c=2)
                                    src = src.rearrange("(c p) n -> p c n", c=2)
                                sp.dma_start(dst, src).then_inc(*sig["wd_in"].more(2))
                        sp.dma_start(WD[0:88, 24 * 128:26 * 128].rearrange("p (c n) -> p c n", c=2),
                                     A["sd2"].rearrange("(c p) n -> p c n", c=2)).then_inc(*sig["wd_in"].more(2))
                for n in range(total):
                    for piece in pieces.get(n, []):
                        if piece[0] == "mt":
                            mt_dma(sp, piece[1])
                        elif piece[0] == "w":
                            stage_dma(sp, piece[1], piece[2])
                        elif piece[0] == "xt" and ITEMS[piece[1]][0] == "F0":
                            lora_dma(sp, piece[1])
                        elif piece[0] == "v" and piece[2] == 1 and piece[1] + 1 < 12:
                            if piece[1] + 1 >= 2:
                                sp.wait_ge(*sig["v_psum"].at((piece[1] - 1, 1)))
                            load_cr(sp, piece[1] + 1)
                if kind == "F3":
                    sp.wait_ge(*sig["f3_y"].at(i))
                    sp.dma_start(out.rearrange("b (t p) d -> p b t d", p=128)[:, b, :, :],
                                 x[:, b * T:(b + 1) * T, :]).then_inc(*sig["out_done"].mark(b))
            sp.wait_ge(*sig["out_done"].at(B - 1))

        @block.tensor
        def _(pe):
            def k_proj(a):
                layer, b = a // B, a % B
                if a == 0:
                    pe.wait_ge(*sig["ctx_in"].at(0))
                if b == 0:
                    pe.wait_ge(*sig[f"wA_in{layer}"].at(0))
                if a >= 2 and is_attn(item_of(a - 2) + 1):
                    pe.wait_ge(*sig["vb"].at((a - 1, 1)))
                elif a >= 1:
                    pe.wait_ge(*sig["kt"].at(a - 1))
                for j in range(2):
                    mm = pe.matmul(PS[0:KJ, 5, j * D:(j + 1) * D], ctxT[:, b, j * KJ:(j + 1) * KJ], WA[:, layer % 2, 1, :],
                                   start=True, stop=True)
                mm.then_inc(*sig["k_psum"].mark(a))

            def k_transposes(a):
                pe.wait_ge(*sig["kx_l"].at(a))
                pe.wait_ge(*sig["kx_b"].at(a))
                last_bank4_5(a)
                for g in range(G):
                    for j in range(2):
                        mm = pe.transpose(PS[0:KX_ROWS, 4 + g // 2, (g % 2) * KC + j * KJ:(g % 2) * KC + (j + 1) * KJ],
                                          KX[:, j, g, 0:KX_ROWS], ident[0:KJ, 0:KJ])
                mm.then_inc(*sig["kt_psum"].mark(a))

            def last_bank4_5(a):
                pe.wait_ge(*sig["k"].at(a))
                if a >= 2:
                    if is_attn(item_of(a - 2) + 1):
                        pe.wait_ge(*sig["mt"].at(a - 1))
                    if is_attn(item_of(a - 2) + 2):
                        pe.wait_ge(*sig["xt"].at(item_of(a - 2) + 2))
                    if is_ffn(item_of(a - 2) + 1):
                        pe.wait_ge(*sig["xt"].at(item_of(a - 2) + 1))
                        kindn = ITEMS[item_of(a - 2) + 1][0]
                        if kindn == "F0":
                            pe.wait_ge(*sig["lora_w"].at((item_of(a - 2) + 1, 1)))
                        else:
                            pe.wait_ge(*sig["lg"].at(item_of(a - 2) + 1))

            def v_blocks(a, part):
                layer, b = a // B, a % B
                rows, chunks = chunk_shape(layer)
                if part == 0:
                    pe.wait_ge(*sig[f"cr_in{a % 2}"].at(a))
                    if a >= 1:
                        pe.wait_ge(*sig["q"].at(a))
                    if a == 0:
                        pe.wait_ge(*sig["mem_ready"].at(0))
                        pe.wait_ge(*sig["const_in"].at(0))
                        pe.wait_ge(*sig["kt"].at(1))
                if part == 1 and a >= 1:
                    if a > 1:
                        pe.wait_ge(*sig["kt"].at(a))
                for c in range(4 * part, min(4 * part + 4, chunks)):
                    o = PS[0:rows, 4 + part, (c % 4) * D:(c % 4 + 1) * D]
                    cols = slice(c * rows, (c + 1) * rows)
                    mem = layer == 0 and c in (2, 3, 5, 6)
                    pe.matmul(o, CR[:, a % 2, cols], WA[:, layer % 2, 2, :], start=True, stop=False)
                    ind = IND0[:, cols] if layer == 0 else IND0[:, 0:rows]
                    mm = pe.matmul(o, ind, BVr[:, layer, :], start=False, stop=not mem)
                    if mem:
                        mm = pe.matmul(o, MR[:, cols], ident[:, :], start=False, stop=True)
                mm.then_inc(*sig["v_psum"].mark((a, part)))

            def xt(j):
                pe.wait_ge(*sig["xn"].at(j))
                if j >= 1:
                    bank4_free_for_xt(j)
                for t in range(T):
                    mm = pe.transpose(PS[:, 4, t * 128:(t + 1) * 128], xn[:, j % 2, t, :], ident[:, :])
                mm.then_inc(*sig["xt_psum"].mark(j))

            def bank4_free_for_xt(j):
                if is_attn(j):
                    if j == 1:
                        pe.wait_ge(*sig["mt"].at(0))
                    else:
                        if is_attn(j - 1):
                            pe.wait_ge(*sig["mt"].at(ITEMS[j - 1][1] * B + ITEMS[j - 1][2]))
                        else:
                            pe.wait_ge(*sig["xt"].at(j - 1))
                            pe.wait_ge(*sig["lg" if ITEMS[j - 1][0] != "F0" else "lora_w"].at(j - 1 if ITEMS[j - 1][0] != "F0" else (j - 1, 1)))
                elif ITEMS[j][2] == 0 and is_attn(j - 1):
                    a_last = ITEMS[j - 1][1] * B + 3
                    pe.wait_ge(*sig["mt"].at(a_last))
                    if a_last + 1 < 12:
                        pe.wait_ge(*sig["kt"].at(a_last + 1))
                else:
                    pe.wait_ge(*sig["xt"].at(j - 1))
                    if ITEMS[j - 1][0] == "F0":
                        pe.wait_ge(*sig["lora_w"].at((j - 1, 1)))
                    if ITEMS[j][2] == 1 and is_attn(j - 2) and ITEMS[j][1] < 2:
                        pe.wait_ge(*sig["kt"].at((ITEMS[j][1] + 1) * B + 1))

            def q_proj(a):
                i, layer = item_of(a), a // B
                pe.wait_ge(*sig["xt"].at(i))
                if a == 0:
                    pe.wait_ge(*sig["vb"].at((0, 0)))
                elif is_attn(i - 1):
                    pe.wait_ge(*sig["kt"].at(a))
                for t in range(T):
                    mm = pe.matmul(PS[:, 4, t * D:(t + 1) * D], xT[:, i % 2, t * 128:(t + 1) * 128], WA[:, layer % 2, 0, :],
                                   start=True, stop=True)
                mm.then_inc(*sig["q_psum"].mark(a))

            def qxt(a, g):
                bank = 5 - g % 2
                pe.wait_ge(*sig["qx_l"].at(a))
                if g == 0:
                    pe.wait_ge(*sig["vb"].at((a, 0)))
                    pe.wait_ge(*sig["vb"].at((a, 1)))
                    if a >= 1 and is_attn(item_of(a) - 1) and a + 1 < 12:
                        pe.wait_ge(*sig["k"].at(a + 1))
                if g >= 2:
                    pe.wait_ge(*sig["qxt"].at((a, g - 2)))
                for t in range(T):
                    mm = pe.transpose(PS[0:KX_ROWS, bank, t * 128:(t + 1) * 128], QX[:, t, g, 0:KX_ROWS], ident[:, :])
                mm.then_inc(*sig["qxt_psum"].mark((a, g)))

            def scores_for_max(i_main, a, kk):
                g, t, layer = kk // T, kk % T, a // B
                bank, before = mx_banks(i_main, kk)
                pe.wait_ge(*sig["qxt"].at((a, g)))
                pe.wait_ge(*sig["kb"].at((a, g)))
                if before >= 0:
                    pe.wait_ge(*sig["mx"].at((a, before)))
                elif bank == 4:
                    pe.wait_ge(*sig["qxt"].at((a, 3)))
                lhsT = QXT[0:KX_ROWS, a % 2, g, t * 128:(t + 1) * 128]
                for f in range(2):
                    if layer == 0:
                        mm = pe.matmul(PS[:, bank + f, 0:HALF0], lhsT,
                                       KB0[0:KX_ROWS, a % 2, g, f * HALF0:(f + 1) * HALF0], start=True, stop=True)
                    else:
                        mm = pe.matmul(PS[:, bank + f, 0:2 * KC], lhsT,
                                       KB1[0:KX_ROWS, a % 2, g, f * 2 * KC:(f + 1) * 2 * KC], start=True, stop=True)
                mm.then_inc(*sig["mx_psum"].mark((a, kk)))

            def maxima_transposed(a):
                pe.wait_ge(*sig["mx_all"].at(a))
                for t in range(T):
                    mm = pe.transpose(PS[0:H, 4, t * 128:(t + 1) * 128], mneg[:, a % 2, t, :], ident[:, :])
                mm.then_inc(*sig["mt_psum"].mark(a))

            def router(j):
                kind = ITEMS[j][0]
                w, n = (RW1, E1) if kind == "F1" else (GW2, E2)
                pe.wait_ge(*sig["xt"].at(j))
                pe.wait_ge(*sig["w3_in"].at(0))
                if ITEMS[j][2] > 0:
                    pe.wait_ge(*sig["lg"].at(j - 1))
                else:
                    bank5_free_after_attention(j)
                for t in range(T):
                    mm = pe.matmul(PS[:, 5, t * n:(t + 1) * n], xT[:, j % 2, t * 128:(t + 1) * 128], w[:, :],
                                   start=True, stop=True)
                mm.then_inc(*sig["lg_psum"].mark(j))

            def bank5_free_after_attention(j):
                a_last = ITEMS[j - 1][1] * B + 3
                if a_last + 2 < 12:
                    pe.wait_ge(*sig["k"].at(a_last + 2))

            def lora(j):
                pe.wait_ge(*sig["lora_bd"].at(j))
                if ITEMS[j][2] > 0:
                    pe.wait_ge(*sig["lora_w"].at((j - 1, 1)))
                else:
                    bank5_free_after_attention(j)
                for n in range(2):
                    if n:
                        pe.wait_ge(*sig["lora_w"].at((j, 0)))
                    mm = pe.matmul(PS[:, 5, :], OD[:, n, :], EBD[:, n, :], start=True, stop=True)
                    if n == 0:
                        mm.then_inc(*sig["lora_psum"].mark((j, 0)))
                mm.then_inc(*sig["lora_psum"].mark(j))

            def piece(i, p):
                name = p[0]
                if name == "kproj":
                    k_proj(p[1])
                elif name == "kt":
                    k_transposes(p[1])
                elif name == "v":
                    v_blocks(p[1], p[2])
                elif name == "xt":
                    xt(p[1])
                elif name == "q":
                    q_proj(p[1])
                elif name == "qxt":
                    qxt(p[1], p[2])
                elif name == "max":
                    scores_for_max(i, p[1], p[2])
                elif name == "mt":
                    maxima_transposed(p[1])
                elif name == "late":
                    if ITEMS[p[1]][0] in ("F1", "F2"):
                        router(p[1])
                    elif ITEMS[p[1]][0] == "F0":
                        lora(p[1])

            def attention_step(i, n):
                _, layer, b = ITEMS[i]
                a = layer * B + b
                rows, chunks = chunk_shape(layer)
                N = 4 * chunks
                if n < N:
                    c, g = n // 4, n % 4
                    if n == 0:
                        pe.wait_ge(*sig["shift_in"].at(a))
                        for g2 in range(G):
                            pe.wait_ge(*sig["kb"].at((a, g2)))
                        if i > 0:
                            pe.wait_ge(*sig["resid"].at(i - 1))
                    if n >= 2:
                        pe.wait_ge(*sig["p"].at((i, n - 2)))
                    pe.matmul(PS[0:rows, n % 2, :], KB(layer)[0:K_ALL, a % 2, g, c * rows:(c + 1) * rows],
                              QXT[0:K_ALL, a % 2, g, :], start=True, stop=True).then_inc(*sig["st"].mark((i, n)))
                for name, lag, bank in (("pv", 2, 6), ("dn", 4, 7)):
                    m = n - lag
                    if 0 <= m < N:
                        c, g = m // 4, m % 4
                        pe.wait_ge(*sig["p"].at((i, m)))
                        if m == 0 and name == "pv":
                            pe.wait_ge(*sig["vb"].at((a, 0)))
                            pe.wait_ge(*sig["vb"].at((a, 1)))
                        mask = MV0 if layer == 0 else MV1
                        lhsT = VB[0:rows, a % 2, c, g * 32:(g + 1) * 32] if name == "pv" else mask[0:rows, c, 0:32]
                        pe.matmul(PS[32 * g:32 * g + 32, bank, :], lhsT, P[0:rows, m % 6, :],
                                  start=(c == 0), stop=(c == chunks - 1)).then_inc(*sig[name].mark((i, m)))

            def attention_end(i):
                _, layer, b = ITEMS[i]
                pe.wait_ge(*sig["on"].at(i))
                for t in range(T):
                    mm = pe.matmul(PS[:, 0, t * D:(t + 1) * D], ON[:, t * 128:(t + 1) * 128], WA[:, layer % 2, 3, :],
                                   start=True, stop=True)
                mm.then_inc(*sig["o_psum"].mark(i))

            def up(i, kt):
                kind, layer, b = ITEMS[i]
                e, col, rows, slot = ffn_tiles(kind)[kt]
                bank = 2 * (kt % 2)
                if kt == 0:
                    pe.wait_ge(*sig["resid"].at(i - 1))
                    pe.wait_ge(*sig["xl"].at(i))
                    if kind == "F0":
                        pe.wait_ge(*sig["lora_l"].at(i))
                    elif b == 0:
                        pe.wait_ge(*sig["w_l"].at(len(weight_chunks(1)) - 1 if layer == 1 else 8 + len(weight_chunks(2)) - 1))
                if kt >= 2:
                    pe.wait_ge(*sig["h_gelu" if kind == "F0" else "h"].at((i, kt - 2)))
                for m in range(1 if kind == "F0" else 2):
                    if kind == "F0":
                        w = [W1E[:, b % 2, hl, col:col + rows] for hl in range(2)]
                    else:
                        w = [UP(layer)[:, m, hl, col:col + rows] for hl in range(2)]
                    o = PS[0:rows, bank + m, :]
                    pe.matmul(o, w[0], xH[:, i % 2, :], start=True, stop=False)
                    pe.matmul(o, w[0], xL[:, i % 2, :], start=False, stop=False)
                    pe.matmul(o, w[1], xH[:, i % 2, :], start=False, stop=True).then_inc(*sig["up"].mark((i, kt, m)))

            def down(i, e):
                kind, layer, b = ITEMS[i]
                tiles = [(n, tl) for n, tl in enumerate(ffn_tiles(kind)) if tl[0] == e]
                pe.wait_ge(*sig["h_gelu" if kind == "F0" else "h"].at((i, tiles[-1][0])))
                if e == 0 and b == 0:
                    if kind != "F0":
                        pe.wait_ge(*sig["wd_in"].at(layer))
                if e >= 2:
                    pe.wait_ge(*sig["acc"].at((i, e - 2)))
                if e == 0 and kind == "F0":
                    pe.wait_ge(*sig["lora_w"].at((i, 1)))
                for t in range(T):
                    for j, (n, (_, _, rows, slot)) in enumerate(tiles):
                        rhs = W2E[:, b % 2, j * 128:(j + 1) * 128] if kind == "F0" else WD[0:rows, slot * 128:(slot + 1) * 128]
                        mm = pe.matmul(PS[:, 6 + e % 2, t * 128:(t + 1) * 128], HH[0:rows, e % 2, j, t * 128:(t + 1) * 128], rhs,
                                       start=(j == 0), stop=(j == len(tiles) - 1))
                mm.then_inc(*sig["y"].mark((i, e)))

            def ffn_step(i, n):
                kind = ITEMS[i][0]
                tiles = ffn_tiles(kind)
                if n < len(tiles):
                    up(i, n)
                for e in range(tiles[-1][0] + 1):
                    last = max(m for m, tl in enumerate(tiles) if tl[0] == e)
                    if n == last + 2:
                        down(i, e)

            def attention3(i):
                b = ITEMS[i][2]
                pe.wait_ge(*sig["resid"].at(i - 1))
                pe.wait_ge(*sig["xt"].at(i))
                pe.wait_ge(*sig["w3_in"].at(0))
                pe.wait_ge(*sig["w_proj3_in"].at(0))
                pe.matmul(PS[:, 0, :], W3[:, 0, :], xT[:, i % 2, :], start=True, stop=True).then_inc(*sig["a3_psum"].mark((i, 0)))
                pe.matmul(PS[:, 1, 0:KC], W3[:, 1, :], ctxT[:, b, :], start=True, stop=True).then_inc(*sig["a3_psum"].mark((i, 1)))
                for j in range(2):
                    mm = pe.matmul(PS[0:KJ, 2, j * D:(j + 1) * D], ctxT[:, b, j * KJ:(j + 1) * KJ], W3[:, 2, :], start=True, stop=True)
                mm.then_inc(*sig["a3_psum"].mark((i, 2)))
                pe.wait_ge(*sig["a3_qk"].at(i))
                for t in range(T):
                    mm = pe.matmul(PS[:, 6 + t // 2, (t % 2) * KC:(t % 2 + 1) * KC], QT3[:, t * 128:(t + 1) * 128], KT3, start=True, stop=True)
                mm.then_inc(*sig["a3_s"].mark(i))
                pe.wait_ge(*sig["a3_p"].at((i, T - 1)))
                for t in range(T):
                    for j in range(2):
                        mm = pe.transpose(PS[0:KJ, t // 2, (t % 2) * 256 + j * 128:(t % 2) * 256 + (j + 1) * 128],
                                          P3[:, t, j * KJ:(j + 1) * KJ], ident[:, :])
                mm.then_inc(*sig["a3_ptp"].mark(i))
                pe.wait_ge(*sig["a3_pt"].at(i))
                pe.wait_ge(*sig["a3_v"].at(i))
                for t in range(T):
                    for j in range(2):
                        lo = (t % 2) * 256 + j * 128
                        mm = pe.matmul(PS[:, 3, t * 128:(t + 1) * 128], PT3[:, t // 2, lo:lo + 128], V3[:, j, :],
                                       start=(j == 0), stop=(j == 1))
                mm.then_inc(*sig["a3_o"].mark(i))

            def ffn3(i):
                pe.wait_ge(*sig["resid"].at(i - 1))
                pe.wait_ge(*sig["xt"].at(i))
                pe.wait_ge(*sig["w_ffn3_in"].at(0))
                for t in range(T):
                    mm = pe.matmul(PS[:, t, 0:2 * D + E3], xT[:, i % 2, t * 128:(t + 1) * 128], WF3[:, 0:2 * D + E3], start=True, stop=True)
                mm.then_inc(*sig["f3_psum"].mark(i))

            pe.wait_ge(*sig["mem_ready"].at(0))
            pe.wait_ge(*sig["const_in"].at(0))
            for g in range(G):
                mm = pe.transpose(PS[0:KX_ROWS, 4, g * KM:(g + 1) * KM], MKX[:, g, 0:KX_ROWS], ident[0:KM, 0:KM])
            mm.then_inc(*sig["mem_kt_psum"].mark(0))
            pe.wait_ge(*sig["mem_kt"].at(0))
            k_proj(0)
            k_transposes(0)
            k_proj(1)
            k_transposes(1)
            v_blocks(0, 0)
            v_blocks(0, 1)
            pe.wait_ge(*sig["vb"].at((0, 0)))
            xt(0)
            q_proj(0)
            for g in range(G):
                qxt(0, g)
            for kk in range(G * T):
                scores_for_max(0, 0, kk)
            maxima_transposed(0)
            xt(1)
            for i in range(len(ITEMS)):
                kind = ITEMS[i][0]
                total, pieces = all_slots(i)
                for n in range(total):
                    if kind == "A":
                        attention_step(i, n)
                    elif kind in ("F0", "F1", "F2"):
                        ffn_step(i, n)
                    elif n == 0:
                        attention3(i) if kind == "A3" else ffn3(i)
                    for p in pieces.get(n, []):
                        piece(i, p)
                    if kind == "A" and n == n_slots(i) + 5 - 1 and total > n_slots(i) + 5 - 1:
                        attention_end(i)
                if kind == "A" and total <= n_slots(i) + 4:
                    attention_end(i)

        @block.vector
        def _(dve):
            def ln_stats(j):
                b = ITEMS[j][2]
                if j < B:
                    dve.wait_ge(*sig[f"x_in{b}"].at(0))
                else:
                    dve.wait_ge(*sig["resid"].at(j - B))
                if j >= 2:
                    dve.wait_ge(*sig["xn"].at(j - 2))
                for t in range(T):
                    dve.bn_stats(st6[:, j % 2, t, :], x[:, b * T + t, :]).then_inc(*sig["ln_stats"].mark((j, t)))
                for t in range(T):
                    dve.wait_ge(*sig["ln_stats"].at((j, t)))
                    dve.bn_aggr(mvar[:, j % 2, t, :], st6[:, j % 2, t, :]).then_inc(*sig["ln_aggr"].mark((j, t)))

            def k_bias(a):
                layer = a // B
                dve.wait_ge(*sig["k_psum"].at(a))
                if a >= 1:
                    dve.wait_ge(*sig["kx_l"].at(a - 1))
                    dve.wait_ge(*sig["kx_h"].at(a - 1))
                dve.tensor_tensor(k[:, :].rearrange("p (j n) -> p j n", j=2), PS[0:KJ, 5, 0:2 * D].rearrange("p (j n) -> p j n", j=2),
                                  BK[:, layer % 2, None, :].to_broadcast([KJ, 2, D]), ALU.add).then_inc(*sig["k"].mark(a))

            def k_mean_square(a):
                if a // B == 1:
                    dve.wait_ge(*sig["k_sq"].at(a))
                    dve.tensor_reduce(kms[:, :], ka[:, :].rearrange("p (h d) -> p h d", d=HD), AX.X, ALU.add).then_inc(*sig["k_ms"].mark(a))

            def v_mask(a, part):
                layer = a // B
                rows, chunks = chunk_shape(layer)
                mask = MV0 if layer == 0 else MV1
                c0, c1 = 4 * part, min(4 * part + 4, chunks)
                dve.wait_ge(*sig["v_psum"].at((a, part)))
                if a >= 2 and part == 0:
                    dve.wait_ge(*sig["pv"].at((item_of(a - 2), 4 * chunk_shape((a - 2) // B)[1] - 1)))
                if a == B and part == 0:
                    dve.wait_ge(*sig["wA_in1"].at(0))
                dve.tensor_tensor(VB[0:rows, a % 2, c0:c1, :].rearrange("p c (g n) -> p c g n", g=G),
                                  PS[0:rows, 4 + part, 0:(c1 - c0) * D].rearrange("p (c g n) -> p c g n", g=G, n=HL * HD),
                                  mask[0:rows, c0:c1, None, :].to_broadcast([rows, c1 - c0, G, HL * HD]), ALU.mult).then_inc(*sig["vb"].mark((a, part)))

            def q_bias(a):
                layer = a // B
                dve.wait_ge(*sig["q_psum"].at(a))
                if a >= 1:
                    dve.wait_ge(*sig["qx_l"].at(a - 1))
                    dve.wait_ge(*sig["qx_h"].at(a - 1))
                dve.tensor_tensor(q[:, :].rearrange("p (t n) -> p t n", t=T), PS[:, 4, :].rearrange("p (t n) -> p t n", t=T),
                                  BQ[:, layer % 2, None, :].to_broadcast([128, T, D]), ALU.add).then_inc(*sig["q"].mark(a))

            def q_chain(a):
                layer = a // B
                if layer == 1:
                    dve.wait_ge(*sig["q_sq"].at(a))
                    dve.tensor_reduce(qms[:, :], qa[:, :].rearrange("p (h d) -> p h d", d=HD), AX.X, ALU.add).then_inc(*sig["q_ms"].mark(a))
                    dve.wait_ge(*sig["q_rr"].at(a))
                    dve.wait_ge(*sig["q"].at(a))
                    dve.tensor_tensor(qb[:, :].rearrange("p (h d) -> p h d", d=HD), q[:, :].rearrange("p (h d) -> p h d", d=HD),
                                      qrr[:, :, None].to_broadcast([128, T * H, HD]), ALU.mult).then_inc(*sig["q_ready"].mark(a))
                if layer == 2:
                    qv = q[:, :].rearrange("p (t h i s) -> p t h i s", t=T, h=H, s=2)
                    bv = qb[:, :].rearrange("p (t h i s) -> p t h i s", t=T, h=H, s=2)
                    dve.wait_ge(*sig["q"].at(a))
                    for s, (lo, hi) in enumerate(((8, 12), (12, 16))):
                        dve.tensor_tensor(bv[:, :, :, :, s], qv[:, :, :, :, 1 - s],
                                          ropeq[:, :, None, lo:hi].to_broadcast([128, T, H, 4]), ALU.mult).then_inc(*sig["q_t2"].mark((a, s)))
                    dve.wait_ge(*sig["q_t1"].at(a))
                    dve.wait_ge(*sig["q_t2"].at((a, 1)))
                    dve.tensor_tensor(q[:, :], qa[:, :], qb[:, :], ALU.add).then_inc(*sig["q_ready"].mark(a))

            def q_of(a):
                return qb if a // B == 1 else q

            def q_split(a):
                dve.wait_ge(*sig["qx_h"].at(a))
                qx = QX[:, :, :, 0:PR].rearrange("p t g (h s d) -> p (t g) h s d", h=HL, s=3)
                dve.tensor_tensor(qx[:, :, :, 1, :], q_of(a)[:, :].rearrange("p (m h d) -> p m h d", h=HL, d=HD),
                                  qx[:, :, :, 0, :], ALU.subtract).then_inc(*sig["qx_l"].mark(a))

            def maxima(i_main, a, kk):
                g, t, layer = kk // T, kk % T, a // B
                bank, _ = mx_banks(i_main, kk)
                dve.wait_ge(*sig["mx_psum"].at((a, kk)))
                if kk == 0 and a >= 2:
                    dve.wait_ge(*sig["mt_psum"].at(a - 2))
                if kk == 0 and layer == 0 and a >= 1:
                    dve.wait_ge(*sig["mx_all"].at(a - 1))
                out_ = mneg[:, a % 2, t, g * HL:(g + 1) * HL].rearrange("p (f h) -> p f h", f=2)
                red = dve.tensor_reduce(out_, PS[:, bank:bank + 2, 0:2 * KC].rearrange("p f (h n) -> p f h n", h=2), AX.X, ALU.max, negate=True)
                if layer == 0:
                    red.then_inc(*sig["mx_mem"].mark((a, kk)))
                    red = dve.tensor_reduce(mneg2[:, t, g * HL:(g + 1) * HL].rearrange("p (f h) -> p f h", f=2),
                                            PS[:, bank:bank + 2, 2 * KC:HALF0].rearrange("p f (h n) -> p f h n", h=2), AX.X, ALU.max, negate=True)
                red.then_inc(*sig["mx"].mark((a, kk)))
                if kk == G * T - 1:
                    dve.wait_ge(*sig["mx"].at((a, kk)))
                    if layer == 0:
                        dve.tensor_tensor(mneg[:, a % 2, :, :], mneg[:, a % 2, :, :], mneg2[:, :, :], ALU.min).then_inc(*sig["mx_all"].mark(a))
                    else:
                        dve.engine_nop().then_inc(*sig["mx_all"].mark(a))

            def x_low(j):
                if ITEMS[j][0] in ("F0", "F1", "F2"):
                    dve.wait_ge(*sig["xh"].at(j))
                    if ITEMS[j][2] >= 2:
                        dve.wait_ge(*sig["y"].at((j - 2, ffn_tiles(ITEMS[j][0])[-1][0])))
                    dve.tensor_tensor(xL[:, j % 2, :], xT[:, j % 2, :], xH[:, j % 2, :], ALU.subtract).then_inc(*sig["xl"].mark(j))

            def gating(key, n, psum_view, bias):
                g8 = gates[:, key[1] % 2, :, 0:n]
                if bias is not None:
                    dve.tensor_tensor(lg[:, :, 0:n], psum_view, bias[:, None, :].to_broadcast([128, T, n]), ALU.add).then_inc(*sig["lg"].mark(key[1]))
                else:
                    dve.tensor_copy(lg[:, :, 0:n], psum_view).then_inc(*sig["lg"].mark(key[1]))
                i = key[1]
                dve.wait_ge(*sig["lg"].at(i))
                l = lg[:, :, 0:n]
                dve.tensor_reduce(lsm[:, 0, :], l, AX.X, ALU.max, negate=True).then_inc(*sig["lg_nm"].mark(i))
                lj = lg[:, :, None, 0:n].to_broadcast([128, T, n, n])
                li = lg[:, :, 0:n, None].to_broadcast([128, T, n, n])
                dve.tensor_tensor(lga[:, :, 0:n, 0:n], lj, li, ALU.is_gt).then_inc(*sig["lg_c"].mark((i, 0)))
                dve.tensor_tensor(lgb[:, :, 0:n, 0:n], lj, li, ALU.is_equal).then_inc(*sig["lg_c"].mark((i, 1)))
                dve.wait_ge(*sig["lg_nm"].at(i))
                dve.tensor_tensor(lsh[:, :, 0:n], l, lsm[:, 0, :, None].to_broadcast([128, T, n]), ALU.add).then_inc(*sig["lg_sh"].mark(i))
                dve.wait_ge(*sig["lg_c"].at((i, 1)))
                dve.tensor_tensor(lgb[:, :, 0:n, 0:n], lgb[:, :, 0:n, 0:n], LT[:, None, 0:n, 0:n].to_broadcast([128, T, n, n]), ALU.mult).then_inc(*sig["lg_c"].mark((i, 2)))
                dve.wait_ge(*sig["lg_c"].at((i, 2)))
                dve.tensor_tensor(lga[:, :, 0:n, 0:n], lga[:, :, 0:n, 0:n], lgb[:, :, 0:n, 0:n], ALU.add).then_inc(*sig["lg_c"].mark((i, 3)))
                dve.wait_ge(*sig["lg_c"].at((i, 3)))
                dve.tensor_reduce(lsh2(n), lga[:, :, 0:n, 0:n], AX.X, ALU.add).then_inc(*sig["lg_c"].mark((i, 4)))
                dve.wait_ge(*sig["lg_c"].at((i, 4)))
                dve.wait_ge(*sig["lg_e"].at(i))
                dve.scalar_tensor_tensor(lsh2(n), lsh2(n), 2.0, le[:, :, 0:n], ALU.is_lt, ALU.mult).then_inc(*sig["lg_es"].mark(i))
                dve.wait_ge(*sig["lg_es"].at(i))
                dve.tensor_reduce(lsm[:, 1, :], lsh2(n), AX.X, ALU.add).then_inc(*sig["lg_sum"].mark(i))
                dve.wait_ge(*sig["lg_sum"].at(i))
                dve.reciprocal(lsm[:, 2, :], lsm[:, 1, :]).then_inc(*sig["lg_r"].mark(i))
                dve.wait_ge(*sig["lg_r"].at(i))
                dve.tensor_tensor(g8, lsh2(n), lsm[:, 2, :, None].to_broadcast([128, T, n]), ALU.mult).then_inc(*sig["gates"].mark(i))

            def lsh2(n):
                return lgb[:, :, 0, 0:n]

            def router(j):
                kind, _, b = ITEMS[j]
                n = E1 if kind == "F1" else E2
                dve.wait_ge(*sig["lg_psum"].at(j))
                if b == 0:
                    dve.wait_ge(*sig["w3_in"].at(0))
                if b >= 1:
                    dve.wait_ge(*sig["gates"].at(j - 1))
                if b >= 2:
                    dve.wait_ge(*sig["acc"].at((j - 2, ffn_tiles(kind)[-1][0])))
                gating(("r", j), n, PS[:, 5, 0:T * n].rearrange("p (t n) -> p t n", t=T), RB1 if kind == "F1" else None)

            def lora(j):
                b = ITEMS[j][2]
                if b == 0:
                    dve.wait_ge(*sig["w_ffn0_in"].at(0))
                dve.wait_ge(*sig["lora_psum"].at((j, 0)))
                if b >= 2:
                    dve.wait_ge(*sig["y"].at((j - 2, 0)))
                if b >= 1:
                    dve.wait_ge(*sig["lora_l"].at(j - 1))
                dve.scalar_tensor_tensor(qa[:, :], PS[:, 5, :], scale0[:, :], W1T, ALU.mult, ALU.add).then_inc(*sig["lora_w"].mark((j, 0)))
                dve.wait_ge(*sig["lora_psum"].at(j))
                dve.scalar_tensor_tensor(W2E[:, b % 2, :], PS[:, 5, :], scale0[:, :], W2T, ALU.mult, ALU.add).then_inc(*sig["lora_w"].mark((j, 1)))
                dve.wait_ge(*sig["lora_h"].at(j))
                dve.tensor_tensor(W1E[:, b % 2, 1, :], qa[:, :], W1E[:, b % 2, 0, :], ALU.subtract).then_inc(*sig["lora_l"].mark(j))

            def piece(i, p):
                name = p[0]
                if name == "ln":
                    ln_stats(p[1])
                elif name == "kproj":
                    k_bias(p[1])
                elif name == "kchain":
                    k_mean_square(p[1])
                elif name == "v":
                    v_mask(p[1], p[2])
                elif name == "q":
                    q_bias(p[1])
                elif name == "qchain":
                    q_chain(p[1])
                elif name == "qsplit":
                    q_split(p[1])
                elif name == "max":
                    maxima(i, p[1], p[2])
                elif name == "after_xt":
                    x_low(p[1])
                elif name == "late":
                    if ITEMS[p[1]][0] in ("F1", "F2"):
                        router(p[1])
                    elif ITEMS[p[1]][0] == "F0":
                        lora(p[1])

            def attention_end(i):
                _, layer, b = ITEMS[i]
                N = n_slots(i)
                dve.wait_ge(*sig["dn"].at((i, N - 1)))
                if i > 0:
                    dve.wait_ge(*sig["resid"].at(i - 1))
                dve.reciprocal(RD, PS[:, 7, :]).then_inc(*sig["rden"].mark(i))
                dve.wait_ge(*sig["rden"].at(i))
                dve.tensor_tensor(ON, PS[:, 6, :], RD, ALU.mult).then_inc(*sig["on"].mark(i))
                dve.wait_ge(*sig["o_psum"].at(i))
                dve.wait_ge(*sig["bias_in_x"].at(i))
                xb = x[:, b * T:(b + 1) * T, :]
                dve.tensor_tensor(xb, PS[:, 0, :].rearrange("p (t n) -> p t n", t=T), xb, ALU.add).then_inc(*sig["resid"].mark(i))

            def ffn_step(i, n):
                kind, layer, b = ITEMS[i]
                tiles = ffn_tiles(kind)
                if n < len(tiles) and kind != "F0":
                    e, col, rows, slot = tiles[n]
                    j = n - min(m for m, tl in enumerate(tiles) if tl[0] == e)
                    dve.wait_ge(*sig["act"].at((i, n)))
                    dve.wait_ge(*sig["up"].at((i, n, 1)))
                    if e >= 2:
                        dve.wait_ge(*sig["y"].at((i, e - 2)))
                    elif b > 0:
                        dve.wait_ge(*sig["resid"].at(i - 1))
                    dve.tensor_tensor(HH[0:rows, e % 2, j, :], PS[0:rows, 2 * (n % 2) + 1, :], SS[0:rows, n % 2, :], ALU.mult).then_inc(*sig["h"].mark((i, n)))
                for e in range(tiles[-1][0] + 1):
                    last = max(m for m, tl in enumerate(tiles) if tl[0] == e)
                    if n == last + 3:
                        accumulate(i, e)

            def accumulate(i, e):
                kind, layer, b = ITEMS[i]
                last_e = ffn_tiles(kind)[-1][0]
                dve.wait_ge(*sig["y"].at((i, e)))
                if e == 0:
                    dve.wait_ge(*sig["xn"].at(i))
                    if kind == "F0":
                        dve.wait_ge(*sig["bias_in_x"].at(i))
                    else:
                        dve.wait_ge(*sig["gates"].at(i))
                else:
                    dve.wait_ge(*sig["acc"].at((i, e - 1)))
                if kind == "F0" or e == E2:
                    xb = x[:, b * T:(b + 1) * T, :]
                    ins = dve.tensor_tensor(xb, PS[:, 6 + e % 2, :].rearrange("p (t n) -> p t n", t=T), xb, ALU.add)
                else:
                    for t in range(T):
                        xt_ = x[:, b * T + t, :]
                        ins = dve.scalar_tensor_tensor(xt_, PS[:, 6 + e % 2, t * 128:(t + 1) * 128], gates[:, i % 2, t, e:e + 1], xt_, ALU.mult, ALU.add)
                ins.then_inc(*sig["acc"].mark((i, e)))
                if e == last_e:
                    dve.wait_ge(*sig["acc"].at((i, e)))
                    dve.engine_nop().then_inc(*sig["resid"].mark(i))

            def attention3(i):
                b = ITEMS[i][2]
                dve.wait_ge(*sig["a3_psum"].at((i, 2)))
                dve.wait_ge(*sig["w_proj3_in"].at(0))
                if i > 0:
                    dve.wait_ge(*sig["resid"].at(i - 1))
                dve.tensor_tensor(V3, PS[0:KJ, 2, 0:2 * D].rearrange("p (j n) -> p j n", j=2), BV3[:, None, :].to_broadcast([KJ, 2, D]), ALU.add).then_inc(*sig["a3_v"].mark(i))
                dve.wait_ge(*sig["a3_s"].at(i))
                dve.tensor_reduce(lsm[:, 0, :].rearrange("p (f h) -> p f h", f=2), PS[:, 6:8, 0:2 * KC].rearrange("p f (h n) -> p f h n", h=2), AX.X, ALU.max, negate=True).then_inc(*sig["a3_nm"].mark(i))
                dve.wait_ge(*sig["a3_nm"].at(i))
                dve.tensor_scalar(lsm[:, 1, :], lsm[:, 0, :], SCALE3, None, ALU.mult).then_inc(*sig["a3_nms"].mark(i))
                dve.wait_ge(*sig["a3_p"].at((i, T - 1)))
                dve.reciprocal(lsm[:, 3, :], lsm[:, 2, :]).then_inc(*sig["a3_r"].mark(i))
                dve.wait_ge(*sig["a3_r"].at(i))
                dve.wait_ge(*sig["a3_o"].at(i))
                dve.wait_ge(*sig["xn"].at(i))
                for t in range(T):
                    xt_ = x[:, b * T + t, :]
                    ins = dve.scalar_tensor_tensor(xt_, PS[:, 3, t * 128:(t + 1) * 128], lsm[:, 3, t:t + 1], xt_, ALU.mult, ALU.add)
                ins.then_inc(*sig["resid"].mark(i))

            def ffn3(i):
                b = ITEMS[i][2]
                dve.wait_ge(*sig["f3_psum"].at(i))
                dve.wait_ge(*sig["resid"].at(i - 1))
                gating(("f3", i), E3, PS[:, 0:T, 2 * D:2 * D + E3], None)
                dve.wait_ge(*sig["gates"].at(i))
                dve.tensor_reduce(lsm[:, 3, :], gates[:, i % 2, :, 0:E3], AX.X, ALU.add).then_inc(*sig["f3_y"].mark((i, 0)))
                dve.wait_ge(*sig["f3_y"].at((i, 0)))
                dve.wait_ge(*sig["bias_in_x"].at(i))
                for t in range(T):
                    xt_ = x[:, b * T + t, :]
                    ins = dve.scalar_tensor_tensor(xt_, PS[:, t, 0:D], lsm[:, 3, t:t + 1], xt_, ALU.mult, ALU.add)
                ins.then_inc(*sig["f3_y"].mark((i, 1)))
                dve.wait_ge(*sig["f3_y"].at((i, 1)))
                xb = x[:, b * T:(b + 1) * T, :]
                dve.tensor_tensor(xb, PS[:, 0:T, D:2 * D], xb, ALU.add).then_inc(*sig["f3_y"].mark(i))
                dve.wait_ge(*sig["f3_y"].at(i))
                dve.engine_nop().then_inc(*sig["resid"].mark(i))

            dve.wait_ge(*sig["mask_in"].at(0))
            dve.memset(KEEP[:, :, :, :], 1.0).then_inc(*sig["init_dve"].mark(0))
            dve.memset(KBIAS[:, :, :, :], 0.0).then_inc(*sig["init_dve"].mark(1))
            dve.wait_ge(*sig["init_dve"].at(1))
            dve.tensor_copy(KEEP[:, 0, :, :], mraw0[:, :, :]).then_inc(*sig["init_dve"].mark(2))
            dve.tensor_copy(KEEP[:, 2, :, :], mraw2[:, :, :]).then_inc(*sig["init_dve"].mark(3))
            dve.wait_ge(*sig["init_dve"].at(3))
            dve.tensor_scalar(KEEP[:, :, :, :], KEEP[:, :, :, :], 0.0, None, ALU.not_equal).then_inc(*sig["init_dve"].mark(4))
            dve.wait_ge(*sig["init_dve"].at(4))
            dve.tensor_scalar(KBIAS[:, :, :, :], KEEP[:, :, :, :], BIG, -BIG, ALU.mult, ALU.add).then_inc(*sig["mask_ready"].mark(0))
            ln_stats(0)
            ln_stats(1)
            k_bias(0)
            k_mean_square(0)
            k_bias(1)
            v_mask(0, 0)
            v_mask(0, 1)
            q_bias(0)
            q_chain(0)
            q_split(0)
            for kk in range(G * T):
                maxima(0, 0, kk)
            for i in range(len(ITEMS)):
                kind = ITEMS[i][0]
                total, pieces = all_slots(i)
                if first_of_kind(i):
                    dve.wait_ge(*sig["resid"].at(i - 1))
                for n in range(total):
                    if kind in ("F0", "F1", "F2"):
                        ffn_step(i, n)
                    elif kind in ("A3", "F3") and n == 0:
                        attention3(i) if kind == "A3" else ffn3(i)
                    for p in pieces.get(n, []):
                        piece(i, p)
                    if kind == "A" and n == n_slots(i) + 3:
                        attention_end(i)

        @block.scalar
        def _(act):
            def k_split(a):
                layer = a // B
                act.wait_ge(*sig["k_ready"].at(a))
                if a >= 1:
                    act.wait_ge(*sig["kt_psum"].at(a - 1))
                kx = KX[:, :, :, 0:PR].rearrange("p j g (h s d) -> p (j g) h s d", h=HL, s=3).bitcast(F32R)
                src = k[:, :].rearrange("p (m h d) -> p m h d", h=HL, d=HD)
                for s in range(2):
                    act.activation(kx[:, :, :, s, :], src, ACT.Copy).then_inc(*sig["kx_h"].more(a))

            def kt_out(a):
                act.wait_ge(*sig["kt_psum"].at(a))
                if a < 2:
                    act.wait_ge(*sig["init_pool"].at(0))
                else:
                    act.wait_ge(*sig["kb"].at((a - 2, G - 1)))
                act.activation(KT[0:KX_ROWS, a % 2, :, :].rearrange("p (f g) n -> p f (g n)", f=2), PS[0:KX_ROWS, 4:6, 0:2 * KC], ACT.Copy).then_inc(*sig["kt"].mark(a))

            def xt_out(j):
                act.wait_ge(*sig["xt_psum"].at(j))
                if j >= 2:
                    kind = ITEMS[j - 2][0]
                    if kind == "A":
                        act.wait_ge(*sig["q_psum"].at(ITEMS[j - 2][1] * B + ITEMS[j - 2][2]))
                    elif kind in ("F1", "F2"):
                        act.wait_ge(*sig["lg_psum"].at(j - 2))
                    if kind in ("F0", "F1", "F2"):
                        act.wait_ge(*sig["xl"].at(j - 2))
                    if kind == "A3":
                        act.wait_ge(*sig["a3_psum"].at((j - 2, 0)))
                    if kind == "F3":
                        act.wait_ge(*sig["f3_psum"].at(j - 2))
                act.activation(xT[:, j % 2, :], PS[:, 4, :], ACT.Copy).then_inc(*sig["xt"].mark(j))

            def x_high(j):
                if ITEMS[j][0] in ("F0", "F1", "F2"):
                    act.wait_ge(*sig["xt"].at(j))
                    if ITEMS[j][2] >= 2:
                        act.wait_ge(*sig["y"].at((j - 2, ffn_tiles(ITEMS[j][0])[-1][0])))
                    act.activation(xH[:, j % 2, :], xT[:, j % 2, :], ACT.Copy).then_inc(*sig["xh"].mark(j))

            def q_split(a):
                layer = a // B
                if layer == 0:
                    act.wait_ge(*sig["q"].at(a))
                else:
                    act.wait_ge(*sig["q_ready"].at(a))
                if a >= 1:
                    act.wait_ge(*sig["qxt_psum"].at((a - 1, G - 1)))
                else:
                    act.wait_ge(*sig["init_pool"].at(0))
                src = (qb if layer == 1 else q)[:, :].rearrange("p (m h d) -> p m h d", h=HL, d=HD)
                qx = QX[:, :, :, 0:PR].rearrange("p t g (h s d) -> p (t g) h s d", h=HL, s=3).bitcast(F32R)
                for s in (0, 2):
                    act.activation(qx[:, :, :, s, :], src, ACT.Copy).then_inc(*sig["qx_h"].more(a))

            def qxt_out(a, g):
                act.wait_ge(*sig["qxt_psum"].at((a, g)))
                if a >= 2 and g == 0:
                    act.wait_ge(*sig["st"].at((item_of(a - 2), n_slots(item_of(a - 2)) - 1)))
                act.activation(QXT[0:KX_ROWS, a % 2, g, :], PS[0:KX_ROWS, 5 - g % 2, :], ACT.Copy).then_inc(*sig["qxt"].mark((a, g)))

            def mt_out(a):
                act.wait_ge(*sig["mt_psum"].at(a))
                if a >= 1:
                    act.wait_ge(*sig["shift_in"].at(a - 1))
                act.activation(mT[:, :], PS[0:H, 4, :], ACT.Copy).then_inc(*sig["mt"].mark(a))

            def w_high(layer, c):
                which, lo, w = weight_chunks(layer)[c]
                serial = c + (8 if layer == 2 else 0)
                act.wait_ge(*sig[f"stage_in{serial % 2}"].at(serial))
                act.activation(UP(layer)[:, which, 0, lo:lo + w], stage[:, serial % 2, 0:w], ACT.Copy).then_inc(*sig["w_h"].mark(serial))

            def gate_exp(i, n):
                act.wait_ge(*sig["lg_sh"].at(i))
                act.activation(le[:, :, 0:n], lsh[:, :, 0:n], ACT.Exp).then_inc(*sig["lg_e"].mark(i))

            def piece(i, p):
                name = p[0]
                if name == "kchain":
                    k_split(p[1])
                elif name == "kt":
                    kt_out(p[1])
                elif name == "xt":
                    xt_out(p[1])
                elif name == "after_xt":
                    x_high(p[1])
                elif name == "qsplit":
                    q_split(p[1])
                elif name == "qxt":
                    qxt_out(p[1], p[2])
                elif name == "mt":
                    mt_out(p[1])
                elif name == "w":
                    w_high(p[1], p[2])
                elif name == "late":
                    kind = ITEMS[p[1]][0]
                    if kind in ("F1", "F2"):
                        gate_exp(p[1], E1 if kind == "F1" else E2)
                    elif kind == "F0":
                        j = p[1]
                        act.wait_ge(*sig["lora_w"].at((j, 0)))
                        if ITEMS[j][2] >= 2:
                            act.wait_ge(*sig["y"].at((j - 2, 0)))
                        act.activation(W1E[:, ITEMS[j][2] % 2, 0, :], qa[:, :], ACT.Copy).then_inc(*sig["lora_h"].mark(j))

            def exps(i, n):
                _, layer, b = ITEMS[i]
                rows, _ = chunk_shape(layer)
                act.wait_ge(*sig["st"].at((i, n)))
                if n >= 6:
                    act.wait_ge(*sig["dn"].at((i, n - 6)))
                elif i > 0 and b > 0:
                    act.wait_ge(*sig["dn"].at((i - 1, n_slots(i - 1) - 1)))
                act.activation(P[0:rows, n % 6, :], PS[0:rows, n % 2, :], ACT.Exp, scale=SCALE).then_inc(*sig["p"].mark((i, n)))

            def ffn_step(i, n):
                kind, layer, b = ITEMS[i]
                e, col, rows, slot = ffn_tiles(kind)[n]
                bank = 2 * (n % 2)
                act.wait_ge(*sig["up"].at((i, n, 0)))
                if kind == "F0":
                    if n == 0:
                        act.wait_ge(*sig["resid"].at(i - 1))
                        act.wait_ge(*sig["w_ffn0_in"].at(0))
                    act.activation(HH[0:rows, 0, n, :], PS[0:rows, bank, :], ACT.Gelu, bias=b1T[:, n:n + 1]).then_inc(*sig["h_gelu"].mark((i, n)))
                else:
                    if n >= 2:
                        act.wait_ge(*sig["h"].at((i, n - 2)))
                    elif b > 0:
                        act.wait_ge(*sig["resid"].at(i - 1))
                    act.activation(SS[0:rows, n % 2, :], PS[0:rows, bank, :], ACT.Silu).then_inc(*sig["act"].mark((i, n)))

            def attention3(i):
                act.wait_ge(*sig["a3_psum"].at((i, 0)))
                act.wait_ge(*sig["resid"].at(i - 1))
                act.wait_ge(*sig["w3_in"].at(0))
                act.activation(QT3, PS[:, 0, :], ACT.Identity, bias=bqk3[:, 0:1]).then_inc(*sig["a3_qk"].more(i))
                act.wait_ge(*sig["a3_psum"].at((i, 1)))
                act.activation(KT3, PS[:, 1, 0:KC], ACT.Identity, bias=bqk3[:, 1:2]).then_inc(*sig["a3_qk"].more(i))
                act.wait_ge(*sig["a3_nms"].at(i))
                for t in range(T):
                    act.activation(P3[:, t, :], PS[:, 6 + t // 2, (t % 2) * KC:(t % 2 + 1) * KC], ACT.Exp, bias=lsm[:, 1, t:t + 1],
                                   scale=SCALE3, accum_out=lsm[:, 2, t:t + 1]).then_inc(*sig["a3_p"].mark((i, t)))
                act.wait_ge(*sig["a3_ptp"].at(i))
                act.activation(PT3, PS[0:KJ, 0:2, :], ACT.Copy).then_inc(*sig["a3_pt"].mark(i))

            act.wait_ge(*sig["mem_kt_psum"].at(0))
            act.wait_ge(*sig["init_pool"].at(0))
            act.activation(KTM[0:KX_ROWS, :, :], PS[0:KX_ROWS, 4, 0:G * KM].rearrange("p (g n) -> p g n", g=G), ACT.Copy).then_inc(*sig["mem_kt"].mark(0))
            k_split(0)
            kt_out(0)
            k_split(1)
            kt_out(1)
            xt_out(0)
            q_split(0)
            for g in range(G):
                qxt_out(0, g)
            mt_out(0)
            xt_out(1)
            for i in range(len(ITEMS)):
                kind = ITEMS[i][0]
                total, pieces = all_slots(i)
                if first_of_kind(i):
                    act.wait_ge(*sig["resid"].at(i - 1))
                for n in range(total):
                    if kind == "A" and n < n_slots(i):
                        exps(i, n)
                    elif kind in ("F0", "F1", "F2") and n < n_slots(i):
                        ffn_step(i, n)
                    elif kind == "A3" and n == 0:
                        attention3(i)
                    elif kind == "F3" and n == 0:
                        gate_exp(i, E3)
                    for p in pieces.get(n, []):
                        piece(i, p)

        @block.gpsimd
        def _(pool):
            def layer_norm(j):
                b = ITEMS[j][2]
                pool.wait_ge(*sig["ln_aggr"].at((j, T - 1)))
                if j >= 2:
                    pool.wait_ge(*sig["xt_psum"].at(j - 2))
                    if ITEMS[j - 2][0] == "F0":
                        pool.wait_ge(*sig["lora_in"].at(j - 2))
                pool.tensor_scalar(rstd[:, j % 2, :], mvar[:, j % 2, :, 1], LN_EPS, None, ALU.add).then_inc(*sig["ln_var"].mark(j))
                pool.wait_ge(*sig["ln_var"].at(j))
                pool.tensor_tensor(rstd[:, j % 2, :], rstd[:, j % 2, :], half[:, 0:T], ALU.pow).then_inc(*sig["ln_rstd"].mark(j))
                pool.wait_ge(*sig["ln_rstd"].at(j))
                for t in range(T):
                    ins = pool.tensor_scalar(xn[:, j % 2, t, :], x[:, b * T + t, :], mvar[:, j % 2, t, 0:1], rstd[:, j % 2, t:t + 1], ALU.subtract, ALU.mult)
                ins.then_inc(*sig["xn"].mark(j))
                slot = bias_slot(j)
                if slot is not None:
                    if slot < 3:
                        pool.wait_ge(*sig[f"wA_in{slot}"].at(0))
                    else:
                        pool.wait_ge(*sig["w_ffn0_in" if slot == 3 else "w3_in"].at(0))
                    pool.wait_ge(*sig["xn"].at(j))
                    xb = x[:, b * T:(b + 1) * T, :]
                    pool.tensor_tensor(xb, xb, BO[:, slot, None, :].to_broadcast([128, T, D]), ALU.add).then_inc(*sig["bias_in_x"].mark(j))

            def k_chain(a):
                layer, b = a // B, a % B
                pool.wait_ge(*sig["k"].at(a))
                if layer == 1:
                    pool.tensor_tensor(ka[:, :], k[:, :], k[:, :], ALU.mult).then_inc(*sig["k_sq"].mark(a))
                    pool.wait_ge(*sig["k_ms"].at(a))
                    pool.tensor_scalar(krr[:, :], kms[:, :], 1.0 / HD, RMS_EPS, ALU.mult, ALU.add).then_inc(*sig["k_var"].mark(a))
                    pool.wait_ge(*sig["k_var"].at(a))
                    pool.tensor_tensor(krr[:, :], krr[:, :], half[0:KJ, 0:2 * H], ALU.pow).then_inc(*sig["k_rr"].mark(a))
                    pool.wait_ge(*sig["k_rr"].at(a))
                    kv = k[:, :].rearrange("p (h d) -> p h d", d=HD)
                    pool.tensor_tensor(kv, kv, krr[:, :, None].to_broadcast([KJ, 2 * H, HD]), ALU.mult).then_inc(*sig["k_n"].mark(a))
                    pool.wait_ge(*sig["k_n"].at(a))
                    pool.wait_ge(*sig["gkq_ready"].at(0))
                    pool.tensor_tensor(kv, kv, gq[:, 0, None, :].to_broadcast([KJ, 2 * H, HD]), ALU.mult).then_inc(*sig["k_ready"].mark(a))
                if layer == 2:
                    kv = k[:, :].rearrange("p (j h d) -> p j h d", j=2, d=HD)
                    kp = k[:, :].rearrange("p (j h i s) -> p j h i s", j=2, h=H, s=2)
                    bp = kb[:, :].rearrange("p (j h i s) -> p j h i s", j=2, h=H, s=2)
                    pool.tensor_tensor(ka[:, :].rearrange("p (j h d) -> p j h d", j=2, d=HD), kv,
                                       ropek[:, :, None, 0:8].to_broadcast([KJ, 2, H, HD]), ALU.mult).then_inc(*sig["k_t1"].mark(a))
                    for s, (lo, hi) in enumerate(((8, 12), (12, 16))):
                        pool.tensor_tensor(bp[:, :, :, :, s], kp[:, :, :, :, 1 - s],
                                           ropek[:, :, None, lo:hi].to_broadcast([KJ, 2, H, 4]), ALU.mult).then_inc(*sig["k_t2"].mark((a, s)))
                    pool.wait_ge(*sig["k_t1"].at(a))
                    pool.wait_ge(*sig["k_t2"].at((a, 1)))
                    pool.tensor_tensor(k[:, :], ka[:, :], kb[:, :], ALU.add).then_inc(*sig["k_n"].mark(a))
                    pool.wait_ge(*sig["k_n"].at(a))
                if layer != 1:
                    kj = k[:, :].rearrange("p (j n) -> p j n", j=2)
                    pool.wait_ge(*sig["mask_ready"].at(0))
                    pool.tensor_tensor(kj, kj, KEEP[:, layer, b, :, None].to_broadcast([KJ, 2, D]), ALU.mult).then_inc(*sig["k_ready"].mark(a))
                pool.wait_ge(*sig["mask_ready"].at(0))
                if a >= 1:
                    pool.wait_ge(*sig["kt_psum"].at(a - 1))
                pool.tensor_copy(KX[:, :, :, PR:PR + 1], KBIAS[:, layer, b, :, None, None].to_broadcast([KJ, 2, G, 1])).then_inc(*sig["kx_b"].mark(a))
                pool.wait_ge(*sig["kx_h"].at(a))
                kx = KX[:, :, :, 0:PR].rearrange("p j g (h s d) -> p (j g) h s d", h=HL, s=3)
                pool.tensor_tensor(kx[:, :, :, 2, :], k[:, :].rearrange("p (m h d) -> p m h d", h=HL, d=HD), kx[:, :, :, 0, :],
                                   ALU.subtract).then_inc(*sig["kx_l"].mark(a))

            def k_expand(a):
                layer = a // B
                pool.wait_ge(*sig["kt"].at(a))
                if a >= 2:
                    pool.wait_ge(*sig["st"].at((item_of(a - 2), n_slots(item_of(a - 2)) - 1)))
                for g in range(G):
                    kin = KT[:, a % 2, g, :]
                    if layer == 0:
                        ctx_cols, _ = layout0(KB0[:, a % 2, g, :])
                        pool.tensor_tensor(ctx_cols, kin[:, None, None, :].to_broadcast([K_ALL, 2, 2, KC]),
                                           maskk[:, :].rearrange("p (f h) -> p f h", f=2)[:, :, :, None].to_broadcast([K_ALL, 2, 2, KC]),
                                           ALU.mult).then_inc(*sig["kb"].mark((a, g)))
                    else:
                        pool.tensor_tensor(KB1[:, a % 2, g, 0:HL * KC].rearrange("p (h n) -> p h n", h=HL),
                                           kin[:, None, :].to_broadcast([K_ALL, HL, KC]),
                                           maskk[:, :, None].to_broadcast([K_ALL, HL, KC]), ALU.mult).then_inc(*sig["kb"].mark((a, g)))

            def q_chain(a):
                layer = a // B
                if layer == 1:
                    pool.wait_ge(*sig["q"].at(a))
                    pool.tensor_tensor(qa[:, :], q[:, :], q[:, :], ALU.mult).then_inc(*sig["q_sq"].mark(a))
                    pool.wait_ge(*sig["q_ms"].at(a))
                    pool.tensor_scalar(qrr[:, :], qms[:, :], 1.0 / HD, RMS_EPS, ALU.mult, ALU.add).then_inc(*sig["q_var"].mark(a))
                    pool.wait_ge(*sig["q_var"].at(a))
                    pool.tensor_tensor(qrr[:, :], qrr[:, :], half[:, 0:T * H], ALU.pow).then_inc(*sig["q_rr"].mark(a))
                if layer == 2:
                    pool.wait_ge(*sig["q"].at(a))
                    if a % B == 0:
                        pool.wait_ge(*sig["wA_in2"].at(0))
                    pool.tensor_tensor(qa[:, :].rearrange("p (t h d) -> p t h d", t=T, d=HD), q[:, :].rearrange("p (t h d) -> p t h d", t=T, d=HD),
                                       ropeq[:, :, None, 0:8].to_broadcast([128, T, H, HD]), ALU.mult).then_inc(*sig["q_t1"].mark(a))

            def w_low(layer, c):
                which, lo, w = weight_chunks(layer)[c]
                serial = c + (8 if layer == 2 else 0)
                pool.wait_ge(*sig["w_h"].at(serial))
                pool.tensor_tensor(UP(layer)[:, which, 1, lo:lo + w], stage[:, serial % 2, 0:w], UP(layer)[:, which, 0, lo:lo + w],
                                   ALU.subtract).then_inc(*sig["w_l"].mark(serial))

            def lora_rows(j):
                pool.wait_ge(*sig["lora_in"].at(j))
                if ITEMS[j][2] > 0:
                    pool.wait_ge(*sig["lora_psum"].at(j - 1))
                else:
                    pool.wait_ge(*sig["w_ffn0_in"].at(0))
                pool.tensor_tensor(EBD[:, 0, :].rearrange("p (i n) -> p i n", i=4), EV[:, 0, None, :].to_broadcast([4, 4, D]),
                                   eye4[:, :, None].to_broadcast([4, 4, D]), ALU.mult).then_inc(*sig["lora_bd"].mark((j, 0)))
                pool.tensor_tensor(EBD[:, 1, :].rearrange("p (b i n) -> p b i n", b=4, i=4),
                                   EV[:, 1, :].rearrange("p (n b) -> p b n", b=4)[:, :, None, :].to_broadcast([4, 4, 4, 32]),
                                   eye4[:, None, :, None].to_broadcast([4, 4, 4, 32]), ALU.mult).then_inc(*sig["lora_bd"].mark(j))

            def piece(i, p):
                name = p[0]
                if name == "ln":
                    layer_norm(p[1])
                elif name == "kchain":
                    k_chain(p[1])
                elif name == "kexp":
                    k_expand(p[1])
                elif name == "qchain":
                    q_chain(p[1])
                elif name == "w":
                    w_low(p[1], p[2])
                elif name == "after_xt" and ITEMS[p[1]][0] == "F0":
                    lora_rows(p[1])

            n_init = 0
            for t_, v in ((CR[:, :, :], 0.0), (KT[:, :, :, :], 1.0), (KTM[:, :, :], 1.0), (QX[:, :, :, :], 1.0), (MKX[:, :, :], 0.0),
                          (half[:, :], -0.5), (MR, 0.0)):
                ins = pool.memset(t_, v)
                n_init += 1
                ins.then_inc(*sig["init_pool"].more(0))
            pool.wait_ge(*sig["init_pool"].at(0))
            for r in range(2):
                for g in range(G):
                    ins = pool.memset(KB0[:, r, g, 2 * HALF0:R0 * C0].bitcast(I32), 0)
                    ins.then_inc(*sig["init_act"].more(0))
                    ins = pool.memset(KB1[:, r, g, HL * KC:R1 * C1].bitcast(I32), 0)
                    ins.then_inc(*sig["init_act"].more(0))
            pool.wait_ge(*sig["mem_in"].at(0))
            pool.tensor_scalar(mk[:, :], mk[:, :], float(np.sqrt(HD)), None, ALU.mult).then_inc(*sig["mem_ready"].more("k"))
            pool.wait_ge(*sig["mem_ready"].at("k"))
            mx = MKX[:, :, 0:PR].rearrange("p g (h s d) -> p g h s d", h=HL, s=3)
            mk_ = mk[:, :].rearrange("p (g h d) -> p g h d", g=G, d=HD)
            for s in range(2):
                pool.tensor_copy(mx[:, :, :, s, :].bitcast(F32R), mk_).then_inc(*sig["mem_ready"].more("h"))
            pool.wait_ge(*sig["mem_ready"].at("h"))
            pool.tensor_tensor(mx[:, :, :, 2, :], mk_, mx[:, :, :, 0, :], ALU.subtract).then_inc(*sig["mem_ready"].more("l"))
            _, mem_cols = layout0(MR)
            for f in range(2):
                pool.tensor_scalar(mem_cols[:, f, :, :], mvT[:, None, :].to_broadcast([128, 2, KM]), float(np.sqrt(KM)), None, ALU.mult).then_inc(*sig["mem_ready"].more(0))
            layer_norm(0)
            k_chain(0)
            pool.wait_ge(*sig["const_in"].at(0))
            pool.wait_ge(*sig["mem_kt"].at(0))
            for r in range(2):
                for g in range(G):
                    _, mem_cols = layout0(KB0[:, r, g, :])
                    pool.tensor_tensor(mem_cols, KTM[:, g, None, None, :].to_broadcast([K_ALL, 2, 2, KM]),
                                       maskk[:, :].rearrange("p (f h) -> p f h", f=2)[:, :, :, None].to_broadcast([K_ALL, 2, 2, KM]),
                                       ALU.mult).then_inc(*sig["mem_kb"].more(0))
            k_expand(0)
            k_chain(1)
            q_chain(0)
            layer_norm(1)
            pool.wait_ge(*sig["wA_in1"].at(0))
            pool.tensor_tensor(gq[:, 0, :], gq[:, 0, :], gq[:, 1, :], ALU.mult).then_inc(*sig["gkq_ready"].mark(0))
            for i in range(len(ITEMS)):
                total, pieces = all_slots(i)
                for n in range(total):
                    for p in pieces.get(n, []):
                        piece(i, p)

    return {name: dict(s.seen) for name, s in sig.items()}


def constants():
    c = {}
    c["ident"] = np.eye(128, dtype=np.float32)
    c["eye4"] = np.eye(4, dtype=np.float32)
    m = np.zeros((K_ALL, HL), np.float32)
    for r in range(PR):
        m[r, r // (3 * HD)] = 1
    m[PR, :] = 1
    for h in range(HL):
        m[KX_ROWS + h, h] = 1
    c["maskk"] = m
    heads0 = sum([[2 * f] * KC + [2 * f + 1] * KC + [2 * f] * KM + [2 * f + 1] * KM for f in range(2)], [])
    ctx0 = sum([[1] * (2 * KC) + [0] * (2 * KM) for f in range(2)], [])
    heads1 = sum([[h] * KC for h in range(HL)], [])
    for name, heads, isctx, rows, chunks in (("0", heads0, ctx0, R0, C0), ("1", heads1, [1] * len(heads1), R1, C1)):
        mv = np.zeros((rows, chunks, G, HL, HD), np.float32)
        ind = np.zeros((1, rows * chunks), np.float32)
        for r, (h, ic) in enumerate(zip(heads, isctx)):
            mv[r % rows, r // rows, :, h, :] = 1
            ind[0, r] = ic
        c["mv" + name] = mv.reshape(rows, chunks, G, HL * HD)[:, :, 0, :]
        c["ind" + name] = ind
    inv = np.float32(10000.0) ** (np.arange(0, HD, 2, dtype=np.float32) / np.float32(HD))
    theta = (np.arange(S, dtype=np.float32)[:, None] / inv).astype(np.float32)
    sin, cos = np.sin(theta).astype(np.float32), np.cos(theta).astype(np.float32)
    for name, n, p in (("q", T, 128), ("k", 2, KJ)):
        lay = lambda a: np.ascontiguousarray(a[:n * p].reshape(n, p, -1).transpose(1, 0, 2))
        c["cos" + name] = lay(np.repeat(cos, 2, axis=-1))
        c["nsin" + name] = lay(-sin)
        c["sin" + name] = lay(sin)
    c["sink"] = c.pop("sink")
    c["lt"] = np.tril(np.ones((8, 8), np.float32), -1)
    return c


def kernel(**inp):
    import numpy as _np
    import concourse.bacc as _bacc
    from concourse import mybir as _mybir
    from concourse.bass_utils import run_bass_kernel_spmd as _run

    a = {n: _np.asarray(v) for n, v in inp.items()}
    tr = lambda w: _np.ascontiguousarray(w.T)
    arrays = {
        "x": a["x"], "ctxT": _np.ascontiguousarray(a["ctx_1024"].transpose(2, 0, 1)),
        "mask0": a["mask_Bx1x1xS2_ik0"].reshape(B, 2, KJ).transpose(2, 0, 1), "mask2": a["mask_Bx1x1xS2_bf1"].reshape(B, 2, KJ).transpose(2, 0, 1).view(_np.uint8),
        "wqT0": tr(a["L0_xattn_Wq"]), "wkT0": tr(a["L0_xattn_Wk"]), "wvT0": tr(a["L0_xattn_Wv"]), "woT0": tr(a["L0_xattn_Wo"]),
        "bq0": a["L0_xattn_bq"], "bk0": a["L0_xattn_bk"], "bv0": a["L0_xattn_bv"], "bo0": a["L0_xattn_bo"],
        "mk0": a["L0_xattn_m_k"].reshape(KM, D), "mvT0": tr(a["L0_xattn_m_v"].reshape(KM, D)),
        "w1T0": tr(a["L0_ffn_W1"]), "b1T0": tr(a["L0_ffn_b1"].reshape(4, 128)),
        "w2T0": _np.ascontiguousarray(a["L0_ffn_W2"].T.reshape(4, 128, D).transpose(1, 0, 2)),
        "b2_0": a["L0_ffn_b2"], "scale0": a["L0_ffn_scale"].reshape(1, 1),
        "wq1": a["L1_xattn_Wq"], "wkv1": a["L1_xattn_Wkv"], "wo1": a["L1_xattn_Wproj"], "bq1": a["L1_xattn_bq"],
        "bkv1": a["L1_xattn_bkv"], "bo1": a["L1_xattn_bproj"], "gq1": a["L1_xattn_gq"], "gk1": a["L1_xattn_gk"],
        "rw1": a["L1_ffn_router_w"], "rb1": a["L1_ffn_router_b"], "w1_1": a["L1_ffn_w1"], "w3_1": a["L1_ffn_w3"],
        "w2_1": _np.ascontiguousarray(a["L1_ffn_w2"].reshape(E1 * 4, 128, D).transpose(1, 0, 2)),
        "wq2": a["L2_xattn_w_q"], "wk2": a["L2_xattn_w_k"], "wv2": a["L2_xattn_w_v"], "wo2": a["L2_xattn_w_o"],
        "bq2": a["L2_xattn_b_q"], "bk2": a["L2_xattn_b_k"], "bv2": a["L2_xattn_b_v"], "bo2": a["L2_xattn_b_o"],
        "gw2": a["L2_ffn_gate_w"], "wg2": a["L2_ffn_Wg"], "wu2": a["L2_ffn_Wu"], "wd2": a["L2_ffn_Wd"],
        "sg2": a["L2_ffn_Sg"], "su2": a["L2_ffn_Su"], "sd2": a["L2_ffn_Sd"],
        "wq3": a["L3_xattn_Wq"], "bq3": a["L3_xattn_bq"], "wk3": a["L3_xattn_Wk"], "bk3": a["L3_xattn_bk"],
        "wv3": a["L3_xattn_Wv"], "bv3": a["L3_xattn_bv"], "we3T": tr(a["L3_ffn_W_expert"]), "ws3T": tr(a["L3_ffn_W_shared"]),
        "wgate3": a["L3_ffn_W_gate"], "bias3": a["L3_ffn_bias"],
    }
    arrays.update(constants())
    arrays = {f"in_{n}": _np.ascontiguousarray(arrays[n]) for n in ORDER}

    known = None
    for _ in range(2):
        nc = _bacc.Bacc("TRN2", target_bir_lowering=False, num_devices=1)
        aps = {n[3:]: nc.dram_tensor(n, v.shape, _mybir.dt.from_np(v.dtype), kind="ExternalInput").ap() for n, v in arrays.items()}
        out = nc.dram_tensor("out", (B, S, D), F32, kind="ExternalOutput").ap()
        known = program(nc, aps, out, known)
    r = _run(nc, [arrays], core_ids=[0])
    return r.results[0]["out"]
```

```python
import concourse.bass as bass
from concourse import mybir
from contextlib import ExitStack
import numpy as np

F32 = mybir.dt.float32
F32R = mybir.dt.float32r
I32 = mybir.dt.int32
U8 = mybir.dt.uint8
ALU = mybir.AluOpType
ACT = mybir.ActivationFunctionType
AX = mybir.AxisListType

B, S, D = 4, 512, 128
T = S // 128
H, HD = 16, 8
G, HL = 4, 4
KC, KM = 154, 64
KJ = KC // 2
PR = HL * 3 * HD
KX_ROWS = PR + 1
K_ALL = KX_ROWS + HL
XW = 100
N_MAX = 2 * G * T
MT_LAST = 2 * T
R0, C0 = 125, 7
R1, C1 = 124, 5
KT0 = KC + KM
BIG = 1.96875 * 2.0 ** 127
LN_EPS, RMS_EPS = 1e-5, 1e-6
SCALE = float(np.float32(1.0) / np.sqrt(np.float32(HD)))
SCALE3 = float(np.float32(1.0) / np.sqrt(np.float32(D)))
E1, F1 = 4, 512
E2, F2, FS = 8, 352, 176
E3 = 7
W2COLS = E2 * F2 + FS

KINDS = ["A", "F0", "A", "F1", "A", "F2", "A3", "F3"]
ITEMS = [(kind, n // 2, b) for n, kind in enumerate(KINDS) for b in range(B)]


def is_attn(i):
    return 0 <= i < len(ITEMS) and ITEMS[i][0] == "A"


def is_ffn(i):
    return 0 <= i < len(ITEMS) and ITEMS[i][0] != "A"


def item_of(a):
    return (a // B) * 8 + a % B


def chunk_shape(layer):
    return (R0, C0) if layer == 0 else (R1, C1)


def ffn_tiles(kind):
    if kind == "F0":
        return [(0, j * 128, 128, j) for j in range(4)]
    if kind == "F1":
        return [(e, e * F1 + j * 128, 128, e * 4 + j) for e in range(E1) for j in range(4)]
    out = [(e, e * F2 + j * 128, min(128, F2 - j * 128), e * 3 + j) for e in range(E2) for j in range(3)]
    return out + [(E2, E2 * F2 + j * 88, 88, E2 * 3 + j) for j in range(2)]


def weight_chunks(layer):
    if layer == 1:
        return [(m, e * F1, F1) for e in range(E1) for m in range(2)]
    return [(m, e * F2, F2) for e in range(E2) for m in range(2)] + [(m, E2 * F2, FS) for m in range(2)]


def last_expert(kind):
    return ffn_tiles(kind)[-1][0]


def n_slots(i):
    kind, layer, b = ITEMS[i]
    if kind == "A":
        return 4 * chunk_shape(layer)[1]
    return {"F0": 4, "F1": 16, "F2": 26, "A3": 4, "F3": 2}[kind]


def carries_on(i):
    return ITEMS[i][0] in ("F0", "F1", "F2") and i + 1 < len(ITEMS) and ITEMS[i + 1][0] == ITEMS[i][0]


def plan(i):
    slots = {}

    def put(n, *piece):
        slots.setdefault(n, []).append(piece)

    kind, layer, b = ITEMS[i]
    N = n_slots(i)
    a = layer * B + b
    nxt = i + 1
    if i + 2 < len(ITEMS):
        for t in range(T):
            put(0 if kind in ("F0", "A3", "F3") else t, "ln", i + 2, t)
        put(0 if kind in ("F0", "A3", "F3") else 3, "norm", i + 2)
    if kind == "A":
        if is_attn(nxt):
            a1 = a + 1
            if b == 0:
                put(0, "kt", a1)
            for h in range(HL):
                put(h, "kb", a1, h)
            for g in range(G):
                put(1 + g, "qxt", a1, g)
            for m in range(N_MAX):
                put(5 + m * (N - 4) // N_MAX, "max", a1, m)
            put(6 + (N_MAX - MT_LAST) * (N - 4) // N_MAX, "mt", a1, 0)
            put(N + 1, "mt", a1, 1)
            put(N, "v", a1, 0)
            put(N + 1, "v", a1, 1)
        if is_attn(i + 2):
            put(N + 3, "kt", a + 2)
        if is_ffn(nxt):
            put(2, "xt", nxt)
            put(3, "after_xt", nxt)
            for n in range(3):
                put(5 + n, "late", nxt, n)
        if is_attn(i - 1):
            put(6, "finish", i - 1)
        if is_attn(i + 2):
            put(7, "xt", i + 2)
            put(9, "q", a + 2)
            for n, name in ((9, "q1"), (11, "q2"), (12, "q3"), (16, "q4"), (17, "qsplit"), (18, "qlow")):
                put(n, name, a + 2)
        if a + 2 < 12:
            put(10, "kproj", a + 2)
            for n, name in ((10, "k1"), (12, "k2"), (13, "k3"), (N - 2, "ksplit"), (N - 1, "klow")):
                put(n, name, a + 2)
        if i + 2 < len(ITEMS) and ITEMS[i + 2][0] == "F0":
            put(10, "rows", i + 2)
        if layer > 0:
            n_w = len(weight_chunks(layer))
            for c in range(b * n_w // B, (b + 1) * n_w // B):
                put(4 + 3 * (c - b * n_w // B), "w", layer, c)
    elif kind in ("F0", "F1", "F2"):
        short = kind == "F0"
        if is_attn(i - 1):
            put(2, "finish", i - 1)
        if is_attn(nxt):
            a1 = ITEMS[nxt][1] * B + ITEMS[nxt][2]
            put(0, "kt", a1)
            for h in range(HL):
                put(0, "kb", a1, h)
            for g in range(G):
                put(1 + g // 2 if short else 1, "qxt", a1, g)
            for m in range(N_MAX):
                put(3 + m // 8 if short else 2 + m * (N - 3) // N_MAX, "max", a1, m)
            put(6 if short else 12, "mt", a1, 0)
            put(N + 4 if short else N - 1, "mt", a1, 1)
            put(N + 5 if short else 3, "v", a1, 0)
            put(N + 5 if short else 3, "v", a1, 1)
        elif ITEMS[nxt][0] != "A3":
            put(0 if short else 1, "xt", nxt)
            put(0 if short else 1, "after_xt", nxt)
            for n in range(3):
                put(2 if short else 3 + n, "late", nxt, n)
        else:
            put(4, "xt", nxt)
            put(N + 3, "proj3", nxt)
            put(N + 4, "scores3", nxt)
        if is_attn(i + 2):
            a2 = ITEMS[i + 2][1] * B + ITEMS[i + 2][2]
            at = (3, 3, 3, 4, 4, 5, 6, 7) if short else (5, 6, 6, 7, 7, 8, 8, 9)
            for n, name in zip(at, ("xt", "q", "q1", "q2", "q3", "q4", "qsplit", "qlow")):
                put(n, name, i + 2 if name == "xt" else a2)
        if i + 2 < len(ITEMS) and ITEMS[i + 2][0] == "F0":
            put(N, "rows", i + 2)
    elif kind == "A3":
        put(0, "xt", nxt)
        if ITEMS[nxt][0] == "A3":
            put(0, "proj3", nxt)
            put(2, "scores3", nxt)
        else:
            for n in range(3):
                put(2, "late", nxt, n)
    elif nxt < len(ITEMS):
        put(0, "xt", nxt)
        for n in range(3):
            put(1, "late", nxt, n)
    return slots


def all_slots(i):
    p = plan(i)
    tail = 0 if carries_on(i) or ITEMS[i][0] in ("A3", "F3") else 4
    return max([n_slots(i) + tail] + [n + 1 for n in p]), p


class Signal:

    def __init__(self, sem, known, step=1):
        self.sem, self.known, self.step, self.count, self.seen = sem, known, step, 0, {}

    def mark(self, label):
        assert label not in self.seen, label
        self.count += self.step
        self.seen[label] = self.count
        return self.sem, self.step

    def more(self, label):
        self.count += self.step
        self.seen[label] = self.count
        return self.sem, self.step

    def at(self, label):
        return self.sem, (self.known[label] if self.known is not None else 1)


DMA_SIGNALS = ["ident_in", "w_ffn3_in", "w_proj3_in", "x_in0", "x_in1", "x_in2", "x_in3", "const_in", "ctx_in", "mask_in", "wA_in0", "wA_in1", "wA_in2", "w_ffn0_in",
               "cr_in0", "cr_in1", "stage_in0", "stage_in1", "wd_in",
               "shift_in0", "shift_in1", "lora_in", "w3_in", "mem_in", "out_done"]
SIGNALS = [
    "init_pool", "init_dve", "init_kb", "shift_rows0", "shift_rows", "mask_ready", "gkq_ready", "mem_ready", "mem_kb", "mem_kt_psum",
    "ln_stats", "ln_aggr", "ln_var", "ln_rstd", "x_centred", "xn", "bias_in_x", "xt_psum", "xt", "xh", "xl",
    "k_psum", "k", "k_sq", "k_ms", "k_var", "k_seed", "q_seed", "k_rr", "k_n", "k_ready", "k_t1", "k_t2", "kx_h", "kx_b", "kx_l",
    "kt_psum", "kb",
    "v_psum", "vb",
    "q_psum", "q", "q_sq", "q_ms", "q_var", "q_rr", "q_ready", "q_t1", "q_t2", "qx_h", "qx_l", "qxt_psum", "qxt",
    "mx_psum", "mx", "mt_psum", "mt",
    "st", "p", "pv", "dn", "pv_out", "dn_out", "rden", "on", "o_psum", "resid",
    "up", "act", "h", "h_gelu", "y", "acc", "lg_psum", "lg", "lg_nm", "lg_sh", "lg_e", "lg_c", "lg_es", "lg_sum", "lg_r", "gates",
    "lora_bd", "lora_psum", "lora_w", "lora_h", "lora_l", "w_h", "w_l",
    "a3_psum", "a3_q", "a3_k", "a3_v", "a3_s", "a3_nm", "a3_nms", "a3_p", "a3_r", "a3_ptp", "a3_pt", "a3_o", "f3_psum", "f3_y",
]

ORDER = ["x", "ctxT", "mask0", "mask2", "wqT0", "wkT0", "wvT0", "woT0", "bq0", "bk0", "bv0", "bo0", "mk0", "mvT0",
         "w1T0", "b1T0", "w2T0", "b2_0", "scale0",
         "wq1", "wkv1", "wo1", "bq1", "bkv1", "bo1", "gq1", "gk1", "rw1", "rb1", "w1_1", "w3_1", "w2_1",
         "wq2", "wk2", "wv2", "wo2", "bq2", "bk2", "bv2", "bo2", "gw2", "wg2", "wu2", "wd2", "sg2", "su2", "sd2",
         "wq3", "bq3", "wk3", "bk3", "wv3", "bv3", "we3T", "ws3T", "wgate3", "bias3",
         "ident", "maskk", "mv0", "mv1", "ind0", "cosq", "nsinq", "sinq", "cosk", "nsink", "sink", "lt", "eye4"]


def program(nc, A, out, known):
    ctx = ExitStack()
    with ctx:
        def sb(name, shape, dt=F32):
            return ctx.enter_context(nc.sbuf_tensor(name, shape, dt))

        sig = {}
        for name in SIGNALS + DMA_SIGNALS:
            step = 16 if name in DMA_SIGNALS else 1
            sig[name] = Signal(ctx.enter_context(nc.semaphore(name)), known[name] if known else None, step)

        PS = ctx.enter_context(nc.psum_tensor("PS", [128, 8, 512], F32))
        x = sb("x_res", [128, B * T, D])
        ident = sb("ident_sb", [128, 128])
        ctxT = sb("ctxT_sb", [128, B, KC])
        CR = sb("ctx_rep", [128, 2, R0 * C0])
        arena = sb("arena", [128, 12288], F32R)
        WD = sb("down_w", [128, 26 * 128])
        work = sb("work", [128, 5120])
        QXT = sb("qxt_sb", [K_ALL, 2, G, S], F32R)
        KB1 = sb("kb_sb", [K_ALL, 2, G, R1 * C1], F32R)
        KX = sb("kx_sb", [KJ, 2, 2, G, XW])
        QX = sb("qx_sb", [128, T, G, XW])
        q = sb("q_sb", [128, S])
        qa = sb("qa_sb", [128, S])
        qb = sb("qb_sb", [128, S])
        k = sb("k_sb", [KJ, 2 * D])
        ka = sb("ka_sb", [KJ, 2 * D])
        kb = sb("kb_tmp", [KJ, 2 * D])
        VB = sb("vb_sb", [R0, 2, C0, D])
        xn = sb("xn_sb", [128, 2, T, D])
        xT = sb("xt_sb", [128, 2, S])
        xH = sb("xh_sb", [128, 2, S], F32R)
        xL = sb("xl_sb", [128, 2, S], F32R)
        stage = sb("stage", [128, 2, 512])
        MV0 = sb("mv0_sb", [R0, C0, HL * HD])
        MV1 = sb("mv1_sb", [R1, C1, HL * HD])
        IND0 = sb("ind0_sb", [1, R0 * C0])
        maskk = sb("maskk_sb", [K_ALL, HL])
        WA = sb("w_attn", [128, 2, 4, D])
        BQ = sb("b_q", [128, 2, D])
        BK = sb("b_k", [KJ, 2, D])
        BVr = sb("b_v", [1, 3, D])
        BO = sb("b_out", [128, 5, D])
        KEEP = sb("keep", [KJ, 3, B, 2])
        KBIAS = sb("kbias", [KJ, 3, B, 2])
        mraw0 = sb("mask_raw0", [KJ, B, 2], I32)
        mraw2 = sb("mask_raw2", [KJ, B, 2], U8)
        ropeq = sb("rope_q", [128, T, 16])
        ropek = sb("rope_k", [KJ, 2, 16])
        gq = sb("gq_sb", [KJ, 2, HD])
        half = sb("minus_half", [128, 64])
        st6 = sb("bn_st", [128, 2, T, 6])
        mvar = sb("bn_mv", [128, 2, T, 2])
        rstd = sb("rstd", [128, 2, T])
        qms = sb("q_ms_sb", [128, T * H])
        qrr = sb("q_rr_sb", [128, T * H])
        qtmp = sb("q_tmp", [128, T * H])
        ktmp = sb("k_tmp", [KJ, 2 * H])
        kms = sb("k_ms_sb", [KJ, 2 * H])
        krr = sb("k_rr_sb", [KJ, 2 * H])
        mneg = sb("mneg", [128, 2, T, H])
        a3s = sb("a3_small", [128, 4, T])
        gsum = sb("gate_sum", [128, 2, T])
        mT = sb("mt_sb", [H - HL, 2, S], F32R)
        b1T = sb("b1t", [128, 4])
        scale0 = sb("scale0_sb", [128, 1])
        eye4 = sb("eye4_sb", [4, 4])
        LT = sb("lt_sb", [128, 8, 8])
        RW1 = sb("rw1_sb", [128, E1])
        RB1 = sb("rb1_sb", [128, E1])
        GW2 = sb("gw2_sb", [128, E2])
        lg = sb("lg_sb", [128, T, 8])
        lsh = sb("lsh_sb", [128, T, 8])
        le = sb("le_sb", [128, T, 8])
        lga = sb("lga_sb", [128, T, 8, 8])
        lgb = sb("lgb_sb", [128, T, 8, 8])
        lsm = sb("lsm_sb", [128, 4, T])
        gates = sb("gates_sb", [128, 2, T, 8])
        bqk3 = sb("bqk3_sb", [128, 2])
        stage1 = stage[:, :, :].rearrange("p r n -> p (r n)")
        MKX = stage1[0:KM, 0:G * XW].rearrange("p (g n) -> p g n", g=G)
        mk = stage1[0:KM, 400:400 + D]
        mvT = stage1[:, 528:528 + KM]
        EV = qb[0:4, 0:2 * D].rearrange("p (n c) -> p n c", n=2)
        OD = qb[0:4, 2 * D:4 * D].rearrange("p (n c) -> p n c", n=2)
        EBD = work[0:4, 4096:5120].rearrange("p (n c) -> p n c", n=2)
        W3 = WA[:, 1, 0:3, :]
        BV3 = BK[:, 1, :]
        WF3 = WA[:, 0, :, :].rearrange("p n c -> p (n c)")

        W1T = WD[:, 0:512]
        W2T = WD[:, 512:1024]
        W2E = WD[:, 1024:2048].rearrange("p (r n) -> p r n", r=2)
        MR = WD[:, 2048:2048 + R0 * C0]
        KB0 = arena[0:K_ALL, 0:2 * G * R0 * C0].rearrange("p (r g n) -> p r g n", r=2, g=G)
        W1E = arena[:, 7168:7168 + 2048].rearrange("p (r h n) -> p r h n", r=2, h=2)
        UP1 = arena[:, 0:8192].rearrange("p (m h n) -> p m h n", m=2, h=2)
        UP2 = arena[:, 0:4 * W2COLS].rearrange("p (m h n) -> p m h n", m=2, h=2)
        P = work[:, 0:3072].rearrange("p (r n) -> p r n", r=6)
        RD, ON = work[:, 3072:3584], work[:, 3584:4096]
        HH = work[:, 0:4096].rearrange("p (r j n) -> p r j n", r=2, j=4)
        SS = work[:, 4096:5120].rearrange("p (r n) -> p r n", r=2)
        QT3, KT3 = work[:, 0:512], work[:, 512:512 + KC]
        V3 = work[0:KJ, 3072:3584].rearrange("p (r j n) -> p r j n", r=2, j=2)
        P3 = work[:, 1024:1024 + T * KC].rearrange("p (t n) -> p t n", t=T)
        PT3 = work[0:KJ, 2048:3072].rearrange("p (b n) -> p b n", b=2)

        def KB(layer):
            return KB0 if layer == 0 else KB1

        def UP(layer):
            return UP1 if layer == 1 else UP2

        def layout0(t):
            v = t[:, 0:HL * KT0].rearrange("p (h n) -> p h n", h=HL)
            return v[:, :, 0:KC], v[:, :, KC:KT0]

        def bias_slot(i):
            kind, layer, b = ITEMS[i]
            return {"A": layer, "F0": 3, "F3": 4}.get(kind)

        def key_columns(layer, r):
            if layer == 0:
                return KB0[:, r, :, 0:HL * KT0].rearrange("p g (h n) -> p g h n", h=HL)[:, :, :, 0:KC]
            return KB1[:, r, :, 0:HL * KC].rearrange("p g (h n) -> p g h n", h=HL)

        def qxt_bank(i_main, g):
            return (2 if i_main is not None and ITEMS[i_main][0] == "A" else 4) + g % 2

        def root_seed(ms, rr, sums, var, seed, a):
            nc.vector.wait_ge(*sums.at(a))
            nc.vector.tensor_scalar(ms, ms, 1.0 / HD, RMS_EPS, ALU.mult, ALU.add).then_inc(*var.mark(a))
            nc.vector.wait_ge(*var.at(a))
            nc.vector.tensor_scalar(rr.bitcast(I32), ms.bitcast(I32), -0.5, float(0x5F3759DF), ALU.mult, ALU.add).then_inc(*seed.mark(a))

        def root_newton(ms, rr, tmp, seed, step, a):
            nc.gpsimd.wait_ge(*seed.at(a))
            for m in range(3):
                nc.gpsimd.tensor_tensor(tmp, rr, rr, ALU.mult).then_inc(*step.mark((a, m, 0)))
                nc.gpsimd.wait_ge(*step.at((a, m, 0)))
                nc.gpsimd.tensor_tensor(tmp, tmp, ms, ALU.mult).then_inc(*step.mark((a, m, 1)))
                nc.gpsimd.wait_ge(*step.at((a, m, 1)))
                nc.gpsimd.tensor_scalar(tmp, tmp, -0.5, 1.5, ALU.mult, ALU.add).then_inc(*step.mark((a, m, 2)))
                nc.gpsimd.wait_ge(*step.at((a, m, 2)))
                nc.gpsimd.tensor_tensor(rr, rr, tmp, ALU.mult).then_inc(*step.mark((a, m, 3)))
                nc.gpsimd.wait_ge(*step.at((a, m, 3)))

        def shift_signal(layer):
            return sig["shift_rows"] if layer else sig["shift_rows0"]

        def shift_rows(eng, layer, r):
            w = HL * (KT0 if layer == 0 else KC)
            eng.tensor_copy(KB(layer)[PR:K_ALL, r, :, 0:w].rearrange("p g (h n) -> p g h n", h=HL),
                            maskk[PR:K_ALL, None, :, None].to_broadcast([K_ALL - PR, G, HL, w // HL])).then_inc(
                *shift_signal(layer).mark((layer > 0, r)))

        def mt_bank(i_main, part):
            return 2 if part and i_main is not None and ITEMS[i_main][0] == "A" else 4

        def mt_heads(part):
            return (slice(0, H - HL), slice(H - HL, H))[part]

        def mx_bank(i_main, m):
            if i_main is None:
                return (0, 1, 2, 3, 6, 7)[m % 6]
            return (2 if ITEMS[i_main][0] == "A" else 4) + m % 2

        def accumulated(i, e):
            return sig["resid"].at(i) if e == last_expert(ITEMS[i][0]) else sig["acc"].at((i, e))

        def last_of_parity(kind, parity):
            e = last_expert(kind)
            return e if e % 2 == parity else e - 1

        block = ctx.enter_context(nc.Block())

        @block.sync
        def _(sp):
            def load_cr(sp, a):
                if a >= 2:
                    sp.wait_ge(*sig["v_psum"].at((a - 2, 1)))
                src = A["ctxT"][:, a % B, None, :].to_broadcast([128, HL, KC])
                dst = layout0(CR[:, a % 2, :])[0] if a < B else CR[:, a % 2, 0:HL * KC].rearrange("p (h n) -> p h n", h=HL)
                sp.dma_start(dst, src).then_inc(*sig[f"cr_in{a % 2}"].mark(a))

            def mt_dma(sp, a, part):
                sp.wait_ge(*sig["mt"].at((a, part)))
                for g in ((0, 1, 2), (3,))[part]:
                    src = mT[(g % 3) * HL:(g % 3 + 1) * HL, part, :]
                    sp.dma_start(QXT[KX_ROWS:K_ALL, a % 2, g, :].bitcast(F32), src.bitcast(F32)).then_inc(*sig[f"shift_in{part}"].more(a))

            def stage_dma(sp, layer, c):
                which, lo, w = weight_chunks(layer)[c]
                serial = c + (8 if layer == 2 else 0)
                if serial >= 2:
                    sp.wait_ge(*sig["w_l"].at(serial - 2))
                if layer == 1:
                    src = A[("w1_1", "w3_1")[which]][lo // F1]
                elif lo < E2 * F2:
                    src = A[("wg2", "wu2")[which]][lo // F2]
                else:
                    src = A[("sg2", "su2")[which]]
                sp.dma_start(stage[:, serial % 2, 0:w], src).then_inc(*sig[f"stage_in{serial % 2}"].mark(serial))

            def lora_dma(sp, j):
                sp.wait_ge(*sig["xn"].at(j))
                if ITEMS[j][2] > 0:
                    sp.wait_ge(*sig["lora_psum"].at((j - 1, 1)))
                for n in range(2):
                    sp.dma_start(EV[:, n, :], xn[1 + 8 * n:9 + 8 * n:2, j % 2, 0, :]).then_inc(*sig["lora_in"].more(j))
                    sp.dma_start(OD[:, n, :], xn[2 + 8 * n:10 + 8 * n:2, j % 2, 0, :]).then_inc(*sig["lora_in"].more(j))

            def load(dst, src, name, label):
                sp.dma_start(dst, src).then_inc(*sig[name].more(label))

            xv = A["x"].rearrange("b (t p) d -> p b t d", p=128)
            for b in range(B):
                load(x[:, b * T:(b + 1) * T, :], xv[:, b, :, :], f"x_in{b}", 0)
                if b == 0:
                    load(ident[:, :], A["ident"], "ident_in", 0)
                    load(ctxT[:, :, :], A["ctxT"], "ctx_in", 0)
                    load(mraw0[:, :, :], A["mask0"], "mask_in", 0)
                    load(mraw2[:, :, :], A["mask2"], "mask_in", 0)
                    for n, name in enumerate(["wqT0", "wkT0", "wvT0", "woT0"]):
                        load(WA[:, 0, n, :], A[name], "wA_in0", 0)
                    for dst, name in ((BQ[:, 0, :], "bq0"), (BK[:, 0, :], "bk0"), (BVr[:, 0, :], "bv0"), (BO[:, 0, :], "bo0")):
                        load(dst, A[name][None, :].to_broadcast([dst.shape[0], D]), "wA_in0", 0)
                    load(mk[:, :], A["mk0"], "mem_in", 0)
                    load(mvT[:, :], A["mvT0"], "mem_in", 0)
                    load(maskk[:, :], A["maskk"], "const_in", 0)
                    load(MV0[:, :, :], A["mv0"], "const_in", 0)
                    load(IND0[:, :], A["ind0"], "const_in", 0)
            for a in range(2):
                sp.wait_ge(*sig["init_pool"].at(0))
                load_cr(sp, a)
            for dst, name in ((W1T, "w1T0"), (W2T.rearrange("p (j n) -> p j n", j=4), "w2T0"), (b1T[:, :], "b1T0"), (eye4[:, :], "eye4"),
                              (scale0[:, :], None), (BO[:, 3, :], "b2_0")):
                src = A["scale0"].to_broadcast([128, 1]) if name is None else A[name]
                if name == "b2_0":
                    src = src[None, :].to_broadcast([128, D])
                load(dst, src, "w_ffn0_in", 0)
            for n, (name, lo) in enumerate([("wq1", 0), ("wkv1", 0), ("wkv1", D), ("wo1", 0)]):
                load(WA[:, 1, n, :], A[name][:, lo:lo + D], "wA_in1", 0)
            for dst, name, lo in ((BQ[:, 1, :], "bq1", 0), (BK[:, 1, :], "bkv1", 0), (BVr[:, 1, :], "bkv1", D), (BO[:, 1, :], "bo1", 0)):
                load(dst, A[name][None, lo:lo + D].to_broadcast([dst.shape[0], D]), "wA_in1", 0)
            for j, name in enumerate(["gq1", "gk1"]):
                load(gq[:, j, :], A[name][None, :].to_broadcast([KJ, HD]), "wA_in1", 0)
            load(MV1[:, :, :], A["mv1"], "wA_in1", 0)
            load(LT[:, :, :], A["lt"][None, :, :].to_broadcast([128, 8, 8]), "w3_in", 0)
            load(RW1[:, :], A["rw1"], "w3_in", 0)
            load(RB1[:, :], A["rb1"][None, :].to_broadcast([128, E1]), "w3_in", 0)
            load(GW2[:, :], A["gw2"], "w3_in", 0)
            for lo, hi, nq, nk in ((0, 8, "cosq", "cosk"), (8, 12, "nsinq", "nsink"), (12, 16, "sinq", "sink")):
                load(ropeq[:, :, lo:hi], A[nq], "wA_in2", 0)
                load(ropek[:, :, lo:hi], A[nk], "wA_in2", 0)
            load(bqk3[:, 0:1], A["bq3"].rearrange("(p n) -> p n", n=1), "w3_in", 0)
            load(bqk3[:, 1:2], A["bk3"].rearrange("(p n) -> p n", n=1), "w3_in", 0)
            load(BO[:, 4, :], A["bias3"][None, :].to_broadcast([128, D]), "w3_in", 0)

            mt_dma(sp, 0, 0)
            mt_dma(sp, 0, 1)
            for i in range(len(ITEMS)):
                total, pieces = all_slots(i)
                kind, layer, b = ITEMS[i]
                if i == 2 * B - 3:
                    sp.wait_ge(*sig["resid"].at(B - 1))
                    for n, name in enumerate(["wq2", "wk2", "wv2", "wo2"]):
                        load(WA[:, 0, n, :], A[name], "wA_in2", 0)
                    for dst, name in ((BQ[:, 0, :], "bq2"), (BK[:, 0, :], "bk2"), (BVr[:, 2, :], "bv2"), (BO[:, 2, :], "bo2")):
                        load(dst, A[name][None, :].to_broadcast([dst.shape[0], D]), "wA_in2", 0)
                if i == 4 * B - 3:
                    sp.wait_ge(*sig["resid"].at(3 * B - 1))
                    for n, name in enumerate(["wq3", "wk3", "wv3"]):
                        load(W3[:, n, :], A[name], "w_proj3_in", 0)
                    load(BV3[:, :], A["bv3"][None, :].to_broadcast([KJ, D]), "w_proj3_in", 0)
                if i == 6 * B - 3:
                    sp.wait_ge(*sig["resid"].at(5 * B - 1))
                    load(WF3[:, 0:D], A["we3T"], "w_ffn3_in", 0)
                    load(WF3[:, D:2 * D], A["ws3T"], "w_ffn3_in", 0)
                    load(WF3[:, 2 * D:2 * D + E3], A["wgate3"], "w_ffn3_in", 0)
                if kind == "A" and b == 0 and layer > 0:
                    sp.wait_ge(*sig["resid"].at(i - 1))
                    if layer == 1:
                        sp.dma_start(WD[:, 0:2048].rearrange("p (c n) -> p c n", c=16), A["w2_1"]).then_inc(*sig["wd_in"].more(1))
                    else:
                        for e in range(E2):
                            for j, w in ((0, 2 * 128), (2, 96)):
                                dst = WD[0:min(w, 128), (e * 3 + j) * 128:(e * 3 + j + (w + 127) // 128) * 128]
                                src = A["wd2"][e, j * 128:j * 128 + w, :]
                                if j == 0:
                                    dst = dst.rearrange("p (c n) -> p c n", c=2)
                                    src = src.rearrange("(c p) n -> p c n", c=2)
                                sp.dma_start(dst, src).then_inc(*sig["wd_in"].more(2))
                        sp.dma_start(WD[0:88, 24 * 128:26 * 128].rearrange("p (c n) -> p c n", c=2),
                                     A["sd2"].rearrange("(c p) n -> p c n", c=2)).then_inc(*sig["wd_in"].more(2))
                for n in range(total):
                    for piece in pieces.get(n, []):
                        if piece[0] == "mt":
                            mt_dma(sp, piece[1], piece[2])
                        elif piece[0] == "w":
                            stage_dma(sp, piece[1], piece[2])
                        elif piece[0] == "rows":
                            lora_dma(sp, piece[1])
                        elif piece[0] == "v" and piece[2] == 1 and piece[1] + 1 < 12:
                            load_cr(sp, piece[1] + 1)
                if kind == "F3":
                    sp.wait_ge(*sig["resid"].at(i))
                    sp.dma_start(out.rearrange("b (t p) d -> p b t d", p=128)[:, b, :, :],
                                 x[:, b * T:(b + 1) * T, :]).then_inc(*sig["out_done"].mark(b))
            sp.wait_ge(*sig["out_done"].at(B - 1))

        @block.tensor
        def _(pe):
            taken = {}

            def k_proj(a):
                layer, b = a // B, a % B
                if a == 0:
                    pe.wait_ge(*sig["ctx_in"].at(0))
                if b == 0:
                    pe.wait_ge(*sig[f"wA_in{layer}"].at(0))
                if 5 in taken:
                    pe.wait_ge(*taken[5])
                for j in range(2):
                    mm = pe.matmul(PS[0:KJ, 5, j * D:(j + 1) * D], ctxT[:, b, j * KJ:(j + 1) * KJ], WA[:, layer % 2, 1, :],
                                   start=True, stop=True)
                mm.then_inc(*sig["k_psum"].mark(a))
                taken[5] = sig["k"].at(a)

            def k_transposes(a):
                pe.wait_ge(*sig["kx_l"].at(a))
                pe.wait_ge(*sig["kx_b"].at(a))
                pe.wait_ge(*taken[4])
                pe.wait_ge(*taken[5])
                for g in range(G):
                    for j in range(2):
                        mm = pe.transpose(PS[0:KX_ROWS, 4 + g // 2, (g % 2) * KC + j * KJ:(g % 2) * KC + (j + 1) * KJ],
                                          KX[:, a % 2, j, g, 0:KX_ROWS], ident[0:KJ, 0:KJ])
                mm.then_inc(*sig["kt_psum"].mark(a))
                taken[4] = taken[5] = sig["kb"].at((a, HL - 1))

            def v_blocks(a, part):
                layer, b = a // B, a % B
                rows, chunks = chunk_shape(layer)
                if part == 0:
                    pe.wait_ge(*sig[f"cr_in{a % 2}"].at(a))
                    if a == 0:
                        pe.wait_ge(*sig["mem_ready"].at(0))
                        pe.wait_ge(*sig["const_in"].at(0))
                pe.wait_ge(*taken[4 + part])
                for c in range(4 * part, min(4 * part + 4, chunks)):
                    o = PS[0:rows, 4 + part, (c % 4) * D:(c % 4 + 1) * D]
                    cols = slice(c * rows, (c + 1) * rows)
                    mem = layer == 0 and (c + 1) * rows > KC
                    pe.matmul(o, CR[:, a % 2, cols], WA[:, layer % 2, 2, :], start=True, stop=False)
                    ind = IND0[:, cols] if layer == 0 else IND0[:, 0:rows]
                    mm = pe.matmul(o, ind, BVr[:, layer, :], start=False, stop=not mem)
                    if mem:
                        mm = pe.matmul(o, MR[:, cols], ident[:, :], start=False, stop=True)
                mm.then_inc(*sig["v_psum"].mark((a, part)))
                taken[4 + part] = sig["vb"].at((a, part))

            def xt(j):
                pe.wait_ge(*sig["xn"].at(j))
                if j == 0:
                    pe.wait_ge(*sig["ident_in"].at(0))
                if 4 in taken:
                    pe.wait_ge(*taken[4])
                for t in range(T):
                    mm = pe.transpose(PS[:, 4, t * 128:(t + 1) * 128], xn[:, j % 2, t, :], ident[:, :])
                mm.then_inc(*sig["xt_psum"].mark(j))
                taken[4] = sig["xt"].at(j)

            def q_proj(a):
                i, layer = item_of(a), a // B
                pe.wait_ge(*sig["xt"].at(i))
                pe.wait_ge(*taken[4])
                for t in range(T):
                    mm = pe.matmul(PS[:, 4, t * D:(t + 1) * D], xT[:, i % 2, t * 128:(t + 1) * 128], WA[:, layer % 2, 0, :],
                                   start=True, stop=True)
                mm.then_inc(*sig["q_psum"].mark(a))
                taken[4] = sig["q"].at(a)

            def qxt(i_main, a, g):
                bank = qxt_bank(i_main, g)
                pe.wait_ge(*sig["qx_l"].at(a))
                if bank in taken:
                    pe.wait_ge(*taken[bank])
                for t in range(T):
                    mm = pe.transpose(PS[0:KX_ROWS, bank, t * 128:(t + 1) * 128], QX[:, t, g, 0:KX_ROWS], ident[:, :])
                mm.then_inc(*sig["qxt_psum"].mark((a, g)))
                taken[bank] = sig["qxt"].at((a, g))

            def scores_for_max(i_main, a, m):
                g, f, t, layer = m // (2 * T), m // T % 2, m % T, a // B
                bank = mx_bank(i_main, m)
                if m % (2 * T) == 0:
                    pe.wait_ge(*sig["qxt"].at((a, g)))
                    pe.wait_ge(*sig["kb"].at((a, HL - 1)))
                    if a < 2:
                        pe.wait_ge(*sig["mem_kb"].at(0))
                if bank in taken:
                    pe.wait_ge(*taken[bank])
                w = 2 * (KT0 if layer == 0 else KC)
                pe.matmul(PS[:, bank, 0:w], QXT[0:KX_ROWS, a % 2, g, t * 128:(t + 1) * 128],
                          KB(layer)[0:KX_ROWS, a % 2, g, f * w:(f + 1) * w], start=True, stop=True).then_inc(*sig["mx_psum"].mark((a, m)))
                taken[bank] = sig["mx"].at((a, m))

            def maxima_transposed(i_main, a, part):
                bank, heads = mt_bank(i_main, part), mt_heads(part)
                pe.wait_ge(*sig["mx"].at((a, N_MAX - 1 if part else N_MAX - MT_LAST - 1)))
                pe.wait_ge(*taken[bank])
                for t in range(T):
                    mm = pe.transpose(PS[0:heads.stop - heads.start, bank, t * 128:(t + 1) * 128], mneg[:, a % 2, t, heads], ident[:, :])
                mm.then_inc(*sig["mt_psum"].mark((a, part)))
                taken[bank] = sig["mt"].at((a, part))

            def router(j):
                kind = ITEMS[j][0]
                w, n = {"F1": (RW1[:, :], E1), "F2": (GW2[:, :], E2), "F3": (WF3[:, 2 * D:2 * D + E3], E3)}[kind]
                pe.wait_ge(*sig["xt"].at(j))
                pe.wait_ge(*sig["w_ffn3_in" if kind == "F3" else "w3_in"].at(0))
                pe.wait_ge(*taken[5])
                for t in range(T):
                    mm = pe.matmul(PS[:, 5, t * n:(t + 1) * n], xT[:, j % 2, t * 128:(t + 1) * 128], w,
                                   start=True, stop=True)
                mm.then_inc(*sig["lg_psum"].mark(j))
                taken[5] = sig["lg"].at(j)

            def lora(j):
                pe.wait_ge(*sig["lora_bd"].at(j))
                for n in range(2):
                    pe.wait_ge(*taken[5])
                    pe.matmul(PS[:, 5, :], OD[:, n, :], EBD[:, n, :], start=True, stop=True).then_inc(*sig["lora_psum"].mark((j, n)))
                    taken[5] = sig["lora_w"].at((j, n))

            def piece(i, p):
                name = p[0]
                if name == "kproj":
                    k_proj(p[1])
                elif name == "kt":
                    k_transposes(p[1])
                elif name == "v":
                    v_blocks(p[1], p[2])
                elif name == "xt":
                    xt(p[1])
                elif name == "q":
                    q_proj(p[1])
                elif name == "qxt":
                    qxt(i, p[1], p[2])
                elif name == "max":
                    scores_for_max(i, p[1], p[2])
                elif name == "mt":
                    maxima_transposed(i, p[1], p[2])
                elif name == "late" and p[2] == 0:
                    lora(p[1]) if ITEMS[p[1]][0] == "F0" else router(p[1])
                elif name == "finish":
                    attention_out(p[1])
                elif name == "proj3":
                    projections3(p[1])
                elif name == "scores3":
                    scores3(p[1])

            def attention_step(i, n):
                _, layer, b = ITEMS[i]
                a = layer * B + b
                rows, chunks = chunk_shape(layer)
                N = 4 * chunks
                if n < N:
                    c, g = n // 4, n % 4
                    if n == 0:
                        pe.wait_ge(*sig["shift_in0"].at(a))
                        if a < 2:
                            pe.wait_ge(*sig["init_kb"].at(0))
                        if a % B < 2:
                            pe.wait_ge(*shift_signal(layer).at((layer > 0, a % 2)))
                    if n == G - 1:
                        pe.wait_ge(*sig["shift_in1"].at(a))
                    if n % 2 in taken:
                        pe.wait_ge(*taken[n % 2])
                    pe.matmul(PS[0:rows, n % 2, :], KB(layer)[0:K_ALL, a % 2, g, c * rows:(c + 1) * rows],
                              QXT[0:K_ALL, a % 2, g, :], start=True, stop=True).then_inc(*sig["st"].mark((i, n)))
                    taken[n % 2] = sig["p"].at((i, n))
                for name, lag, bank in (("pv", 2, 6), ("dn", 4, 7)):
                    m = n - lag
                    if 0 <= m < N:
                        c, g = m // 4, m % 4
                        pe.wait_ge(*sig["p"].at((i, m)))
                        if m == 0:
                            if name == "pv":
                                pe.wait_ge(*sig["vb"].at((a, 1)))
                            if bank in taken:
                                pe.wait_ge(*taken[bank])
                        mask = MV0 if layer == 0 else MV1
                        lhsT = VB[0:rows, a % 2, c, g * 32:(g + 1) * 32] if name == "pv" else mask[0:rows, c, :]
                        pe.matmul(PS[32 * g:32 * g + 32, bank, :], lhsT, P[0:rows, m % 6, :],
                                  start=(c == 0), stop=(c == chunks - 1)).then_inc(*sig[name].mark((i, m)))
                        if m == N - 1:
                            taken[bank] = sig[name + "_out"].at(i)

            def attention_out(i):
                _, layer, b = ITEMS[i]
                pe.wait_ge(*sig["on"].at(i))
                pe.wait_ge(*taken[5])
                for t in range(T):
                    mm = pe.matmul(PS[:, 5, t * D:(t + 1) * D], ON[:, t * 128:(t + 1) * 128], WA[:, layer % 2, 3, :],
                                   start=True, stop=True)
                mm.then_inc(*sig["o_psum"].mark(i))
                taken[5] = sig["resid"].at(i)

            def up(i, kt):
                kind, layer, b = ITEMS[i]
                e, col, rows, slot = ffn_tiles(kind)[kt]
                bank = 2 * (kt % 2)
                if kt == 0:
                    pe.wait_ge(*sig["xl"].at(i))
                    if kind == "F0":
                        pe.wait_ge(*sig["lora_l"].at(i))
                    elif b == 0:
                        pe.wait_ge(*sig["w_l"].at(len(weight_chunks(1)) - 1 if layer == 1 else 8 + len(weight_chunks(2)) - 1))
                for m in range(1 if kind == "F0" else 2):
                    pe.wait_ge(*taken[bank + m])
                    taken[bank + m] = sig["h_gelu" if kind == "F0" else "h"].at((i, kt))
                for m in range(1 if kind == "F0" else 2):
                    if kind == "F0":
                        w = [W1E[:, b % 2, hl, col:col + rows] for hl in range(2)]
                    else:
                        w = [UP(layer)[:, m, hl, col:col + rows] for hl in range(2)]
                    o = PS[0:rows, bank + m, :]
                    pe.matmul(o, w[0], xH[:, i % 2, :], start=True, stop=False)
                    pe.matmul(o, w[0], xL[:, i % 2, :], start=False, stop=False)
                    pe.matmul(o, w[1], xH[:, i % 2, :], start=False, stop=True).then_inc(*sig["up"].mark((i, kt, m)))

            def down(i, e):
                kind, layer, b = ITEMS[i]
                tiles = [(n, tl) for n, tl in enumerate(ffn_tiles(kind)) if tl[0] == e]
                pe.wait_ge(*sig["h_gelu" if kind == "F0" else "h"].at((i, tiles[-1][0])))
                if e == 0 and b == 0:
                    if kind != "F0":
                        pe.wait_ge(*sig["wd_in"].at(layer))
                bank = 6 + (b if kind == "F0" else e) % 2
                pe.wait_ge(*taken[bank])
                taken[bank] = accumulated(i, e)
                if kind == "F0":
                    pe.wait_ge(*sig["lora_w"].at((i, 1)))
                for t in range(T):
                    for j, (n, (_, _, rows, slot)) in enumerate(tiles):
                        rhs = W2E[:, b % 2, j * 128:(j + 1) * 128] if kind == "F0" else WD[0:rows, slot * 128:(slot + 1) * 128]
                        mm = pe.matmul(PS[:, bank, t * 128:(t + 1) * 128], HH[0:rows, bank - 6, j, t * 128:(t + 1) * 128], rhs,
                                       start=(j == 0), stop=(j == len(tiles) - 1))
                mm.then_inc(*sig["y"].mark((i, e)))

            def ffn_step(i, n):
                kind = ITEMS[i][0]
                tiles = ffn_tiles(kind)
                if n < len(tiles):
                    up(i, n)
                if n < 4 and carries_on(i - 1):
                    downs(i - 1, n + len(tiles))
                if n < len(tiles) or not carries_on(i):
                    downs(i, n)

            def downs(i, n):
                tiles = ffn_tiles(ITEMS[i][0])
                for e in range(tiles[-1][0] + 1):
                    last = max(m for m, tl in enumerate(tiles) if tl[0] == e)
                    if n == last + 2:
                        down(i, e)

            def projections3(i):
                b = ITEMS[i][2]
                pe.wait_ge(*sig["xt"].at(i))
                pe.wait_ge(*sig["w_proj3_in"].at(0))
                pe.wait_ge(*taken[0])
                pe.matmul(PS[:, 0, :], W3[:, 0, :], xT[:, i % 2, :], start=True, stop=True).then_inc(*sig["a3_psum"].mark((i, 0)))
                pe.wait_ge(*taken[1])
                pe.matmul(PS[:, 1, 0:KC], W3[:, 1, :], ctxT[:, b, :], start=True, stop=True)
                for j in range(2):
                    mm = pe.matmul(PS[0:KJ, 1, 256 + j * D:256 + (j + 1) * D], ctxT[:, b, j * KJ:(j + 1) * KJ], W3[:, 2, :], start=True, stop=True)
                mm.then_inc(*sig["a3_psum"].mark((i, 1)))
                taken[0] = sig["a3_q"].at(i)
                taken[1] = sig["a3_v"].at(i)

            def scores3(i):
                pe.wait_ge(*sig["a3_q"].at(i))
                pe.wait_ge(*sig["a3_k"].at(i))
                pe.wait_ge(*taken[2])
                pe.wait_ge(*taken[3])
                for t in range(T):
                    mm = pe.matmul(PS[:, 2 + t // 2, (t % 2) * KC:(t % 2 + 1) * KC], QT3[:, t * 128:(t + 1) * 128], KT3, start=True, stop=True)
                mm.then_inc(*sig["a3_s"].mark(i))
                taken[2] = taken[3] = sig["a3_p"].at((i, T - 1))

            def attention3_step(i, n):
                if n == 1:
                    pe.wait_ge(*sig["a3_p"].at((i, T - 1)))
                    pe.wait_ge(*taken[6])
                    pe.wait_ge(*taken[7])
                    for t in range(T):
                        for j in range(2):
                            mm = pe.transpose(PS[0:KJ, 6 + t // 2, (t % 2) * 256 + j * 128:(t % 2) * 256 + (j + 1) * 128],
                                              P3[:, t, j * KJ:(j + 1) * KJ], ident[:, :])
                    mm.then_inc(*sig["a3_ptp"].mark(i))
                    taken[6] = taken[7] = sig["a3_pt"].at(i)
                elif n == 3:
                    pe.wait_ge(*sig["a3_pt"].at(i))
                    pe.wait_ge(*taken[5])
                    for t in range(T):
                        for j in range(2):
                            lo = (t % 2) * 256 + j * 128
                            mm = pe.matmul(PS[:, 5, t * 128:(t + 1) * 128], PT3[:, t // 2, lo:lo + 128], V3[:, i % 2, j, :],
                                           start=(j == 0), stop=(j == 1))
                    mm.then_inc(*sig["a3_o"].mark(i))
                    taken[5] = sig["resid"].at(i)

            def ffn3(i):
                bank = 2 * (i % 2)
                pe.wait_ge(*taken[bank])
                pe.wait_ge(*taken[bank + 1])
                pe.wait_ge(*sig["w_ffn3_in"].at(0))
                for t in range(T):
                    mm = pe.matmul(PS[:, bank + t // 2, (t % 2) * 2 * D:(t % 2 + 1) * 2 * D], xT[:, i % 2, t * 128:(t + 1) * 128], WF3[:, 0:2 * D],
                                   start=True, stop=True)
                mm.then_inc(*sig["f3_psum"].mark(i))
                taken[bank] = taken[bank + 1] = sig["resid"].at(i)

            k_proj(0)
            xt(0)
            q_proj(0)
            pe.wait_ge(*sig["mem_ready"].at(0))
            for g in range(G):
                mm = pe.transpose(PS[0:KX_ROWS, 6, g * KM:(g + 1) * KM], MKX[:, g, 0:KX_ROWS], ident[0:KM, 0:KM])
            mm.then_inc(*sig["mem_kt_psum"].mark(0))
            taken[6] = sig["mem_kb"].at(0)
            k_transposes(0)
            xt(1)
            k_proj(1)
            for g in range(G):
                qxt(None, 0, g)
            q_proj(1)
            for m in range(N_MAX):
                scores_for_max(None, 0, m)
                if m == 8:
                    v_blocks(0, 0)
                if m == 20:
                    v_blocks(0, 1)
                if m == N_MAX - 5:
                    maxima_transposed(None, 0, 0)
            maxima_transposed(None, 0, 1)
            for i in range(len(ITEMS)):
                kind = ITEMS[i][0]
                total, pieces = all_slots(i)
                for n in range(total):
                    now = pieces.get(n, [])
                    first = [p for p in now if p[0] == "max" and kind in ("F1", "F2")][:1]
                    if first:
                        piece(i, first[0])
                        now = [p for p in now if p != first[0]]
                    if kind == "A":
                        attention_step(i, n)
                    elif kind in ("F0", "F1", "F2"):
                        ffn_step(i, n)
                    elif kind == "A3":
                        attention3_step(i, n)
                    elif n == 0:
                        ffn3(i)
                    for p in now:
                        piece(i, p)

        @block.vector
        def _(dve):
            def ln_stats(j, t):
                b = ITEMS[j][2]
                if t == 0:
                    if j < B:
                        dve.wait_ge(*sig[f"x_in{b}"].at(0))
                    else:
                        dve.wait_ge(*sig["resid"].at(j - B))
                    if j >= 2:
                        dve.wait_ge(*sig["xn"].at(j - 2))
                dve.bn_stats(st6[:, j % 2, t, :], x[:, b * T + t, :]).then_inc(*sig["ln_stats"].mark((j, t)))
                dve.wait_ge(*sig["ln_stats"].at((j, t)))
                dve.bn_aggr(mvar[:, j % 2, t, :], st6[:, j % 2, t, :]).then_inc(*sig["ln_aggr"].mark((j, t)))

            def k_bias(a):
                layer = a // B
                dve.wait_ge(*sig["k_psum"].at(a))
                if a >= 1:
                    dve.wait_ge(*sig["kx_l"].at(a - 1))
                    dve.wait_ge(*sig["kx_h"].at(a - 1))
                dve.tensor_tensor(k[:, :].rearrange("p (j n) -> p j n", j=2), PS[0:KJ, 5, 0:2 * D].rearrange("p (j n) -> p j n", j=2),
                                  BK[:, layer % 2, None, :].to_broadcast([KJ, 2, D]), ALU.add).then_inc(*sig["k"].mark(a))

            def k_mean_square(a):
                if a // B == 1:
                    dve.wait_ge(*sig["k_sq"].at(a))
                    dve.tensor_reduce(kms[:, :], ka[:, :].rearrange("p (h d) -> p h d", d=HD), AX.X, ALU.add).then_inc(*sig["k_ms"].mark(a))
                    root_seed(kms[:, :], krr[:, :], sig["k_ms"], sig["k_var"], sig["k_seed"], a)

            def v_mask(a, part):
                layer = a // B
                rows, chunks = chunk_shape(layer)
                mask = MV0 if layer == 0 else MV1
                c0, c1 = 4 * part, min(4 * part + 4, chunks)
                dve.wait_ge(*sig["v_psum"].at((a, part)))
                if a >= 2 and part == 0:
                    dve.wait_ge(*sig["pv"].at((item_of(a - 2), n_slots(item_of(a - 2)) - 1)))
                if a == B and part == 0:
                    dve.wait_ge(*sig["wA_in1"].at(0))
                dve.tensor_tensor(VB[0:rows, a % 2, c0:c1, :].rearrange("p c (g n) -> p c g n", g=G),
                                  PS[0:rows, 4 + part, 0:(c1 - c0) * D].rearrange("p (c g n) -> p c g n", g=G, n=HL * HD),
                                  mask[0:rows, c0:c1, None, :].to_broadcast([rows, c1 - c0, G, HL * HD]), ALU.mult).then_inc(*sig["vb"].mark((a, part)))

            def q_bias(a):
                layer = a // B
                dve.wait_ge(*sig["q_psum"].at(a))
                if a >= 1:
                    dve.wait_ge(*sig["qx_l"].at(a - 1))
                    dve.wait_ge(*sig["qx_h"].at(a - 1))
                dve.tensor_tensor(q[:, :].rearrange("p (t n) -> p t n", t=T), PS[:, 4, :].rearrange("p (t n) -> p t n", t=T),
                                  BQ[:, layer % 2, None, :].to_broadcast([128, T, D]), ALU.add).then_inc(*sig["q"].mark(a))

            def q_mean_square(a):
                layer = a // B
                if layer == 1:
                    dve.wait_ge(*sig["q_sq"].at(a))
                    dve.tensor_reduce(qms[:, :], qa[:, :].rearrange("p (h d) -> p h d", d=HD), AX.X, ALU.add).then_inc(*sig["q_ms"].mark(a))
                    root_seed(qms[:, :], qrr[:, :], sig["q_ms"], sig["q_var"], sig["q_seed"], a)
                if layer == 2:
                    qv = q[:, :].rearrange("p (t h i s) -> p t h i s", t=T, h=H, s=2)
                    bv = qb[:, :].rearrange("p (t h i s) -> p t h i s", t=T, h=H, s=2)
                    dve.wait_ge(*sig["q"].at(a))
                    for s, (lo, hi) in enumerate(((8, 12), (12, 16))):
                        dve.tensor_tensor(bv[:, :, :, :, s], qv[:, :, :, :, 1 - s],
                                          ropeq[:, :, None, lo:hi].to_broadcast([128, T, H, 4]), ALU.mult).then_inc(*sig["q_t2"].mark((a, s)))

            def q_finish(a):
                layer = a // B
                if layer == 1:
                    dve.wait_ge(*sig["q_rr"].at((a, 2, 3)))
                    dve.wait_ge(*sig["q"].at(a))
                    dve.tensor_tensor(qb[:, :].rearrange("p (h d) -> p h d", d=HD), q[:, :].rearrange("p (h d) -> p h d", d=HD),
                                      qrr[:, :, None].to_broadcast([128, T * H, HD]), ALU.mult).then_inc(*sig["q_ready"].mark(a))
                if layer == 2:
                    dve.wait_ge(*sig["q_t1"].at(a))
                    dve.wait_ge(*sig["q_t2"].at((a, 1)))
                    dve.tensor_tensor(q[:, :], qa[:, :], qb[:, :], ALU.add).then_inc(*sig["q_ready"].mark(a))

            def maxima(i_main, a, m):
                g, f, t, layer = m // (2 * T), m // T % 2, m % T, a // B
                dve.wait_ge(*sig["mx_psum"].at((a, m)))
                if m == 0 and a >= 2:
                    dve.wait_ge(*sig["mt_psum"].at((a - 2, 1)))
                h0 = g * HL + 2 * f
                dve.tensor_reduce(mneg[:, a % 2, t, h0:h0 + 2],
                                  PS[:, mx_bank(i_main, m), 0:2 * (KT0 if layer == 0 else KC)].rearrange("p (h n) -> p h n", h=2),
                                  AX.X, ALU.max, negate=True).then_inc(*sig["mx"].mark((a, m)))

            def x_low(j):
                if ITEMS[j][0] in ("F0", "F1", "F2"):
                    dve.wait_ge(*sig["xh"].at(j))
                    if ITEMS[j][2] >= 2:
                        dve.wait_ge(*sig["y"].at((j - 2, ffn_tiles(ITEMS[j][0])[-1][0])))
                    dve.tensor_tensor(xL[:, j % 2, :], xT[:, j % 2, :], xH[:, j % 2, :], ALU.subtract).then_inc(*sig["xl"].mark(j))

            def gating(i, n, psum_view, bias, part):
                g8 = gates[:, i % 2, :, 0:n]
                l = lg[:, :, 0:n]
                if part == 0:
                    if bias is not None:
                        dve.tensor_tensor(l, psum_view, bias[:, None, :].to_broadcast([128, T, n]), ALU.add).then_inc(*sig["lg"].mark(i))
                    else:
                        dve.tensor_copy(l, psum_view).then_inc(*sig["lg"].mark(i))
                    dve.wait_ge(*sig["lg"].at(i))
                    dve.tensor_reduce(lsm[:, 0, :], l, AX.X, ALU.max, negate=True).then_inc(*sig["lg_nm"].mark(i))
                    lj = lg[:, :, None, 0:n].to_broadcast([128, T, n, n])
                    li = lg[:, :, 0:n, None].to_broadcast([128, T, n, n])
                    dve.tensor_tensor(lga[:, :, 0:n, 0:n], lj, li, ALU.is_gt).then_inc(*sig["lg_c"].mark((i, 0)))
                    dve.wait_ge(*sig["lg_nm"].at(i))
                    dve.tensor_tensor(lsh[:, :, 0:n], l, lsm[:, 0, :, None].to_broadcast([128, T, n]), ALU.add).then_inc(*sig["lg_sh"].mark(i))
                    dve.tensor_tensor(lgb[:, :, 0:n, 0:n], lj, li, ALU.is_equal).then_inc(*sig["lg_c"].mark((i, 1)))
                elif part == 1:
                    dve.wait_ge(*sig["lg_c"].at((i, 1)))
                    dve.tensor_tensor(lgb[:, :, 0:n, 0:n], lgb[:, :, 0:n, 0:n], LT[:, None, 0:n, 0:n].to_broadcast([128, T, n, n]), ALU.mult).then_inc(*sig["lg_c"].mark((i, 2)))
                    dve.wait_ge(*sig["lg_c"].at((i, 2)))
                    dve.tensor_tensor(lga[:, :, 0:n, 0:n], lga[:, :, 0:n, 0:n], lgb[:, :, 0:n, 0:n], ALU.add).then_inc(*sig["lg_c"].mark((i, 3)))
                    dve.wait_ge(*sig["lg_c"].at((i, 3)))
                    dve.tensor_reduce(lsh2(n), lga[:, :, 0:n, 0:n], AX.X, ALU.add).then_inc(*sig["lg_c"].mark((i, 4)))
                else:
                    dve.wait_ge(*sig["lg_c"].at((i, 4)))
                    dve.wait_ge(*sig["lg_e"].at(i))
                    dve.scalar_tensor_tensor(lsh2(n), lsh2(n), 2.0, le[:, :, 0:n], ALU.is_lt, ALU.mult).then_inc(*sig["lg_es"].mark(i))
                    dve.wait_ge(*sig["lg_es"].at(i))
                    dve.tensor_reduce(lsm[:, 1, :], lsh2(n), AX.X, ALU.add).then_inc(*sig["lg_sum"].mark(i))
                    dve.wait_ge(*sig["lg_sum"].at(i))
                    dve.reciprocal(lsm[:, 2, :], lsm[:, 1, :]).then_inc(*sig["lg_r"].mark(i))
                    dve.wait_ge(*sig["lg_r"].at(i))
                    dve.tensor_tensor(g8, lsh2(n), lsm[:, 2, :, None].to_broadcast([128, T, n]), ALU.mult).then_inc(*sig["gates"].mark(i))

            def lsh2(n):
                return lgb[:, :, 0, 0:n]

            def router(j, part):
                kind, _, b = ITEMS[j]
                n = {"F1": E1, "F2": E2, "F3": E3}[kind]
                if part == 0:
                    dve.wait_ge(*sig["lg_psum"].at(j))
                    if b == 0:
                        dve.wait_ge(*sig["w3_in"].at(0))
                    if b >= 1:
                        dve.wait_ge(*sig["gates"].at(j - 1))
                if part == 2 and b >= 2:
                    dve.wait_ge(*sig["resid"].at(j - 2))
                gating(j, n, PS[:, 5, 0:T * n].rearrange("p (t n) -> p t n", t=T), RB1 if kind == "F1" else None, part)

            def lora(j):
                b = ITEMS[j][2]
                if b == 0:
                    dve.wait_ge(*sig["w_ffn0_in"].at(0))
                dve.wait_ge(*sig["lora_psum"].at((j, 0)))
                if b >= 2:
                    dve.wait_ge(*sig["y"].at((j - 2, 0)))
                if b >= 1:
                    dve.wait_ge(*sig["lora_l"].at(j - 1))
                    dve.wait_ge(*sig["lora_h"].at(j - 1))
                dve.scalar_tensor_tensor(qa[:, :], PS[:, 5, :], scale0[:, :], W1T, ALU.mult, ALU.add).then_inc(*sig["lora_w"].mark((j, 0)))
                dve.wait_ge(*sig["lora_psum"].at((j, 1)))
                dve.scalar_tensor_tensor(W2E[:, b % 2, :], PS[:, 5, :], scale0[:, :], W2T, ALU.mult, ALU.add).then_inc(*sig["lora_w"].mark((j, 1)))
                dve.wait_ge(*sig["lora_h"].at(j))
                dve.tensor_tensor(W1E[:, b % 2, 1, :], qa[:, :], W1E[:, b % 2, 0, :], ALU.subtract).then_inc(*sig["lora_l"].mark(j))

            def piece(i, p):
                name = p[0]
                if name == "ln":
                    ln_stats(p[1], p[2])
                elif name == "kproj":
                    k_bias(p[1])
                elif name == "k2":
                    k_mean_square(p[1])
                elif name == "v":
                    v_mask(p[1], p[2])
                elif name == "q":
                    q_bias(p[1])
                elif name == "q2":
                    q_mean_square(p[1])
                elif name == "q4":
                    q_finish(p[1])
                elif name == "max":
                    maxima(i, p[1], p[2])
                elif name == "after_xt":
                    x_low(p[1])
                elif name == "late":
                    if ITEMS[p[1]][0] != "F0":
                        router(p[1], p[2])
                    elif p[2] == 0:
                        lora(p[1])
                elif name == "finish":
                    attention_out(p[1])
                elif name == "proj3":
                    projections3(p[1])
                elif name == "scores3":
                    maxima3(p[1])

            def attention_end(i):
                dve.wait_ge(*sig["dn_out"].at(i))
                dve.reciprocal(RD, RD).then_inc(*sig["rden"].mark(i))
                dve.wait_ge(*sig["rden"].at(i))
                dve.wait_ge(*sig["pv_out"].at(i))
                dve.tensor_tensor(ON, ON, RD, ALU.mult).then_inc(*sig["on"].mark(i))

            def attention_out(i):
                b = ITEMS[i][2]
                dve.wait_ge(*sig["o_psum"].at(i))
                dve.wait_ge(*sig["bias_in_x"].at(i))
                xb = x[:, b * T:(b + 1) * T, :]
                dve.tensor_tensor(xb, PS[:, 5, :].rearrange("p (t n) -> p t n", t=T), xb, ALU.add).then_inc(*sig["resid"].mark(i))

            def ffn_step(i, n):
                kind, layer, b = ITEMS[i]
                tiles = ffn_tiles(kind)
                if n < len(tiles) and kind != "F0":
                    e, col, rows, slot = tiles[n]
                    j = n - min(m for m, tl in enumerate(tiles) if tl[0] == e)
                    dve.wait_ge(*sig["act"].at((i, n)))
                    dve.wait_ge(*sig["up"].at((i, n, 1)))
                    if j == 0:
                        if e >= 2:
                            dve.wait_ge(*sig["y"].at((i, e - 2)))
                        elif b > 0:
                            dve.wait_ge(*sig["y"].at((i - 1, last_of_parity(kind, e % 2))))
                        else:
                            dve.wait_ge(*sig["o_psum" if e else "dn"].at(i - 1 if e else (i - 1, n_slots(i - 1) - 1)))
                    dve.tensor_tensor(HH[0:rows, e % 2, j, :], PS[0:rows, 2 * (n % 2) + 1, :], SS[0:rows, n % 2, :], ALU.mult).then_inc(*sig["h"].mark((i, n)))
                if n < 4 and carries_on(i - 1):
                    accumulations(i - 1, n + len(tiles))
                if n < len(tiles) or not carries_on(i):
                    accumulations(i, n)

            def accumulations(i, n):
                tiles = ffn_tiles(ITEMS[i][0])
                for e in range(tiles[-1][0] + 1):
                    last = max(m for m, tl in enumerate(tiles) if tl[0] == e)
                    if n == last + 3:
                        accumulate(i, e)

            def accumulate(i, e):
                kind, layer, b = ITEMS[i]
                bank = 6 + (b if kind == "F0" else e) % 2
                dve.wait_ge(*sig["y"].at((i, e)))
                if e == 0:
                    dve.wait_ge(*sig["xn"].at(i))
                    if kind == "F0":
                        dve.wait_ge(*sig["bias_in_x"].at(i))
                    else:
                        dve.wait_ge(*sig["gates"].at(i))
                else:
                    dve.wait_ge(*sig["acc"].at((i, e - 1)))
                if kind == "F0" or e == E2:
                    xb = x[:, b * T:(b + 1) * T, :]
                    ins = dve.tensor_tensor(xb, PS[:, bank, :].rearrange("p (t n) -> p t n", t=T), xb, ALU.add)
                else:
                    for t in range(T):
                        xt_ = x[:, b * T + t, :]
                        ins = dve.scalar_tensor_tensor(xt_, PS[:, bank, t * 128:(t + 1) * 128], gates[:, i % 2, t, e:e + 1], xt_, ALU.mult, ALU.add)
                if e == last_expert(kind):
                    ins.then_inc(*sig["resid"].mark(i))
                else:
                    ins.then_inc(*sig["acc"].mark((i, e)))

            def projections3(i):
                dve.wait_ge(*sig["a3_psum"].at((i, 1)))
                dve.wait_ge(*sig["w_proj3_in"].at(0))
                if ITEMS[i][2] == 0:
                    dve.wait_ge(*sig["resid"].at(i - 1))
                else:
                    dve.wait_ge(*sig["a3_s"].at(i - 1))
                if ITEMS[i][2] >= 2:
                    dve.wait_ge(*sig["a3_o"].at(i - 2))
                dve.tensor_scalar(KT3, PS[:, 1, 0:KC], bqk3[:, 1:2], None, ALU.add).then_inc(*sig["a3_k"].mark(i))
                dve.tensor_tensor(V3[:, i % 2, :, :], PS[0:KJ, 1, 256:512].rearrange("p (j n) -> p j n", j=2), BV3[:, None, :].to_broadcast([KJ, 2, D]),
                                  ALU.add).then_inc(*sig["a3_v"].mark(i))

            def maxima3(i):
                dve.wait_ge(*sig["a3_s"].at(i))
                if ITEMS[i][2] >= 1:
                    dve.wait_ge(*sig["a3_p"].at((i - 1, T - 1)))
                dve.tensor_reduce(a3s[:, 0, :].rearrange("p (f h) -> p f h", f=2), PS[:, 2:4, 0:2 * KC].rearrange("p f (h n) -> p f h n", h=2), AX.X, ALU.max, negate=True).then_inc(*sig["a3_nm"].mark(i))
                dve.wait_ge(*sig["a3_nm"].at(i))
                dve.tensor_scalar(a3s[:, 1, :], a3s[:, 0, :], SCALE3, None, ALU.mult).then_inc(*sig["a3_nms"].mark(i))

            def attention3_step(i, n):
                b = ITEMS[i][2]
                if n == 1:
                    dve.wait_ge(*sig["a3_p"].at((i, T - 1)))
                    dve.reciprocal(a3s[:, 3, :], a3s[:, 2, :]).then_inc(*sig["a3_r"].mark(i))
                elif n == 3:
                    dve.wait_ge(*sig["a3_r"].at(i))
                    dve.wait_ge(*sig["a3_o"].at(i))
                    dve.wait_ge(*sig["xn"].at(i))
                    for t in range(T):
                        xt_ = x[:, b * T + t, :]
                        ins = dve.scalar_tensor_tensor(xt_, PS[:, 5, t * 128:(t + 1) * 128], a3s[:, 3, t:t + 1], xt_, ALU.mult, ALU.add)
                    ins.then_inc(*sig["resid"].mark(i))

            def ffn3(i):
                b, bank = ITEMS[i][2], 2 * (i % 2)
                dve.wait_ge(*sig["gates"].at(i))
                dve.tensor_reduce(gsum[:, i % 2, :], gates[:, i % 2, :, 0:E3], AX.X, ALU.add).then_inc(*sig["f3_y"].mark((i, 0)))
                dve.wait_ge(*sig["f3_psum"].at(i))
                dve.wait_ge(*sig["f3_y"].at((i, 0)))
                dve.wait_ge(*sig["bias_in_x"].at(i))
                for t in range(T):
                    xt_ = x[:, b * T + t, :]
                    ins = dve.scalar_tensor_tensor(xt_, PS[:, bank + t // 2, (t % 2) * 2 * D:(t % 2) * 2 * D + D], gsum[:, i % 2, t:t + 1], xt_, ALU.mult, ALU.add)
                ins.then_inc(*sig["f3_y"].mark((i, 1)))
                dve.wait_ge(*sig["f3_y"].at((i, 1)))
                xb = x[:, b * T:(b + 1) * T, :].rearrange("p (f h) n -> p f h n", f=2)
                dve.tensor_tensor(xb, PS[:, bank:bank + 2, :].rearrange("p f (h n) -> p f h n", h=2)[:, :, :, D:2 * D], xb, ALU.add).then_inc(*sig["resid"].mark(i))

            for t in range(T):
                ln_stats(0, t)
            k_bias(0)
            dve.wait_ge(*sig["mask_in"].at(0))
            dve.memset(KEEP[:, :, :, :], 1.0).then_inc(*sig["init_dve"].mark(0))
            dve.memset(KBIAS[:, :, :, :], 0.0).then_inc(*sig["init_dve"].mark(1))
            dve.wait_ge(*sig["init_dve"].at(1))
            dve.tensor_copy(KEEP[:, 0, :, :], mraw0[:, :, :]).then_inc(*sig["init_dve"].mark(2))
            dve.tensor_copy(KEEP[:, 2, :, :], mraw2[:, :, :]).then_inc(*sig["init_dve"].mark(3))
            dve.wait_ge(*sig["init_dve"].at(3))
            dve.tensor_scalar(KEEP[:, :, :, :], KEEP[:, :, :, :], 0.0, None, ALU.not_equal).then_inc(*sig["init_dve"].mark(4))
            dve.wait_ge(*sig["init_dve"].at(4))
            dve.tensor_scalar(KBIAS[:, :, :, :], KEEP[:, :, :, :], BIG, -BIG, ALU.mult, ALU.add).then_inc(*sig["mask_ready"].mark(0))
            dve.wait_ge(*sig["const_in"].at(0))
            for r_ in range(2):
                shift_rows(dve, 0, r_)
            q_bias(0)
            for t in range(T):
                ln_stats(1, t)
            k_bias(1)
            q_bias(1)
            for m in range(N_MAX):
                maxima(None, 0, m)
                if m == 13:
                    v_mask(0, 0)
                if m == 25:
                    v_mask(0, 1)
            for i in range(len(ITEMS)):
                kind = ITEMS[i][0]
                total, pieces = all_slots(i)
                for n in range(total):
                    now = pieces.get(n, [])
                    if kind in ("F1", "F2"):
                        for p in [p for p in now if p[0] == "max"]:
                            piece(i, p)
                        now = [p for p in now if p[0] != "max"]
                    if kind in ("F0", "F1", "F2"):
                        ffn_step(i, n)
                    elif kind == "A3":
                        attention3_step(i, n)
                    elif kind == "F3" and n == 0:
                        ffn3(i)
                    for p in now:
                        piece(i, p)
                    if kind == "A" and n == n_slots(i) + 3:
                        attention_end(i)

        @block.scalar
        def _(act):
            def k_split(a):
                layer = a // B
                act.wait_ge(*sig["k_ready"].at(a))
                if a >= 2:
                    act.wait_ge(*sig["kt_psum"].at(a - 2))
                kx = KX[:, a % 2, :, :, 0:PR].rearrange("p j g (h s d) -> p (j g) h s d", h=HL, s=3).bitcast(F32R)
                src = k[:, :].rearrange("p (m h d) -> p m h d", h=HL, d=HD)
                for s in range(2):
                    act.activation(kx[:, :, :, s, :], src, ACT.Copy).then_inc(*sig["kx_h"].more(a))

            def kb_out(a, h):
                layer = a // B
                act.wait_ge(*sig["kt_psum"].at(a))
                if h == 0:
                    act.wait_ge(*shift_signal(layer).at((layer > 0, a % 2)))
                    if a >= 2:
                        act.wait_ge(*sig["st"].at((item_of(a - 2), n_slots(item_of(a - 2)) - 1)))
                act.activation(key_columns(layer, a % 2)[0:KX_ROWS, :, h, :].rearrange("p (f g) n -> p f g n", f=2),
                               PS[0:KX_ROWS, 4:6, 0:2 * KC].rearrange("p f (g n) -> p f g n", g=2), ACT.Copy,
                               scale=maskk[0:KX_ROWS, h:h + 1]).then_inc(*sig["kb"].mark((a, h)))

            def xt_out(j):
                act.wait_ge(*sig["xt_psum"].at(j))
                if j >= 2:
                    kind = ITEMS[j - 2][0]
                    if kind == "A":
                        act.wait_ge(*sig["q_psum"].at(ITEMS[j - 2][1] * B + ITEMS[j - 2][2]))
                    elif kind in ("F1", "F2", "F3"):
                        act.wait_ge(*sig["lg_psum"].at(j - 2))
                    if kind in ("F0", "F1", "F2"):
                        act.wait_ge(*sig["xl"].at(j - 2))
                    if kind == "A3":
                        act.wait_ge(*sig["a3_psum"].at((j - 2, 0)))
                    if kind == "F3":
                        act.wait_ge(*sig["f3_psum"].at(j - 2))
                act.activation(xT[:, j % 2, :], PS[:, 4, :], ACT.Copy).then_inc(*sig["xt"].mark(j))

            def x_high(j):
                if ITEMS[j][0] in ("F0", "F1", "F2"):
                    act.wait_ge(*sig["xt"].at(j))
                    if ITEMS[j][2] >= 2:
                        act.wait_ge(*sig["y"].at((j - 2, ffn_tiles(ITEMS[j][0])[-1][0])))
                    act.activation(xH[:, j % 2, :], xT[:, j % 2, :], ACT.Copy).then_inc(*sig["xh"].mark(j))

            def q_split(a):
                layer = a // B
                if layer == 0:
                    act.wait_ge(*sig["q"].at(a))
                else:
                    act.wait_ge(*sig["q_ready"].at(a))
                if a >= 1:
                    act.wait_ge(*sig["qxt_psum"].at((a - 1, G - 1)))
                else:
                    act.wait_ge(*sig["init_pool"].at(0))
                src = (qb if layer == 1 else q)[:, :].rearrange("p (m h d) -> p m h d", h=HL, d=HD)
                qx = QX[:, :, :, 0:PR].rearrange("p t g (h s d) -> p (t g) h s d", h=HL, s=3).bitcast(F32R)
                for s in (0, 2):
                    act.activation(qx[:, :, :, s, :], src, ACT.Copy).then_inc(*sig["qx_h"].more(a))

            def qxt_out(i_main, a, g):
                act.wait_ge(*sig["qxt_psum"].at((a, g)))
                if a >= 2 and g == 0:
                    act.wait_ge(*sig["st"].at((item_of(a - 2), n_slots(item_of(a - 2)) - 1)))
                act.activation(QXT[0:KX_ROWS, a % 2, g, :], PS[0:KX_ROWS, qxt_bank(i_main, g), :], ACT.Copy).then_inc(*sig["qxt"].mark((a, g)))

            def mt_out(i_main, a, part):
                heads = mt_heads(part)
                act.wait_ge(*sig["mt_psum"].at((a, part)))
                if a >= 1:
                    act.wait_ge(*sig[f"shift_in{part}"].at(a - 1))
                act.activation(mT[0:heads.stop - heads.start, part, :], PS[0:heads.stop - heads.start, mt_bank(i_main, part), :],
                               ACT.Copy).then_inc(*sig["mt"].mark((a, part)))

            def w_high(layer, c):
                which, lo, w = weight_chunks(layer)[c]
                serial = c + (8 if layer == 2 else 0)
                act.wait_ge(*sig[f"stage_in{serial % 2}"].at(serial))
                act.activation(UP(layer)[:, which, 0, lo:lo + w], stage[:, serial % 2, 0:w], ACT.Copy).then_inc(*sig["w_h"].mark(serial))

            def gate_exp(i, n):
                act.wait_ge(*sig["lg_sh"].at(i))
                act.activation(le[:, :, 0:n], lsh[:, :, 0:n], ACT.Exp).then_inc(*sig["lg_e"].mark(i))

            def piece(i, p):
                name = p[0]
                if name == "ksplit":
                    k_split(p[1])
                elif name == "kb":
                    kb_out(p[1], p[2])
                elif name == "xt":
                    xt_out(p[1])
                elif name == "after_xt":
                    x_high(p[1])
                elif name == "qsplit":
                    q_split(p[1])
                elif name == "qxt":
                    qxt_out(i, p[1], p[2])
                elif name == "mt":
                    mt_out(i, p[1], p[2])
                elif name == "proj3":
                    projections3(p[1])
                elif name == "scores3":
                    exps3(p[1])
                elif name == "w":
                    w_high(p[1], p[2])
                elif name == "late" and p[2] == 0:
                    kind = ITEMS[p[1]][0]
                    if kind != "F0":
                        gate_exp(p[1], {"F1": E1, "F2": E2, "F3": E3}[kind])
                    else:
                        j = p[1]
                        act.wait_ge(*sig["lora_w"].at((j, 0)))
                        if ITEMS[j][2] >= 2:
                            act.wait_ge(*sig["y"].at((j - 2, 0)))
                        act.activation(W1E[:, ITEMS[j][2] % 2, 0, :], qa[:, :], ACT.Copy).then_inc(*sig["lora_h"].mark(j))

            def attention_end(i, n):
                N = n_slots(i)
                if n == N + 1:
                    act.wait_ge(*sig["pv"].at((i, N - 1)))
                    if i > 0 and is_attn(i - 1):
                        act.wait_ge(*sig["o_psum"].at(i - 1))
                    elif i > 0:
                        act.wait_ge(*sig["resid"].at(i - 1))
                    act.activation(ON, PS[:, 6, :], ACT.Copy).then_inc(*sig["pv_out"].mark(i))
                elif n == N + 3:
                    act.wait_ge(*sig["dn"].at((i, N - 1)))
                    if i > 0 and is_attn(i - 1):
                        act.wait_ge(*sig["on"].at(i - 1))
                    act.activation(RD, PS[:, 7, :], ACT.Copy).then_inc(*sig["dn_out"].mark(i))

            def exps(i, n):
                _, layer, b = ITEMS[i]
                rows, _ = chunk_shape(layer)
                act.wait_ge(*sig["st"].at((i, n)))
                if n >= 6:
                    act.wait_ge(*sig["dn"].at((i, n - 6)))
                elif n == 0 and i > 0:
                    act.wait_ge(*(sig["dn"].at((i - 1, n_slots(i - 1) - 1)) if b > 0 else sig["resid"].at(i - 1)))
                act.activation(P[0:rows, n % 6, :], PS[0:rows, n % 2, :], ACT.Exp, scale=SCALE).then_inc(*sig["p"].mark((i, n)))

            def ffn_step(i, n):
                kind, layer, b = ITEMS[i]
                e, col, rows, slot = ffn_tiles(kind)[n]
                bank = 2 * (n % 2)
                act.wait_ge(*sig["up"].at((i, n, 0)))
                if kind == "F0":
                    if n == 0:
                        act.wait_ge(*sig["w_ffn0_in"].at(0))
                        if b == 0:
                            act.wait_ge(*sig["dn"].at((i - 1, n_slots(i - 1) - 1)))
                        elif b == 1:
                            act.wait_ge(*sig["o_psum"].at(i - 2))
                        else:
                            act.wait_ge(*sig["y"].at((i - 2, 0)))
                    act.activation(HH[0:rows, b % 2, n, :], PS[0:rows, bank, :], ACT.Gelu, bias=b1T[:, n:n + 1]).then_inc(*sig["h_gelu"].mark((i, n)))
                else:
                    if n >= 2:
                        act.wait_ge(*sig["h"].at((i, n - 2)))
                    elif b > 0:
                        act.wait_ge(*sig["h"].at((i - 1, n_slots(i) - 2 + n)))
                    act.activation(SS[0:rows, n % 2, :], PS[0:rows, bank, :], ACT.Silu).then_inc(*sig["act"].mark((i, n)))

            def projections3(i):
                act.wait_ge(*sig["a3_psum"].at((i, 0)))
                if ITEMS[i][2] == 0:
                    act.wait_ge(*sig["w3_in"].at(0))
                    act.wait_ge(*sig["resid"].at(i - 1))
                else:
                    act.wait_ge(*sig["a3_s"].at(i - 1))
                act.activation(QT3, PS[:, 0, :], ACT.Identity, bias=bqk3[:, 0:1]).then_inc(*sig["a3_q"].mark(i))

            def exps3(i):
                act.wait_ge(*sig["a3_nms"].at(i))
                if ITEMS[i][2] >= 1:
                    act.wait_ge(*sig["a3_ptp"].at(i - 1))
                    act.wait_ge(*sig["a3_r"].at(i - 1))
                for t in range(T):
                    act.activation(P3[:, t, :], PS[:, 2 + t // 2, (t % 2) * KC:(t % 2 + 1) * KC], ACT.Exp, bias=a3s[:, 1, t:t + 1],
                                   scale=SCALE3, accum_out=a3s[:, 2, t:t + 1]).then_inc(*sig["a3_p"].mark((i, t)))

            def attention3_step(i, n):
                if n == 1:
                    act.wait_ge(*sig["a3_ptp"].at(i))
                    if ITEMS[i][2] >= 1:
                        act.wait_ge(*sig["a3_o"].at(i - 1))
                    act.activation(PT3, PS[0:KJ, 6:8, :], ACT.Copy).then_inc(*sig["a3_pt"].mark(i))

            xt_out(0)
            k_split(0)
            q_split(0)
            for h in range(HL):
                kb_out(0, h)
            act.wait_ge(*sig["mem_kt_psum"].at(0))
            for r_ in range(2):
                mem_cols = KB0[:, r_, :, 0:HL * KT0].rearrange("p g (h n) -> p g h n", h=HL)[:, :, :, KC:KT0]
                for h in range(HL):
                    act.activation(mem_cols[0:KX_ROWS, :, h, :], PS[0:KX_ROWS, 6, 0:G * KM].rearrange("p (g n) -> p g n", g=G), ACT.Copy,
                                   scale=maskk[0:KX_ROWS, h:h + 1]).then_inc(*sig["mem_kb"].more(0))
            xt_out(1)
            for g in range(G):
                qxt_out(None, 0, g)
            k_split(1)
            q_split(1)
            mt_out(None, 0, 0)
            mt_out(None, 0, 1)
            for i in range(len(ITEMS)):
                kind = ITEMS[i][0]
                total, pieces = all_slots(i)
                for n in range(total):
                    if kind == "A" and n < n_slots(i):
                        exps(i, n)
                    elif kind == "A":
                        attention_end(i, n)
                    elif kind in ("F0", "F1", "F2") and n < n_slots(i):
                        ffn_step(i, n)
                    elif kind == "A3":
                        attention3_step(i, n)
                    for p in pieces.get(n, []):
                        piece(i, p)

        @block.gpsimd
        def _(pool):
            def layer_norm(j):
                b = ITEMS[j][2]
                pool.wait_ge(*sig["ln_aggr"].at((j, T - 1)))
                if j >= 2:
                    pool.wait_ge(*sig["xt_psum"].at(j - 2))
                    if ITEMS[j - 2][0] == "F0":
                        pool.wait_ge(*sig["lora_in"].at(j - 2))
                pool.tensor_scalar(rstd[:, j % 2, :], mvar[:, j % 2, :, 1], LN_EPS, None, ALU.add).then_inc(*sig["ln_var"].mark(j))
                pool.wait_ge(*sig["ln_var"].at(j))
                pool.tensor_tensor(rstd[:, j % 2, :], rstd[:, j % 2, :], half[:, 0:T], ALU.pow).then_inc(*sig["ln_rstd"].mark(j))
                pool.wait_ge(*sig["ln_rstd"].at(j))
                pool.tensor_tensor(xn[:, j % 2, :, :], x[:, b * T:(b + 1) * T, :], mvar[:, j % 2, :, 0:1].to_broadcast([128, T, D]),
                                   ALU.subtract).then_inc(*sig["x_centred"].mark(j))
                pool.wait_ge(*sig["x_centred"].at(j))
                pool.tensor_tensor(xn[:, j % 2, :, :], xn[:, j % 2, :, :], rstd[:, j % 2, :, None].to_broadcast([128, T, D]),
                                   ALU.mult).then_inc(*sig["xn"].mark(j))
                slot = bias_slot(j)
                if slot is not None:
                    if slot < 3:
                        pool.wait_ge(*sig[f"wA_in{slot}"].at(0))
                    else:
                        pool.wait_ge(*sig["w_ffn0_in" if slot == 3 else "w3_in"].at(0))
                    pool.wait_ge(*sig["xn"].at(j))
                    xb = x[:, b * T:(b + 1) * T, :]
                    pool.tensor_tensor(xb, xb, BO[:, slot, None, :].to_broadcast([128, T, D]), ALU.add).then_inc(*sig["bias_in_x"].mark(j))

            def k_square(a):
                layer = a // B
                if layer == 1:
                    pool.wait_ge(*sig["k"].at(a))
                    pool.tensor_tensor(ka[:, :], k[:, :], k[:, :], ALU.mult).then_inc(*sig["k_sq"].mark(a))

            def k_finish(a):
                layer, b = a // B, a % B
                pool.wait_ge(*sig["k"].at(a))
                if layer == 1:
                    root_newton(kms[:, :], krr[:, :], ktmp[:, :], sig["k_seed"], sig["k_rr"], a)
                    kv = k[:, :].rearrange("p (h d) -> p h d", d=HD)
                    pool.tensor_tensor(kv, kv, krr[:, :, None].to_broadcast([KJ, 2 * H, HD]), ALU.mult).then_inc(*sig["k_n"].mark(a))
                    pool.wait_ge(*sig["k_n"].at(a))
                    pool.wait_ge(*sig["gkq_ready"].at(0))
                    pool.tensor_tensor(kv, kv, gq[:, 0, None, :].to_broadcast([KJ, 2 * H, HD]), ALU.mult).then_inc(*sig["k_ready"].mark(a))
                if layer == 2:
                    kv = k[:, :].rearrange("p (j h d) -> p j h d", j=2, d=HD)
                    kp = k[:, :].rearrange("p (j h i s) -> p j h i s", j=2, h=H, s=2)
                    bp = kb[:, :].rearrange("p (j h i s) -> p j h i s", j=2, h=H, s=2)
                    pool.tensor_tensor(ka[:, :].rearrange("p (j h d) -> p j h d", j=2, d=HD), kv,
                                       ropek[:, :, None, 0:8].to_broadcast([KJ, 2, H, HD]), ALU.mult).then_inc(*sig["k_t1"].mark(a))
                    for s, (lo, hi) in enumerate(((8, 12), (12, 16))):
                        pool.tensor_tensor(bp[:, :, :, :, s], kp[:, :, :, :, 1 - s],
                                           ropek[:, :, None, lo:hi].to_broadcast([KJ, 2, H, 4]), ALU.mult).then_inc(*sig["k_t2"].mark((a, s)))
                    pool.wait_ge(*sig["k_t1"].at(a))
                    pool.wait_ge(*sig["k_t2"].at((a, 1)))
                    pool.tensor_tensor(k[:, :], ka[:, :], kb[:, :], ALU.add).then_inc(*sig["k_n"].mark(a))
                    pool.wait_ge(*sig["k_n"].at(a))
                if layer != 1:
                    kj = k[:, :].rearrange("p (j n) -> p j n", j=2)
                    pool.wait_ge(*sig["mask_ready"].at(0))
                    pool.tensor_tensor(kj, kj, KEEP[:, layer, b, :, None].to_broadcast([KJ, 2, D]), ALU.mult).then_inc(*sig["k_ready"].mark(a))
                pool.wait_ge(*sig["mask_ready"].at(0))
                if a >= 2:
                    pool.wait_ge(*sig["kt_psum"].at(a - 2))
                pool.tensor_copy(KX[:, a % 2, :, :, PR:PR + 1], KBIAS[:, layer, b, :, None, None].to_broadcast([KJ, 2, G, 1])).then_inc(*sig["kx_b"].mark(a))

            def k_low(a):
                pool.wait_ge(*sig["kx_h"].at(a))
                kx = KX[:, a % 2, :, :, 0:PR].rearrange("p j g (h s d) -> p (j g) h s d", h=HL, s=3)
                pool.tensor_tensor(kx[:, :, :, 2, :], k[:, :].rearrange("p (m h d) -> p m h d", h=HL, d=HD), kx[:, :, :, 0, :],
                                   ALU.subtract).then_inc(*sig["kx_l"].mark(a))

            def q_low(a):
                pool.wait_ge(*sig["qx_h"].at(a))
                qx = QX[:, :, :, 0:PR].rearrange("p t g (h s d) -> p (t g) h s d", h=HL, s=3)
                pool.tensor_tensor(qx[:, :, :, 1, :], (qb if a // B == 1 else q)[:, :].rearrange("p (m h d) -> p m h d", h=HL, d=HD),
                                   qx[:, :, :, 0, :], ALU.subtract).then_inc(*sig["qx_l"].mark(a))

            def q_square(a):
                layer = a // B
                if layer == 1:
                    if a == B:
                        pool.wait_ge(*sig["lora_l"].at(2 * B - 1))
                    pool.wait_ge(*sig["q"].at(a))
                    pool.tensor_tensor(qa[:, :], q[:, :], q[:, :], ALU.mult).then_inc(*sig["q_sq"].mark(a))
                if layer == 2:
                    pool.wait_ge(*sig["q"].at(a))
                    if a % B == 0:
                        pool.wait_ge(*sig["wA_in2"].at(0))
                    pool.tensor_tensor(qa[:, :].rearrange("p (t h d) -> p t h d", t=T, d=HD), q[:, :].rearrange("p (t h d) -> p t h d", t=T, d=HD),
                                       ropeq[:, :, None, 0:8].to_broadcast([128, T, H, HD]), ALU.mult).then_inc(*sig["q_t1"].mark(a))

            def q_root(a):
                if a // B == 1:
                    root_newton(qms[:, :], qrr[:, :], qtmp[:, :], sig["q_seed"], sig["q_rr"], a)

            def w_low(layer, c):
                which, lo, w = weight_chunks(layer)[c]
                serial = c + (8 if layer == 2 else 0)
                pool.wait_ge(*sig["w_h"].at(serial))
                pool.tensor_tensor(UP(layer)[:, which, 1, lo:lo + w], stage[:, serial % 2, 0:w], UP(layer)[:, which, 0, lo:lo + w],
                                   ALU.subtract).then_inc(*sig["w_l"].mark(serial))

            def lora_rows(j):
                pool.wait_ge(*sig["lora_in"].at(j))
                if ITEMS[j][2] > 0:
                    pool.wait_ge(*sig["lora_psum"].at((j - 1, 1)))
                else:
                    pool.wait_ge(*sig["w_ffn0_in"].at(0))
                pool.tensor_tensor(EBD[:, 0, :].rearrange("p (i n) -> p i n", i=4), EV[:, 0, None, :].to_broadcast([4, 4, D]),
                                   eye4[:, :, None].to_broadcast([4, 4, D]), ALU.mult).then_inc(*sig["lora_bd"].mark((j, 0)))
                pool.tensor_tensor(EBD[:, 1, :].rearrange("p (b i n) -> p b i n", b=4, i=4),
                                   EV[:, 1, :].rearrange("p (n b) -> p b n", b=4)[:, :, None, :].to_broadcast([4, 4, 4, 32]),
                                   eye4[:, None, :, None].to_broadcast([4, 4, 4, 32]), ALU.mult).then_inc(*sig["lora_bd"].mark(j))

            def piece(i, p):
                name = p[0]
                if name == "norm":
                    layer_norm(p[1])
                elif name == "k1":
                    k_square(p[1])
                elif name == "k3":
                    k_finish(p[1])
                elif name == "klow":
                    k_low(p[1])
                elif name == "q1":
                    q_square(p[1])
                elif name == "q3":
                    q_root(p[1])
                elif name == "qlow":
                    q_low(p[1])
                elif name == "w":
                    w_low(p[1], p[2])
                elif name == "rows":
                    lora_rows(p[1])

            n_init = 0
            for t_, v in ((CR[:, :, :], 0.0), (QX[:, :, :, :], 1.0), (MKX[:, :, :], 0.0),
                          (half[:, :], -0.5), (MR, 0.0)):
                ins = pool.memset(t_, v)
                n_init += 1
                ins.then_inc(*sig["init_pool"].more(0))
            pool.wait_ge(*sig["init_pool"].at(0))
            for r in range(2):
                for g in range(G):
                    ins = pool.memset(KB0[:, r, g, HL * KT0:R0 * C0].bitcast(I32), 0)
                    ins.then_inc(*sig["init_kb"].more(0))
                    ins = pool.memset(KB1[:, r, g, HL * KC:R1 * C1].bitcast(I32), 0)
                    ins.then_inc(*sig["init_kb"].more(0))
            layer_norm(0)
            k_finish(0)
            k_low(0)
            pool.wait_ge(*sig["mem_in"].at(0))
            pool.tensor_scalar(mk[:, :], mk[:, :], float(np.sqrt(HD)), None, ALU.mult).then_inc(*sig["mem_ready"].more("k"))
            pool.wait_ge(*sig["mem_ready"].at("k"))
            mx = MKX[:, :, 0:PR].rearrange("p g (h s d) -> p g h s d", h=HL, s=3)
            mk_ = mk[:, :].rearrange("p (g h d) -> p g h d", g=G, d=HD)
            for s in range(2):
                pool.tensor_copy(mx[:, :, :, s, :].bitcast(F32R), mk_).then_inc(*sig["mem_ready"].more("h"))
            pool.wait_ge(*sig["mem_ready"].at("h"))
            pool.tensor_tensor(mx[:, :, :, 2, :], mk_, mx[:, :, :, 0, :], ALU.subtract).then_inc(*sig["mem_ready"].more("l"))
            _, mem_cols = layout0(MR)
            for h in range(HL):
                pool.tensor_scalar(mem_cols[:, h, :], mvT[:, :], float(np.sqrt(KM)), None, ALU.mult).then_inc(*sig["mem_ready"].more(0))
            q_low(0)
            layer_norm(1)
            k_finish(1)
            k_low(1)
            q_low(1)
            pool.wait_ge(*sig["qx_l"].at(1))
            for r_ in range(2):
                shift_rows(pool, 1, r_)
                pool.wait_ge(*sig["shift_rows"].at((True, r_)))
            pool.wait_ge(*sig["wA_in1"].at(0))
            pool.tensor_tensor(gq[:, 0, :], gq[:, 0, :], gq[:, 1, :], ALU.mult).then_inc(*sig["gkq_ready"].mark(0))
            for i in range(len(ITEMS)):
                total, pieces = all_slots(i)
                for n in range(total):
                    for p in pieces.get(n, []):
                        piece(i, p)

    return {name: dict(s.seen) for name, s in sig.items()}


def constants():
    c = {}
    c["ident"] = np.eye(128, dtype=np.float32)
    c["eye4"] = np.eye(4, dtype=np.float32)
    m = np.zeros((K_ALL, HL), np.float32)
    for r in range(PR):
        m[r, r // (3 * HD)] = 1
    m[PR, :] = 1
    for h in range(HL):
        m[KX_ROWS + h, h] = 1
    c["maskk"] = m
    heads0 = sum([[h] * KT0 for h in range(HL)], [])
    ctx0 = ([1] * KC + [0] * KM) * HL
    heads1 = sum([[h] * KC for h in range(HL)], [])
    for name, heads, isctx, rows, chunks in (("0", heads0, ctx0, R0, C0), ("1", heads1, [1] * len(heads1), R1, C1)):
        mv = np.zeros((rows, chunks, G, HL, HD), np.float32)
        ind = np.zeros((1, rows * chunks), np.float32)
        for r, (h, ic) in enumerate(zip(heads, isctx)):
            mv[r % rows, r // rows, :, h, :] = 1
            ind[0, r] = ic
        c["mv" + name] = mv.reshape(rows, chunks, G, HL * HD)[:, :, 0, :]
        c["ind" + name] = ind
    inv = np.float32(10000.0) ** (np.arange(0, HD, 2, dtype=np.float32) / np.float32(HD))
    theta = (np.arange(S, dtype=np.float32)[:, None] / inv).astype(np.float32)
    sin, cos = np.sin(theta).astype(np.float32), np.cos(theta).astype(np.float32)
    for name, n, p in (("q", T, 128), ("k", 2, KJ)):
        lay = lambda a: np.ascontiguousarray(a[:n * p].reshape(n, p, -1).transpose(1, 0, 2))
        c["cos" + name] = lay(np.repeat(cos, 2, axis=-1))
        c["nsin" + name] = lay(-sin)
        c["sin" + name] = lay(sin)
    c["sink"] = c.pop("sink")
    c["lt"] = np.tril(np.ones((8, 8), np.float32), -1)
    return c


def kernel(**inp):
    import numpy as _np
    import concourse.bacc as _bacc
    from concourse import mybir as _mybir
    from concourse.bass_utils import run_bass_kernel_spmd as _run

    a = {n: _np.asarray(v) for n, v in inp.items()}
    tr = lambda w: _np.ascontiguousarray(w.T)
    arrays = {
        "x": a["x"], "ctxT": _np.ascontiguousarray(a["ctx_1024"].transpose(2, 0, 1)),
        "mask0": a["mask_Bx1x1xS2_ik0"].reshape(B, 2, KJ).transpose(2, 0, 1), "mask2": a["mask_Bx1x1xS2_bf1"].reshape(B, 2, KJ).transpose(2, 0, 1).view(_np.uint8),
        "wqT0": tr(a["L0_xattn_Wq"]), "wkT0": tr(a["L0_xattn_Wk"]), "wvT0": tr(a["L0_xattn_Wv"]), "woT0": tr(a["L0_xattn_Wo"]),
        "bq0": a["L0_xattn_bq"], "bk0": a["L0_xattn_bk"], "bv0": a["L0_xattn_bv"], "bo0": a["L0_xattn_bo"],
        "mk0": a["L0_xattn_m_k"].reshape(KM, D), "mvT0": tr(a["L0_xattn_m_v"].reshape(KM, D)),
        "w1T0": tr(a["L0_ffn_W1"]), "b1T0": tr(a["L0_ffn_b1"].reshape(4, 128)),
        "w2T0": _np.ascontiguousarray(a["L0_ffn_W2"].T.reshape(4, 128, D).transpose(1, 0, 2)),
        "b2_0": a["L0_ffn_b2"], "scale0": a["L0_ffn_scale"].reshape(1, 1),
        "wq1": a["L1_xattn_Wq"], "wkv1": a["L1_xattn_Wkv"], "wo1": a["L1_xattn_Wproj"], "bq1": a["L1_xattn_bq"],
        "bkv1": a["L1_xattn_bkv"], "bo1": a["L1_xattn_bproj"], "gq1": a["L1_xattn_gq"], "gk1": a["L1_xattn_gk"],
        "rw1": a["L1_ffn_router_w"], "rb1": a["L1_ffn_router_b"], "w1_1": a["L1_ffn_w1"], "w3_1": a["L1_ffn_w3"],
        "w2_1": _np.ascontiguousarray(a["L1_ffn_w2"].reshape(E1 * 4, 128, D).transpose(1, 0, 2)),
        "wq2": a["L2_xattn_w_q"], "wk2": a["L2_xattn_w_k"], "wv2": a["L2_xattn_w_v"], "wo2": a["L2_xattn_w_o"],
        "bq2": a["L2_xattn_b_q"], "bk2": a["L2_xattn_b_k"], "bv2": a["L2_xattn_b_v"], "bo2": a["L2_xattn_b_o"],
        "gw2": a["L2_ffn_gate_w"], "wg2": a["L2_ffn_Wg"], "wu2": a["L2_ffn_Wu"], "wd2": a["L2_ffn_Wd"],
        "sg2": a["L2_ffn_Sg"], "su2": a["L2_ffn_Su"], "sd2": a["L2_ffn_Sd"],
        "wq3": a["L3_xattn_Wq"], "bq3": a["L3_xattn_bq"], "wk3": a["L3_xattn_Wk"], "bk3": a["L3_xattn_bk"],
        "wv3": a["L3_xattn_Wv"], "bv3": a["L3_xattn_bv"], "we3T": tr(a["L3_ffn_W_expert"]), "ws3T": tr(a["L3_ffn_W_shared"]),
        "wgate3": a["L3_ffn_W_gate"], "bias3": a["L3_ffn_bias"],
    }
    arrays.update(constants())
    arrays = {f"in_{n}": _np.ascontiguousarray(arrays[n]) for n in ORDER}

    known = None
    for _ in range(2):
        nc = _bacc.Bacc("TRN2", target_bir_lowering=False, num_devices=1)
        aps = {n[3:]: nc.dram_tensor(n, v.shape, _mybir.dt.from_np(v.dtype), kind="ExternalInput").ap() for n, v in arrays.items()}
        out = nc.dram_tensor("out", (B, S, D), F32, kind="ExternalOutput").ap()
        known = program(nc, aps, out, known)
    r = _run(nc, [arrays], core_ids=[0])
    return r.results[0]["out"]
```
